# Optimizing a Trainium2 kernel written in Bass

```python
import numpy as np
import jax
import jax.numpy as jnp

def _softmax(x, axis=-1):
    return jax.nn.softmax(x, axis=axis)

def _gelu(x):
    return jax.nn.gelu(x, approximate=True)

def _silu(x):
    return jax.nn.silu(x)

def _sigmoid(x):
    return jax.nn.sigmoid(x)

def _layernorm(x, axis=-1, eps=1e-05):
    m = jnp.mean(x, axis=axis, keepdims=True)
    v = jnp.var(x, axis=axis, keepdims=True)
    return (x - m) / jnp.sqrt(v + eps)

def _scatter_add(tgt, idx, src, axis=0):
    return tgt.at[idx].add(src)

def _segment_sum(src, seg, n):
    return jax.ops.segment_sum(src, seg, n)
kernel_name = 'mk_gps_d2_gnn_r32_3f76d3'

def setup_inputs(seed: int=0):
    np.random.seed(seed)
    _w = jnp.asarray

    def _rec_inputs():
        import jax
        import jax.numpy as jnp
        _gk = jax.random.key(seed)
        x = -0.0003713 + 1 * jax.random.normal(jax.random.fold_in(_gk, 1), (3125, 256), jnp.float32)
        src = jax.random.randint(jax.random.fold_in(_gk, 2), (50000,), 0, 3125, jnp.int32)
        dst = jnp.minimum((3125 * jax.random.uniform(jax.random.fold_in(_gk, 3), (50000,)) ** 2.0).astype(jnp.int32), 99999)
        _o = jnp.argsort(dst, stable=True)
        src = src[_o]
        dst = dst[_o]
        edge_attr_3 = -1.09012e-05 + 0.99985 * jax.random.normal(jax.random.fold_in(_gk, 11), (50000, 3), jnp.float32)
        edge_type_8 = jax.random.randint(jax.random.fold_in(_gk, 13), (50000,), 0, 8, jnp.int32)
        return (x, src, dst, edge_attr_3, edge_type_8)
    x, src, dst, edge_attr_3, edge_type_8 = _rec_inputs()

    def _L0_gnn_setup():
        import jax, jax.numpy as jnp
        import numpy as np
        N = 50000
        E = 12500
        IN = 256
        H = 8
        D = 32
        EF = 3
        key = jax.random.key(seed)
        ks = jax.random.split(key, 8)
        x = jax.random.normal(ks[0], (N, IN), dtype=jnp.float32)
        edge_index = jax.random.randint(ks[1], (2, E), 0, N, dtype=jnp.int64)
        edge_attr = jax.random.normal(ks[2], (E, EF), dtype=jnp.float32)
        W = jax.random.normal(ks[3], (H * D, IN), dtype=jnp.float32) * np.float32(np.sqrt(2.0 / (IN + H * D)))
        a_src = jax.random.normal(ks[4], (H, D), dtype=jnp.float32) * np.float32(np.sqrt(2.0 / (H + D)))
        a_dst = jax.random.normal(ks[5], (H, D), dtype=jnp.float32) * np.float32(np.sqrt(2.0 / (H + D)))
        edge_W = jax.random.normal(ks[6], (H * D, EF), dtype=jnp.float32) * np.float32(np.sqrt(2.0 / (EF + H * D)))
        edge_b = jnp.zeros((H * D,), dtype=jnp.float32)
        bias = jnp.zeros((H * D,), dtype=jnp.float32)
        return {'x': x, 'W': W, 'a_src': a_src, 'a_dst': a_dst, 'edge_W': edge_W, 'edge_b': edge_b, 'bias': bias, 'edge_attr': edge_attr, 'edge_index': edge_index}
    _L0_gnn_all = _L0_gnn_setup()
    _L0_gnn_in = {k: v for k, v in _L0_gnn_all.items() if k in ('W', 'a_src', 'a_dst', 'edge_W', 'edge_b', 'bias')}
    del _L0_gnn_all

    def _L0_mix_setup():
        import jax, jax.numpy as jnp
        import numpy as np
        EMB, HEADS, DEPTH, SEQ, BATCH = (256, 8, 4, 256, 4)
        DH = EMB // HEADS
        FF = 4 * EMB
        EPS = 1e-05

        def _layernorm(x, g, b):
            mu = x.mean(-1, keepdims=True)
            var = ((x - mu) ** 2).mean(-1, keepdims=True)
            return (x - mu) * jax.lax.rsqrt(var + EPS) * g + b

        def _linear_attn(x, Wq, Wk, Wv, Wo, bo):
            b, n, dm = x.shape
            split = lambda t: t.reshape(b, n, HEADS, DH).transpose(0, 2, 1, 3)
            scale = DH ** (-0.25)
            q = jax.nn.softmax(split(x @ Wq) * scale, axis=-1)
            k = jax.nn.softmax(split(x @ Wk) * scale, axis=-2)
            v = split(x @ Wv)
            context = jnp.einsum('bhnd,bhne->bhde', k, v)
            out = jnp.einsum('bhnd,bhde->bhne', q, context)
            out = out.transpose(0, 2, 1, 3).reshape(b, n, dm)
            return out @ Wo + bo

        def _forward(x, Wq, Wk, Wv, Wo, bo, ln1_g, ln1_b, W1, b1, W2, b2, ln2_g, ln2_b):
            for i in range(DEPTH):
                h = _layernorm(x, ln1_g[i], ln1_b[i])
                x = x + _linear_attn(h, Wq[i], Wk[i], Wv[i], Wo[i], bo[i])
                h = _layernorm(x, ln2_g[i], ln2_b[i])
                x = x + (jax.nn.gelu(h @ W1[i] + b1[i], approximate=False) @ W2[i] + b2[i])
            return x
        key = jax.random.key(seed)
        ks = jax.random.split(key, 8)
        w = lambda k, shape: jax.random.normal(k, shape, dtype=jnp.float32) * 0.02
        D = DEPTH
        return {'x': jax.random.normal(ks[0], (BATCH, SEQ, EMB), dtype=jnp.float32), 'Wq': w(ks[1], (D, EMB, EMB)), 'Wk': w(ks[2], (D, EMB, EMB)), 'Wv': w(ks[3], (D, EMB, EMB)), 'Wo': w(ks[4], (D, EMB, EMB)), 'bo': jnp.zeros((D, EMB), jnp.float32), 'ln1_g': jnp.ones((D, EMB), jnp.float32), 'ln1_b': jnp.zeros((D, EMB), jnp.float32), 'W1': w(ks[5], (D, EMB, FF)), 'b1': jnp.zeros((D, FF), jnp.float32), 'W2': w(ks[6], (D, FF, EMB)), 'b2': jnp.zeros((D, EMB), jnp.float32), 'ln2_g': jnp.ones((D, EMB), jnp.float32), 'ln2_b': jnp.zeros((D, EMB), jnp.float32)}
    _L0_mix_all = _L0_mix_setup()
    _L0_mix_in = {k: v for k, v in _L0_mix_all.items() if k in ('Wq', 'Wk', 'Wv', 'Wo', 'bo', 'ln1_g', 'ln1_b', 'W1', 'b1', 'W2', 'b2', 'ln2_g', 'ln2_b')}
    del _L0_mix_all

    def _L0_ffn_setup():
        import jax, jax.numpy as jnp
        import numpy as np
        TOP_K = 2
        LN_EPS = 1e-05
        key = jax.random.key(seed)
        ks = jax.random.split(key, 8)
        B, S, D, E, H = (16, 1024, 256, 8, 1024)
        x = jax.random.normal(ks[0], (B, S, D), dtype=jnp.float32)
        Wr = jax.random.normal(ks[1], (D, E), dtype=jnp.float32) * 0.1
        br = jnp.zeros((E,), dtype=jnp.float32)
        ln_g = jnp.ones((E, D), dtype=jnp.float32)
        ln_b = jnp.zeros((E, D), dtype=jnp.float32)
        W1 = jax.random.normal(ks[2], (E, D, H), dtype=jnp.float32) * (1.0 / np.sqrt(D))
        b1 = jnp.zeros((E, H), dtype=jnp.float32)
        W2 = jax.random.normal(ks[3], (E, H, D), dtype=jnp.float32) * (1.0 / np.sqrt(H))
        b2 = jnp.zeros((E, D), dtype=jnp.float32)
        return {'x': x, 'Wr': Wr, 'br': br, 'ln_g': ln_g, 'ln_b': ln_b, 'W1': W1, 'b1': b1, 'W2': W2, 'b2': b2}
    _L0_ffn_all = _L0_ffn_setup()
    _L0_ffn_in = {k: v for k, v in _L0_ffn_all.items() if k in ('Wr', 'br', 'ln_g', 'ln_b', 'W1', 'b1', 'W2', 'b2')}
    del _L0_ffn_all

    def _L1_gnn_setup():
        import jax, jax.numpy as jnp
        import numpy as np
        N, E, R, H, D = (30000, 9375, 8, 8, 32)
        IN_F = 256
        NEG_SLOPE = 0.2
        key = jax.random.key(seed)
        k = jax.random.split(key, 6)
        x = jax.random.normal(k[0], (N, IN_F), dtype=jnp.float32)
        W = jax.random.normal(k[1], (R, H * D, IN_F), dtype=jnp.float32) * 0.05
        attn_src = jax.random.normal(k[2], (H, D), dtype=jnp.float32) * 0.1
        attn_dst = jax.random.normal(k[3], (H, D), dtype=jnp.float32) * 0.1
        edge_index = jax.random.randint(k[4], (2, E), 0, N, dtype=jnp.int64) if jax.config.read('jax_enable_x64') else jax.random.randint(k[4], (2, E), 0, N, dtype=jnp.int32)
        edge_type = jax.random.randint(k[5], (E,), 0, R, dtype=edge_index.dtype)
        return dict(x=x, W=W, attn_src=attn_src, attn_dst=attn_dst, edge_index=edge_index, edge_type=edge_type)
    _L1_gnn_all = _L1_gnn_setup()
    _L1_gnn_in = {k: v for k, v in _L1_gnn_all.items() if k in ('W', 'attn_src', 'attn_dst')}
    del _L1_gnn_all

    def _L1_mix_setup():
        import jax, jax.numpy as jnp
        import numpy as np
        A, Bc, Cc = (0.5, 1.0, 1.0)
        H = 8
        EPS = 1e-12

        def _normalize(t):
            n = jnp.linalg.norm(t, axis=-1, keepdims=True)
            return t / jnp.maximum(n, EPS)
        key = jax.random.key(seed)
        ks = jax.random.split(key, 5)
        B, N, C = (8, 64, 256)
        D = C // H
        x = jax.random.normal(ks[0], (B, N, C), dtype=jnp.float32)
        Wqkv = jax.random.normal(ks[1], (3 * H * D, C), dtype=jnp.float32) * 0.02
        bqkv = jnp.zeros((3 * H * D,), dtype=jnp.float32)
        Wproj = jax.random.normal(ks[2], (C, H * D), dtype=jnp.float32) * 0.02
        bproj = jnp.zeros((C,), dtype=jnp.float32)
        temperature = jnp.ones((1, H, 1, 1), dtype=jnp.float32)
        return {'x': x, 'Wqkv': Wqkv, 'bqkv': bqkv, 'Wproj': Wproj, 'bproj': bproj, 'temperature': temperature}
    _L1_mix_all = _L1_mix_setup()
    _L1_mix_in = {k: v for k, v in _L1_mix_all.items() if k in ('Wqkv', 'bqkv', 'Wproj', 'bproj', 'temperature')}
    del _L1_mix_all

    def _L1_ffn_setup():
        import jax, jax.numpy as jnp
        import numpy as np
        BN_EPS = 0.001

        def _bn(h, g, b, m, v):
            return g * (h - m) * jax.lax.rsqrt(v + BN_EPS) + b
        key = jax.random.key(seed)
        ks = jax.random.split(key, 8)
        B, F, Df = (256, 64, 256)
        E, H, D = (8, 256, 256)
        s1 = 1.0 / np.sqrt(Df)
        s2 = 1.0 / np.sqrt(H)
        return {'x': jax.random.normal(ks[0], (B, F, Df), jnp.float32), 'Wr': jax.random.normal(ks[1], (Df, E), jnp.float32) * s1, 'br': jnp.zeros((E,), jnp.float32), 'W1': jax.random.normal(ks[2], (E, Df, H), jnp.float32) * s1, 'b1': jnp.zeros((E, H), jnp.float32), 'g1': jnp.ones((E, H), jnp.float32), 'be1': jnp.zeros((E, H), jnp.float32), 'm1': jnp.zeros((E, H), jnp.float32), 'v1': jnp.ones((E, H), jnp.float32), 'W2': jax.random.normal(ks[3], (E, H, H), jnp.float32) * s2, 'b2': jnp.zeros((E, H), jnp.float32), 'g2': jnp.ones((E, H), jnp.float32), 'be2': jnp.zeros((E, H), jnp.float32), 'm2': jnp.zeros((E, H), jnp.float32), 'v2': jnp.ones((E, H), jnp.float32), 'Wo': jax.random.normal(ks[4], (E, H, D), jnp.float32) * s2, 'bo': jnp.zeros((E, D), jnp.float32)}
    _L1_ffn_all = _L1_ffn_setup()
    _L1_ffn_in = {k: v for k, v in _L1_ffn_all.items() if k in ('Wr', 'br', 'W1', 'b1', 'g1', 'be1', 'm1', 'v1', 'W2', 'b2', 'g2', 'be2', 'm2', 'v2', 'Wo', 'bo')}
    del _L1_ffn_all
    return {'x': x, 'src': src, 'dst': dst, 'edge_attr_3': edge_attr_3, 'edge_type_8': edge_type_8, 'L0_gnn_W': _L0_gnn_in['W'], 'L0_gnn_a_src': _L0_gnn_in['a_src'], 'L0_gnn_a_dst': _L0_gnn_in['a_dst'], 'L0_gnn_edge_W': _L0_gnn_in['edge_W'], 'L0_gnn_edge_b': _L0_gnn_in['edge_b'], 'L0_gnn_bias': _L0_gnn_in['bias'], 'L0_mix_Wq': _L0_mix_in['Wq'], 'L0_mix_Wk': _L0_mix_in['Wk'], 'L0_mix_Wv': _L0_mix_in['Wv'], 'L0_mix_Wo': _L0_mix_in['Wo'], 'L0_mix_bo': _L0_mix_in['bo'], 'L0_mix_ln1_g': _L0_mix_in['ln1_g'], 'L0_mix_ln1_b': _L0_mix_in['ln1_b'], 'L0_mix_W1': _L0_mix_in['W1'], 'L0_mix_b1': _L0_mix_in['b1'], 'L0_mix_W2': _L0_mix_in['W2'], 'L0_mix_b2': _L0_mix_in['b2'], 'L0_mix_ln2_g': _L0_mix_in['ln2_g'], 'L0_mix_ln2_b': _L0_mix_in['ln2_b'], 'L0_ffn_Wr': _L0_ffn_in['Wr'], 'L0_ffn_br': _L0_ffn_in['br'], 'L0_ffn_ln_g': _L0_ffn_in['ln_g'], 'L0_ffn_ln_b': _L0_ffn_in['ln_b'], 'L0_ffn_W1': _L0_ffn_in['W1'], 'L0_ffn_b1': _L0_ffn_in['b1'], 'L0_ffn_W2': _L0_ffn_in['W2'], 'L0_ffn_b2': _L0_ffn_in['b2'], 'L1_gnn_W': _L1_gnn_in['W'], 'L1_gnn_attn_src': _L1_gnn_in['attn_src'], 'L1_gnn_attn_dst': _L1_gnn_in['attn_dst'], 'L1_mix_Wqkv': _L1_mix_in['Wqkv'], 'L1_mix_bqkv': _L1_mix_in['bqkv'], 'L1_mix_Wproj': _L1_mix_in['Wproj'], 'L1_mix_bproj': _L1_mix_in['bproj'], 'L1_mix_temperature': _L1_mix_in['temperature'], 'L1_ffn_Wr': _L1_ffn_in['Wr'], 'L1_ffn_br': _L1_ffn_in['br'], 'L1_ffn_W1': _L1_ffn_in['W1'], 'L1_ffn_b1': _L1_ffn_in['b1'], 'L1_ffn_g1': _L1_ffn_in['g1'], 'L1_ffn_be1': _L1_ffn_in['be1'], 'L1_ffn_m1': _L1_ffn_in['m1'], 'L1_ffn_v1': _L1_ffn_in['v1'], 'L1_ffn_W2': _L1_ffn_in['W2'], 'L1_ffn_b2': _L1_ffn_in['b2'], 'L1_ffn_g2': _L1_ffn_in['g2'], 'L1_ffn_be2': _L1_ffn_in['be2'], 'L1_ffn_m2': _L1_ffn_in['m2'], 'L1_ffn_v2': _L1_ffn_in['v2'], 'L1_ffn_Wo': _L1_ffn_in['Wo'], 'L1_ffn_bo': _L1_ffn_in['bo']}

def reference(x, src, dst, edge_attr_3, edge_type_8, L0_gnn_W, L0_gnn_a_src, L0_gnn_a_dst, L0_gnn_edge_W, L0_gnn_edge_b, L0_gnn_bias, L0_mix_Wq, L0_mix_Wk, L0_mix_Wv, L0_mix_Wo, L0_mix_bo, L0_mix_ln1_g, L0_mix_ln1_b, L0_mix_W1, L0_mix_b1, L0_mix_W2, L0_mix_b2, L0_mix_ln2_g, L0_mix_ln2_b, L0_ffn_Wr, L0_ffn_br, L0_ffn_ln_g, L0_ffn_ln_b, L0_ffn_W1, L0_ffn_b1, L0_ffn_W2, L0_ffn_b2, L1_gnn_W, L1_gnn_attn_src, L1_gnn_attn_dst, L1_mix_Wqkv, L1_mix_bqkv, L1_mix_Wproj, L1_mix_bproj, L1_mix_temperature, L1_ffn_Wr, L1_ffn_br, L1_ffn_W1, L1_ffn_b1, L1_ffn_g1, L1_ffn_be1, L1_ffn_m1, L1_ffn_v1, L1_ffn_W2, L1_ffn_b2, L1_ffn_g2, L1_ffn_be2, L1_ffn_m2, L1_ffn_v2, L1_ffn_Wo, L1_ffn_bo):
    import jax
    import jax.numpy as jnp

    def _L0_gnn_ref(x, W, a_src, a_dst, edge_W, edge_b, bias, edge_attr, edge_index):
        import jax, jax.numpy as jnp
        import numpy as np
        N = 50000
        E = 12500
        IN = 256
        H = 8
        D = 32
        EF = 3
        n = x.shape[0]
        h = (x @ W.T).reshape(n, H, D)
        src, dst = (edge_index[0], edge_index[1])
        h_src = h[src]
        h_dst = h[dst]
        alpha = jnp.einsum('ehd,hd->eh', h_src, a_src) + jnp.einsum('ehd,hd->eh', h_dst, a_dst)
        enc = jax.nn.relu(edge_attr @ edge_W.T + edge_b).reshape(-1, H, D)
        alpha = alpha + jnp.sum(enc * h_dst, axis=-1)
        alpha = jnp.where(alpha >= 0, alpha, 0.2 * alpha)
        amax = jax.ops.segment_max(alpha, dst, num_segments=n)
        ex = jnp.exp(alpha - amax[dst])
        denom = jax.ops.segment_sum(ex, dst, num_segments=n)
        attn = ex / jnp.maximum(denom[dst], 1e-10)
        out = jax.ops.segment_sum(h_src * attn[..., None], dst, num_segments=n)
        return out.reshape(n, H * D) + bias

    def _L0_mix_ref(x, Wq, Wk, Wv, Wo, bo, ln1_g, ln1_b, W1, b1, W2, b2, ln2_g, ln2_b):
        import jax, jax.numpy as jnp
        import numpy as np
        EMB, HEADS, DEPTH, SEQ, BATCH = (256, 8, 4, 256, 4)
        DH = EMB // HEADS
        FF = 4 * EMB
        EPS = 1e-05

        def _layernorm(x, g, b):
            mu = x.mean(-1, keepdims=True)
            var = ((x - mu) ** 2).mean(-1, keepdims=True)
            return (x - mu) * jax.lax.rsqrt(var + EPS) * g + b

        def _linear_attn(x, Wq, Wk, Wv, Wo, bo):
            b, n, dm = x.shape
            split = lambda t: t.reshape(b, n, HEADS, DH).transpose(0, 2, 1, 3)
            scale = DH ** (-0.25)
            q = jax.nn.softmax(split(x @ Wq) * scale, axis=-1)
            k = jax.nn.softmax(split(x @ Wk) * scale, axis=-2)
            v = split(x @ Wv)
            context = jnp.einsum('bhnd,bhne->bhde', k, v)
            out = jnp.einsum('bhnd,bhde->bhne', q, context)
            out = out.transpose(0, 2, 1, 3).reshape(b, n, dm)
            return out @ Wo + bo

        def _forward(x, Wq, Wk, Wv, Wo, bo, ln1_g, ln1_b, W1, b1, W2, b2, ln2_g, ln2_b):
            for i in range(DEPTH):
                h = _layernorm(x, ln1_g[i], ln1_b[i])
                x = x + _linear_attn(h, Wq[i], Wk[i], Wv[i], Wo[i], bo[i])
                h = _layernorm(x, ln2_g[i], ln2_b[i])
                x = x + (jax.nn.gelu(h @ W1[i] + b1[i], approximate=False) @ W2[i] + b2[i])
            return x
        return _forward(x, Wq, Wk, Wv, Wo, bo, ln1_g, ln1_b, W1, b1, W2, b2, ln2_g, ln2_b)

    def _L0_ffn_ref(x, Wr, br, ln_g, ln_b, W1, b1, W2, b2):
        import jax, jax.numpy as jnp
        import numpy as np
        TOP_K = 2
        LN_EPS = 1e-05
        B, S, D = x.shape
        N = B * S
        xt = x.reshape(N, D)
        logits = xt @ Wr + br
        probs = jax.nn.softmax(logits, axis=-1)
        top_p, top_idx = jax.lax.top_k(probs, TOP_K)
        weights = top_p / top_p.sum(axis=-1, keepdims=True)
        mu = xt.mean(axis=-1, keepdims=True)
        var = ((xt - mu) ** 2).mean(axis=-1, keepdims=True)
        xn = (xt - mu) * jax.lax.rsqrt(var + LN_EPS)
        xe = xn[None, :, :] * ln_g[:, None, :] + ln_b[:, None, :]
        h = jax.nn.gelu(jnp.einsum('end,edh->enh', xe, W1) + b1[:, None, :], approximate=False)
        y = jnp.einsum('enh,ehd->end', h, W2) + b2[:, None, :]
        y_tok = jnp.transpose(y, (1, 0, 2))
        sel = jnp.take_along_axis(y_tok, top_idx[:, :, None], axis=1)
        out = (weights[:, :, None] * sel).sum(axis=1)
        return out.reshape(B, S, D)

    def _L1_gnn_ref(x, W, attn_src, attn_dst, edge_index, edge_type):
        import jax, jax.numpy as jnp
        import numpy as np
        N, E, R, H, D = (30000, 9375, 8, 8, 32)
        IN_F = 256
        NEG_SLOPE = 0.2
        n = x.shape[0]
        r = W.shape[0]
        h, d = attn_src.shape
        h_all = jnp.einsum('nf,rof->rno', x, W).reshape(r, n, h, d)
        src, dst = (edge_index[0], edge_index[1])
        h_src = h_all[edge_type, src]
        h_dst = h_all[edge_type, dst]
        scores = jnp.einsum('ehd,hd->eh', h_src, attn_src) + jnp.einsum('ehd,hd->eh', h_dst, attn_dst)
        scores = jnp.where(scores > 0, scores, NEG_SLOPE * scores)
        amax = jnp.maximum(jax.ops.segment_max(scores, dst, num_segments=n), 0.0)
        w = jnp.exp(scores - amax[dst])
        denom = jax.ops.segment_sum(w, dst, num_segments=n) + 1e-12
        w = w / denom[dst]
        msg = h_src * w[..., None]
        out = jax.ops.segment_sum(msg, dst, num_segments=n)
        return out.reshape(n, h * d)

    def _L1_mix_ref(x, Wqkv, bqkv, Wproj, bproj, temperature):
        import jax, jax.numpy as jnp
        import numpy as np
        A, Bc, Cc = (0.5, 1.0, 1.0)
        H = 8
        EPS = 1e-12

        def _normalize(t):
            n = jnp.linalg.norm(t, axis=-1, keepdims=True)
            return t / jnp.maximum(n, EPS)
        B, N, C = x.shape
        D = C // H
        scale = float(D) ** 0.25
        qkv = (x @ Wqkv.T + bqkv).reshape(B, N, 3, H, D)
        qkv = jnp.transpose(qkv, (2, 0, 3, 1, 4))
        q, k, v = (qkv[0], qkv[1], qkv[2])
        q = q * scale
        v1 = jnp.concatenate([jnp.ones((B, H, N, 1), dtype=v.dtype), v], axis=-1)
        qn = _normalize(q) * (scale * temperature)
        kn = _normalize(k) * scale
        vN = v1 / N
        kv_mod = jnp.einsum('bhni,bhnj,bhne->bhije', kn, kn, vN)
        kv = jnp.einsum('bhnd,bhne->bhde', kn, vN)
        vsum = jnp.sum(vN, axis=-2)[:, :, None, :]
        y = A * jnp.einsum('bhni,bhnj,bhije->bhne', qn, qn, kv_mod) + scale ** 2 * Bc * jnp.einsum('bhnd,bhde->bhne', qn, kv) + scale ** 4 * Cc * vsum
        y_norm, y = (y[..., :1], y[..., 1:])
        y = y / y_norm
        out = jnp.transpose(y, (0, 2, 1, 3)).reshape(B, N, H * D)
        return out @ Wproj.T + bproj

    def _L1_ffn_ref(x, Wr, br, W1, b1, g1, be1, m1, v1, W2, b2, g2, be2, m2, v2, Wo, bo):
        import jax, jax.numpy as jnp
        import numpy as np
        BN_EPS = 0.001

        def _bn(h, g, b, m, v):
            return g * (h - m) * jax.lax.rsqrt(v + BN_EPS) + b
        feat = jnp.mean(x, axis=0)
        w = jax.nn.softmax(feat @ Wr + br, axis=-1)
        h = jnp.einsum('bfd,edh->bfeh', x, W1) + b1
        h = jax.nn.relu(_bn(h, g1, be1, m1, v1))
        h = jnp.einsum('bfeh,ehk->bfek', h, W2) + b2
        h = jax.nn.relu(_bn(h, g2, be2, m2, v2))
        y = jnp.einsum('bfeh,ehd->bfed', h, Wo) + bo
        return jnp.einsum('bfed,fe->bfd', y, w)
    edge_index = jnp.stack([src, dst])
    xn = _layernorm(x, axis=-1)
    x = x + _L0_gnn_ref(xn, L0_gnn_W, L0_gnn_a_src, L0_gnn_a_dst, L0_gnn_edge_W, L0_gnn_edge_b, L0_gnn_bias, edge_attr_3, edge_index) + _L0_mix_ref(xn[None], L0_mix_Wq, L0_mix_Wk, L0_mix_Wv, L0_mix_Wo, L0_mix_bo, L0_mix_ln1_g, L0_mix_ln1_b, L0_mix_W1, L0_mix_b1, L0_mix_W2, L0_mix_b2, L0_mix_ln2_g, L0_mix_ln2_b)[0]
    x = x + _L0_ffn_ref(_layernorm(x, axis=-1)[None], L0_ffn_Wr, L0_ffn_br, L0_ffn_ln_g, L0_ffn_ln_b, L0_ffn_W1, L0_ffn_b1, L0_ffn_W2, L0_ffn_b2)[0]
    xn = _layernorm(x, axis=-1)
    x = x + _L1_gnn_ref(xn, L1_gnn_W, L1_gnn_attn_src, L1_gnn_attn_dst, edge_index, edge_type_8) + _L1_mix_ref(xn[None], L1_mix_Wqkv, L1_mix_bqkv, L1_mix_Wproj, L1_mix_bproj, L1_mix_temperature)[0]
    x = x + _L1_ffn_ref(_layernorm(x, axis=-1)[None], L1_ffn_Wr, L1_ffn_br, L1_ffn_W1, L1_ffn_b1, L1_ffn_g1, L1_ffn_be1, L1_ffn_m1, L1_ffn_v1, L1_ffn_W2, L1_ffn_b2, L1_ffn_g2, L1_ffn_be2, L1_ffn_m2, L1_ffn_v2, L1_ffn_Wo, L1_ffn_bo)[0]
    return x

_drawn_inputs = setup_inputs


def setup_inputs(seed=0):
    import zlib

    import numpy as np

    out = dict(_drawn_inputs(seed))
    spreads = {'L0_gnn_edge_b': (0.0, 0.1),
     'L0_gnn_bias': (0.0, 0.1),
     'L0_mix_bo': (0.0, 0.1),
     'L0_mix_ln1_g': (1.0, 0.6),
     'L0_mix_ln1_b': (0.0, 0.502),
     'L0_mix_b1': (0.0, 0.1),
     'L0_mix_b2': (0.0, 0.1),
     'L0_mix_ln2_g': (1.0, 0.2),
     'L0_mix_ln2_b': (0.0, 0.379),
     'L0_ffn_br': (0.0, 0.1),
     'L0_ffn_ln_g': (1.0, 0.2),
     'L0_ffn_ln_b': (0.0, 0.321),
     'L0_ffn_b1': (0.0, 0.315),
     'L0_ffn_b2': (0.0, 0.1),
     'L1_mix_bqkv': (0.0, 0.556),
     'L1_mix_bproj': (0.0, 0.1),
     'L1_mix_temperature': (1.0, 0.6),
     'L1_ffn_br': (0.0, 0.8),
     'L1_ffn_b1': (0.0, 0.652),
     'L1_ffn_g1': (1.0, 0.6),
     'L1_ffn_be1': (0.0, 0.725),
     'L1_ffn_m1': (0.0, 0.685),
     'L1_ffn_v1': (1.0, 0.6),
     'L1_ffn_b2': (0.0, 0.491),
     'L1_ffn_g2': (1.0, 0.6),
     'L1_ffn_be2': (0.0, 0.542),
     'L1_ffn_m2': (0.0, 0.483),
     'L1_ffn_v2': (1.0, 0.6),
     'L1_ffn_bo': (0.0, 0.371)}
    factors = {'L0_mix_Wq': 28.131, 'L0_mix_Wk': 24.98, 'L1_mix_Wqkv': 7.471, 'L1_mix_Wproj': 3.522}
    for name, (base, spread) in spreads.items():
        noise = np.random.default_rng([zlib.crc32(name.encode()), seed]).standard_normal(out[name].shape)
        drawn = base * np.exp(spread * noise) if base else spread * noise
        out[name] = jnp.asarray(drawn.astype(out[name].dtype))
    for name, factor in factors.items():
        out[name] = (out[name] * factor).astype(out[name].dtype)
    return out
```

```python
from contextlib import ExitStack

import numpy as np

import concourse.bass as bass
from concourse import mybir

F32 = mybir.dt.float32
I32 = mybir.dt.int32
U32 = mybir.dt.uint32
ALU = mybir.AluOpType
ACT = mybir.ActivationFunctionType
X_AXIS = mybir.AxisListType.X

P = 128
N, D = 3125, 256
NT = -(-N // P)
NP = NT * P
LAST = N - (NT - 1) * P
U = 5
NB = NT // U
CH = U * P // 2
H, DH = 8, 32
HALF = D // P

E = 50000
EP = 125
ET = E // EP
GT = 8
NG = ET // GT
GE = GT * EP
HW = DH + 1
MSG = H * HW
ROW = MSG + H
SKIP = 4000
BIG = 1e30
NEG_SLOPE = 0.2
FT = 4
FQ = ET // FT
R = 8
SLOTS = U


class Phase:

    def __init__(self, nc, name):
        self.nc, self.name, self.sems, self.ctx = nc, name, [], ExitStack()

    def sb(self, name, shape, dtype=F32):
        return self.ctx.enter_context(self.nc.sbuf_tensor(f"{self.name}_{name}", shape, dtype))

    def ps(self, name, shape):
        return self.ctx.enter_context(self.nc.psum_tensor(f"{self.name}_ps_{name}", shape, F32))

    def sem(self, name):
        self.sems.append(self.ctx.enter_context(self.nc.semaphore(f"{self.name}_{name}")))
        return self.sems[-1]

    def open(self):
        self.inner = ExitStack()
        return self.inner.enter_context(self.nc.Block())

    def __enter__(self):
        return self

    def __exit__(self, *error):
        if error[0] is None:
            self.inner.close()
            for s in self.sems:
                self.nc.sync.sem_clear(s)
            self.nc.all_engine_barrier()
            self.ctx.close()


def gate(eng, sem, value, passed):
    eng.wait_ge(sem, value)
    eng.sem_inc(passed, 1)


def load_ahead(block, loaded, ahead):
    if ahead:
        @block.sync
        def _(sp):
            for out, in_ in ahead:
                sp.dma_start(out, in_).then_inc(loaded, 16)
            sp.wait_ge(loaded, 16 * len(ahead))


def load_x(nc, io, X):
    with Phase(nc, "load") as ph:
        loaded = ph.sem("loaded")
        block = ph.open()

        @block.sync
        def _(sp):
            sp.dma_start(X[:, :, :], io["x"].rearrange("(t p) f -> p t f", p=P)).then_inc(loaded, 16)
            sp.wait_ge(loaded, 16)


def norm(nc, name, src, rows, turned, ident, gain=None, bias=None, ahead=()):
    with Phase(nc, name) as ph:
        stats = ph.sb("stats", [P, NT, 6])
        mv = ph.sb("mv", [P, NT, 2])
        var_eps = ph.sb("var_eps", [P, NT])
        std = ph.sb("std", [P, NT])
        rstd = ph.sb("rstd", [P, NT])
        pt = ph.ps("pt", [P, SLOTS, 512])
        s_stats, s_mv, s_var = ph.sem("stats"), ph.sem("mv"), ph.sem("var")
        s_std, s_rstd, s_rows = ph.sem("std"), ph.sem("rstd"), ph.sem("rows")
        s_turned, s_free, s_ahead = ph.sem("turned"), ph.sem("free"), ph.sem("ahead")
        block = ph.open()
        load_ahead(block, s_ahead, ahead)

        @block.vector
        def _(v):
            with v.Fori(0, NT) as t:
                v.bn_stats(stats[:, t, :], src[:, t, :]).then_inc(s_stats, 1)
            v.wait_ge(s_stats, NT)
            for t in range(NT):
                v.bn_aggr(mv[:, t, :], stats[:, t, :]).then_inc(s_mv, 1)
            v.wait_ge(s_mv, NT)
            v.tensor_scalar(var_eps[:, :], mv[:, :, 1], 1e-5, None, ALU.add).then_inc(s_var, 1)
            v.wait_ge(s_std, 1)
            v.reciprocal(rstd[:, :], std[:, :]).then_inc(s_rstd, 1)
            v.wait_ge(s_rstd, 1)
            with v.Fori(0, NT) as t:
                v.tensor_scalar(rows[:, t, :], src[:, t, :], mv[:, t, 0:1], rstd[:, bass.ds(t, 1)],
                                ALU.subtract, ALU.mult).then_inc(s_rows, 1)

        @block.tensor
        def _(pe):
            for t in range(NT):
                pe.wait_ge(s_rows, t + 1)
                pe.wait_ge(s_free, t + 1)
                for a in range(HALF):
                    mm = pe.transpose(pt[:, t % SLOTS, a * P:(a + 1) * P], rows[:, t, a * P:(a + 1) * P], ident[:, :])
                mm.then_inc(s_turned, 1)

        @block.scalar
        def _(act):
            act.sem_inc(s_free, SLOTS)
            act.wait_ge(s_var, 1)
            act.activation(std[:, :], var_eps[:, :], ACT.Sqrt).then_inc(s_std, 1)
            with act.Fori(0, NB) as k:
                for j in range(U):
                    act.wait_ge(s_turned, k * U + j + 1)
                    at = bass.ds(k * (U * P) + j * P, P)
                    if gain is None:
                        last = act.activation(turned[:, :, at], pt[:, j, 0:D].rearrange("p (a n) -> p a n", a=HALF), ACT.Copy)
                    else:
                        for a in range(HALF):
                            last = act.activation(turned[:, a, at], pt[:, j, a * P:(a + 1) * P], ACT.Identity,
                                                  bias=bias[:, a:a + 1], scale=gain[:, a:a + 1])
                    last.then_inc(s_free, 1)


def edge_prep(nc, io, g, more):
    with Phase(nc, "prep") as ph:
        srcc = ph.sb("src", [EP, ET], I32)
        typec = ph.sb("type", [EP, ET], I32)
        nextc = ph.sb("next", [EP, ET], I32)
        firstc = ph.sb("first", [EP, ET], I32)
        base = ph.sb("base", [EP, ET])
        ends = ph.sb("ends", [EP, ET])
        inner = ph.sb("inner", [EP, ET])
        s_in, s_v = ph.sem("in"), ph.sem("v")
        block = ph.open()
        loads = [(g["dst"][:, :], io["dst_c"]), (srcc[:, :], io["src_c"]), (typec[:, :], io["type_c"]),
                 (nextc[:, :], io["next_c"]), (firstc[:, :], io["first_c"]), (g["ident"][:, :], io["ident"]),
                 (g["blocks"][:, :], io["blocks"])] + more

        @block.sync
        def _(sp):
            for out, in_ in loads:
                sp.dma_start(out, in_).then_inc(s_in, 16)

        @block.vector
        def _(v):
            v.wait_ge(s_in, 16 * len(loads))
            for n in ("src0", "dst0", "src1", "dst1", "put"):
                v.memset(g[n][:, :], 0).then_inc(s_v, 1)
            v.tensor_scalar(base[:, :], typec[:, :], float(NP), None, ALU.mult).then_inc(s_v, 1)
            v.tensor_tensor(ends[:, :], g["dst"][:, :], nextc[:, :], ALU.not_equal).then_inc(s_v, 1)
            v.tensor_tensor(inner[:, :], g["dst"][:, :], firstc[:, :], ALU.not_equal).then_inc(s_v, 1)
            v.wait_ge(s_v, 8)
            v.tensor_copy(g["src0"][:, 0:ET], srcc[:, :]).then_inc(s_v, 1)
            v.tensor_copy(g["dst0"][:, 0:ET], g["dst"][:, :]).then_inc(s_v, 1)
            v.tensor_tensor(g["src1"][:, 0:ET], base[:, :], srcc[:, :], ALU.add).then_inc(s_v, 1)
            v.tensor_tensor(g["dst1"][:, 0:ET], base[:, :], g["dst"][:, :], ALU.add).then_inc(s_v, 1)
            v.tensor_tensor(ends[:, :], ends[:, :], inner[:, :], ALU.mult).then_inc(s_v, 1)
            v.wait_ge(s_v, 13)
            v.scalar_tensor_tensor(inner[:, :], g["dst"][:, :], -float(SKIP), ends[:, :],
                                   ALU.add, ALU.mult).then_inc(s_v, 1)
            v.wait_ge(s_v, 14)
            v.tensor_scalar(g["put"][:, 0:ET], inner[:, :], float(SKIP), None, ALU.add).then_inc(s_v, 1)


def gnn_table(nc, io, g, layer, turned, table, dtable):
    rel = R if layer else 1
    with Phase(nc, f"table{layer}") as ph:
        wo = ph.sb("wo", [P, 2, HALF, D])
        wt = ph.sb("wt", [P, 2, HALF, ROW])
        acol = ph.sb("acol", [P, 2, HALF])
        mask = ph.sb("mask", [P, HALF, H])
        ablk = ph.sb("ablk", [P, HALF, 2, H])
        rows = ph.sb("rows", [P, NB, U, ROW])
        pa = ph.ps("pa", [P, HALF, 512])
        ph_ = ph.ps("ph", [P, SLOTS, 512])
        s_w = [ph.sem(f"w{b}") for b in range(2)]
        s_c, s_ab, s_pa, s_wt = ph.sem("c"), ph.sem("ab"), ph.sem("pa"), ph.sem("wt")
        s_h, s_rows = ph.sem("h"), ph.sem("rows")
        s_saved = [ph.sem(f"saved{k}") for k in range(NB)]
        block = ph.open()
        per_store = 1 if dtable is None else 2

        def store(sp, r):
            for k in range(NB):
                sp.wait_ge(s_rows, SLOTS + r * NT + (k + 1) * U)
                at = slice(r * NP + k * U * P, r * NP + (k + 1) * U * P)
                sp.dma_start(table[at, :].rearrange("(t p) w -> p t w", p=P), rows[:, k, :, :]).then_inc(s_saved[k], 16)
                if dtable is not None:
                    sp.dma_start(dtable[at, :].rearrange("(t p) w -> p t w", p=P),
                                 rows[:, k, :, MSG:ROW]).then_inc(s_saved[k], 16)

        @block.sync
        def _(sp):
            sp.dma_start(acol[:, :, :], io[f"a{layer}"]).then_inc(s_c, 16)
            sp.dma_start(mask[:, :, :], io["headmask"]).then_inc(s_c, 16)
            for k in range(NB):
                sp.sem_inc(s_saved[k], 16 * per_store)
            for r in range(rel):
                if r >= 2:
                    sp.wait_ge(s_h, NT * (r - 1))
                sp.dma_start(wo[:, r % 2, :, :], io[f"gnn_w{layer}"][r].rearrange("(a p) i -> p a i", p=P)).then_inc(s_w[r % 2], 16)
                sp.dma_start(wt[:, r % 2, :, :], io[f"gnn_wt{layer}"][r].rearrange("(a p) o -> p a o", p=P)).then_inc(s_w[r % 2], 16)
                if r:
                    store(sp, r - 1)
            store(sp, rel - 1)
            for k in range(NB):
                sp.wait_ge(s_saved[k], 16 * per_store * (rel + 1))

        @block.vector
        def _(v):
            v.wait_ge(s_c, 32)
            for s in range(2):
                for a in range(HALF):
                    v.tensor_scalar(ablk[:, a, s, :], mask[:, a, :], acol[:, s, a:a + 1], None,
                                    ALU.mult).then_inc(s_ab, 1)
            for r in range(rel):
                v.wait_ge(s_w[r % 2], 32 * (r // 2 + 1))
                v.wait_ge(s_pa, r + 1)
                for a in range(HALF):
                    v.tensor_copy(wt[:, r % 2, a, 0:MSG].rearrange("p (h w) -> p h w", w=HW)[:, :, DH],
                                  pa[:, a, 0:H]).then_inc(s_wt, 1)
                    v.tensor_copy(wt[:, r % 2, a, MSG:ROW], pa[:, a, H:2 * H]).then_inc(s_wt, 1)

        @block.tensor
        def _(pe):
            pe.wait_ge(s_ab, 2 * HALF)
            for r in range(rel):
                pe.wait_ge(s_w[r % 2], 32 * (r // 2 + 1))
                if r:
                    pe.wait_ge(s_wt, 4 * r)
                for a in range(HALF):
                    for o in range(HALF):
                        mm = pe.matmul(pa[:, a, 0:2 * H], wo[:, r % 2, o, a * P:(a + 1) * P],
                                       ablk[:, o, :, :].rearrange("p s h -> p (s h)"),
                                       start=(o == 0), stop=(o == HALF - 1))
                mm.then_inc(s_pa, 1)
                pe.wait_ge(s_wt, 4 * (r + 1))
                for t in range(NT):
                    pe.wait_ge(s_rows, r * NT + t + 1)
                    for a in range(HALF):
                        mm = pe.matmul(ph_[:, t % SLOTS, 0:ROW], turned[:, a, t * P:(t + 1) * P],
                                       wt[:, r % 2, a, :], start=(a == 0), stop=(a == HALF - 1))
                    mm.then_inc(s_h, 1)

        @block.scalar
        def _(act):
            act.sem_inc(s_rows, SLOTS)
            with act.Fori(0, rel) as r:
                for k in range(NB):
                    act.wait_ge(s_saved[k], r * (16 * per_store) + 16 * per_store)
                    for j in range(U):
                        act.wait_ge(s_h, r * NT + (k * U + j + 1))
                        act.activation(rows[:, k, j, :], ph_[:, j, 0:ROW], ACT.Copy).then_inc(s_rows, 1)



SLOTS_O = 4


def edges(nc, io, g, layer, table, dtable, totals, firsts):
    idx_src, idx_dst = g[f"src{layer}"], g[f"dst{layer}"]
    encoded = layer == 0
    dw = ROW if encoded else H
    with Phase(nc, f"edges{layer}") as ph:
        Gs = [ph.sb(f"rows_src{b}", [EP, GT, ROW]) for b in range(2)]
        Gd = [ph.sb(f"rows_dst{b}", [EP, GT, dw]) for b in range(2)]
        O = [ph.sb(f"out{b}", [EP, GT, ROW]) for b in range(2)]
        same = [ph.sb(f"same{b}", [EP, GT, EP]) for b in range(2)]
        dstb = [ph.sb(f"dstb{b}", [EP, GT, EP], I32) for b in range(2)]
        dstx = [ph.sb(f"dstx{b}", [GT * H, EP], I32) for b in range(2)]
        slot_s = [ph.sb(f"slot_s{b}", [EP, GT], I32) for b in range(2)]
        slot_d = [ph.sb(f"slot_d{b}", [EP, GT], I32) for b in range(2)]
        slot_o = [ph.sb(f"slot_o{b}", [EP, GT], I32) for b in range(2)]
        blank = ph.sb("blank", [P, ROW])
        pen = ph.sb("pen", [GT * H, EP + 1])
        fwd = ph.sb("fwd", [GT * H, EP])
        bwd = ph.sb("bwd", [GT * H, EP])
        top = ph.sb("top", [GT * H, EP])
        alpha = ph.sb("alpha", [EP, GT, H])
        alpha0 = ph.sb("alpha0", [EP, GT, H])
        below = ph.sb("below", [EP, GT, H])
        p_t = ph.ps("p_t", [P, 512])
        p_m = ph.ps("p_m", [P, 512])
        p_o = ph.ps("p_o", [P, SLOTS_O, 512])
        if encoded:
            attr = [ph.sb(f"attr{b}", [4, GE]) for b in range(2)]
            enc_w = ph.sb("enc_w", [4, D])
            enc = ph.sb("enc", [EP, 2, 2, D])
            dot = ph.sb("dot", [EP, GT, H])
            p_e = ph.ps("p_e", [P, 2, 2, D])
        s_blank, s_clear, s_w = ph.sem("blank"), ph.sem("clear"), ph.sem("w")
        s_chunk = [ph.sem(f"chunk{b}") for b in range(2)]
        s_used = [ph.sem(f"used{b}") for b in range(2)]
        s_slots = [ph.sem(f"slots{b}") for b in range(2)]
        s_put = [ph.sem(f"put{b}") for b in range(2)]
        s_got = g[f"got{layer}"]
        s_scattered = g[f"scattered{layer}"]
        s_ofree = [ph.sem(f"ofree{b}") for b in range(2)]
        s_firsts = [ph.sem(f"firsts{b}") for b in range(2)]
        s_passed, s_pe, s_penc = ph.sem("passed"), ph.sem("pe"), ph.sem("penc")
        s_enc, s_prod, s_encfree, s_pencfree = ph.sem("enc"), ph.sem("prod"), ph.sem("encfree"), ph.sem("pencfree")
        s_chain, s_alpha, s_aT, s_top, s_mT = ph.sem("chain"), ph.sem("alpha"), ph.sem("aT"), ph.sem("top"), ph.sem("mT")
        s_below, s_exp, s_msg, s_same = ph.sem("below"), ph.sem("exp"), ph.sem("msg"), ph.sem("same")
        s_scan = ph.sem("scan")
        s_sum, s_out, s_pen, s_mcopy = ph.sem("sum"), ph.sem("out"), ph.sem("pen"), ph.sem("mcopy")
        block = ph.open()

        def weight(b):
            return Gs[b][:, :, 0:MSG].rearrange("p c (h w) -> p c h w", w=HW)[:, :, :, DH]

        loads = 3 if encoded else 2

        def load_chunk(sp, n, b):
            sp.dma_start(dstb[b][:, :, :].rearrange("p c e -> p (c e)"),
                         io["dst_row"][:, bass.ds(n * GE, GE)].partition_broadcast(EP)).then_inc(s_chunk[b], 16)
            sp.dma_start(dstx[b][:, :], io["dst_x"][n]).then_inc(s_chunk[b], 16)
            if encoded:
                sp.dma_start(attr[b][:, :], io["attr"][:, bass.ds(n * GE, GE)]).then_inc(s_chunk[b], 16)

        @block.sync
        def _(sp):
            if encoded:
                sp.dma_start(enc_w[:, :], io["enc_w"]).then_inc(s_w, 16)
            for b in range(2):
                sp.sem_inc(s_ofree[b], 1)
                load_chunk(sp, b, b)
            sp.wait_ge(s_blank, 2)
            sp.dma_start(totals.rearrange("(t p) w -> p t w", p=P),
                         blank[:, None, :].to_broadcast([P, NT, ROW])).then_inc(s_clear, 16)
            with sp.Fori(0, NG // 2) as k:
                for b in range(2):
                    n = k * 2 + b
                    gate(sp, s_out, n * GT + (SLOTS_O + GT), s_passed)
                    gate(sp, s_mcopy, n + 2, s_passed)
                    sp.dma_start(firsts[bass.ds(n * GT, GT), :].rearrange("(a t) w -> a t w", a=1),
                                 O[b][0:1, :, :]).then_inc(s_firsts[b], 16)
                    gate(sp, s_used[b], 2 * (k + 1), s_passed)
                    if encoded:
                        gate(sp, s_enc, n * (GT // 2) + (2 + GT // 2), s_passed)
                    load_chunk(sp, n + 2, b)
                    gate(sp, s_scattered[b], 16 * GT * (k + 1), s_passed)
                    gate(sp, s_firsts[b], 16 * (k + 1), s_passed)
                    sp.sem_inc(s_ofree[b], 1)
            for b in range(2):
                sp.wait_ge(s_chunk[b], 16 * loads * (NG // 2 + 1))

        @block.gpsimd
        def _(pool):
            pool.memset(blank[:, 0:MSG], 0.0).then_inc(s_blank, 1)
            pool.memset(blank[:, MSG:ROW], -BIG).then_inc(s_blank, 1)

            def gather(k, b):
                gate(pool, s_slots[b], 2 * k + 2, s_passed)
                gate(pool, s_sum, k * (2 * GT) + GT * (b + 1), s_passed)
                for c in range(GT):
                    pool.indirect_dma_start(Gs[b][:, c, :], None, table,
                                            bass.IndirectOffsetOnAxis(ap=slot_s[b][:, c:c + 1], axis=0)).then_inc(s_got[b], 16)
                for c in range(GT):
                    pool.indirect_dma_start(Gd[b][:, c, :], None, table if encoded else dtable,
                                            bass.IndirectOffsetOnAxis(ap=slot_d[b][:, c:c + 1], axis=0)).then_inc(s_got[b], 16)

            def scatter(k, b):
                gate(pool, s_put[b], k + 1, s_passed)
                gate(pool, s_out, k * (2 * GT) + (SLOTS_O + GT * (b + 1)), s_passed)
                gate(pool, s_mcopy, 2 * k + (b + 2), s_passed)
                for c in range(GT):
                    pool.indirect_dma_start(totals, bass.IndirectOffsetOnAxis(ap=slot_o[b][:, c:c + 1], axis=0),
                                            O[b][:, c, :], None, bounds_check=NP - 1,
                                            oob_is_err=False).then_inc(s_scattered[b], 16)

            gather(0, 0)
            pool.wait_ge(s_clear, 16)
            with pool.Fori(0, NG // 2 - 1) as k:
                gather(k, 1)
                scatter(k, 0)
                gather(k + 1, 0)
                scatter(k, 1)
            gather(NG // 2 - 1, 1)
            scatter(NG // 2 - 1, 0)
            scatter(NG // 2 - 1, 1)

        @block.tensor
        def _(pe):
            pe.sem_inc(s_sum, 2 * GT)
            if encoded:
                pe.wait_ge(s_w, 16)
            with pe.Fori(0, NG // 2) as k:
                for b in range(2):
                    n = k * 2 + b
                    if encoded:
                        pe.wait_ge(s_chunk[b], 16 * loads * (k + 1))
                        for q in range(GT // 2):
                            pe.wait_ge(s_enc, n * (GT // 2) + (q + 1))
                            for c in range(2):
                                mm = pe.matmul(p_e[0:EP, q % 2, c, :], attr[b][:, (2 * q + c) * EP:(2 * q + c + 1) * EP],
                                               enc_w[:, :], start=True, stop=True)
                            mm.then_inc(s_penc, 1)
                    gate(pe, s_alpha, n + 1, s_passed)
                    pe.transpose(p_t[0:GT * H, 0:EP], alpha[:, :, :].rearrange("p c h -> p (c h)"),
                                 g["ident"][0:EP, 0:EP]).then_inc(s_aT, 1)
                    gate(pe, s_top, n + 2, s_passed)
                    gate(pe, s_mcopy, n + 1, s_passed)
                    gate(pe, s_below, n + 1, s_passed)
                    pe.transpose(p_m[0:EP, 0:GT * H], top[:, :], g["ident"][0:GT * H, 0:GT * H]).then_inc(s_mT, 1)
                    pe.wait_ge(s_msg, n + 1)
                    for c in range(GT):
                        pe.wait_ge(s_out, n * GT + (c + 1))
                        pe.matmul(p_o[0:EP, c % SLOTS_O, 0:MSG], same[b][:, c, :], Gs[b][:, c, 0:MSG],
                                  start=True, stop=True).then_inc(s_sum, 1)

        @block.scalar
        def _(act):
            act.sem_inc(s_out, SLOTS_O)
            act.sem_inc(s_enc, 2)
            act.sem_inc(s_mcopy, 1)
            with act.Fori(0, NG // 2) as k:
                for b in range(2):
                    n = k * 2 + b
                    if encoded:
                        for q in range(GT // 2):
                            act.wait_ge(s_penc, n * (GT // 2) + (q + 1))
                            act.wait_ge(s_encfree, n * (GT // 2) + (q + 1))
                            act.activation(enc[:, q % 2, :, :], p_e[0:EP, q % 2, :, :], ACT.Relu).then_inc(s_enc, 1)
                    act.wait_ge(s_ofree[b], k + 1)
                    act.wait_ge(s_below, n + 2)
                    act.activation(weight(b), below[:, :, :], ACT.Exp).then_inc(s_exp, 1)
                    act.activation(O[b][:, :, MSG:ROW], p_m[0:EP, 0:GT * H].rearrange("p (c h) -> p c h", h=H),
                                   ACT.Copy).then_inc(s_mcopy, 1)
                    for c in range(GT):
                        act.wait_ge(s_sum, n * GT + (2 * GT + c + 1))
                        act.activation(O[b][:, c, 0:MSG], p_o[0:EP, c % SLOTS_O, 0:MSG], ACT.Copy).then_inc(s_out, 1)

        @block.vector
        def _(v):
            v.memset(pen[:, :], 0.0).then_inc(s_pen, 1)
            v.sem_inc(s_top, 1)
            v.sem_inc(s_below, 1)
            if encoded:
                v.sem_inc(s_encfree, 2)
            for b in range(2):
                v.tensor_copy(slot_s[b][:, :], idx_src[:, b * GT:(b + 1) * GT]).then_inc(s_slots[b], 1)
                v.tensor_copy(slot_d[b][:, :], idx_dst[:, b * GT:(b + 1) * GT]).then_inc(s_slots[b], 1)
            v.wait_ge(s_pen, 1)
            with v.Fori(0, NG // 2) as k:
                for b in range(2):
                    n = k * 2 + b
                    v.wait_ge(s_chunk[b], 16 * loads * (k + 1))
                    v.wait_ge(s_top, n + 1)
                    v.tensor_tensor(pen[:, 1:EP], dstx[b][:, 1:EP], dstx[b][:, 0:EP - 1],
                                    ALU.not_equal).then_inc(s_used[b], 1)
                    v.wait_ge(s_sum, n * GT + GT)
                    v.tensor_tensor(same[b][:, :, :], dstb[b][:, :, :],
                                    g["dst"][:, bass.ds(n * GT, GT)][:, :, None].to_broadcast([EP, GT, EP]),
                                    ALU.is_equal).then_inc(s_used[b], 1)
                    v.wait_ge(s_used[b], 2 * (k + 1))
                    v.tensor_scalar(pen[:, 1:EP], pen[:, 1:EP], -BIG, None, ALU.mult).then_inc(s_pen, 1)
                    v.wait_ge(s_got[b], 32 * GT * (k + 1))
                    v.tensor_copy(slot_s[b][:, :], idx_src[:, bass.ds(n * GT + 2 * GT, GT)]).then_inc(s_slots[b], 1)
                    v.tensor_copy(slot_d[b][:, :], idx_dst[:, bass.ds(n * GT + 2 * GT, GT)]).then_inc(s_slots[b], 1)
                    v.wait_ge(s_ofree[b], k + 1)
                    v.tensor_copy(slot_o[b][:, :], g["put"][:, bass.ds(n * GT, GT)]).then_inc(s_put[b], 1)
                    if encoded:
                        v.tensor_tensor(alpha0[:, :, :], weight(b), Gd[b][:, :, MSG:ROW], ALU.add).then_inc(s_chain, 1)
                        for q in range(GT // 2):
                            v.wait_ge(s_enc, n * (GT // 2) + (q + 3))
                            e4 = enc[:, q % 2, :, :].rearrange("p c (h w) -> p c h w", w=DH)
                            for c in range(2):
                                v.tensor_tensor(e4[:, c], e4[:, c],
                                                Gd[b][:, 2 * q + c, 0:MSG].rearrange("p (h w) -> p h w", w=HW)[:, :, 0:DH],
                                                ALU.mult).then_inc(s_prod, 1)
                            v.wait_ge(s_prod, n * GT + (2 * q + 2))
                            v.tensor_reduce(dot[:, 2 * q:2 * q + 2, :], e4, X_AXIS, ALU.add).then_inc(s_encfree, 1)
                        v.wait_ge(s_encfree, n * (GT // 2) + (GT // 2 + 2))
                        v.wait_ge(s_chain, n * 2 + 1)
                        v.tensor_tensor(alpha0[:, :, :], alpha0[:, :, :], dot[:, :, :], ALU.add).then_inc(s_chain, 1)
                        v.wait_ge(s_chain, n * 2 + 2)
                    else:
                        v.tensor_tensor(alpha0[:, :, :], weight(b), Gd[b][:, :, :], ALU.add).then_inc(s_chain, 1)
                        v.wait_ge(s_chain, n + 1)
                    v.wait_ge(s_below, n + 1)
                    v.scalar_tensor_tensor(alpha[:, :, :], alpha0[:, :, :], NEG_SLOPE, alpha0[:, :, :],
                                           ALU.mult, ALU.max).then_inc(s_alpha, 1)
                    v.wait_ge(s_aT, n + 1)
                    v.wait_ge(s_pen, n + 2)
                    v.tensor_tensor_scan(fwd[:, :], pen[:, 0:EP], p_t[0:GT * H, 0:EP], -BIG,
                                         ALU.add, ALU.max).then_inc(s_scan, 1)
                    v.tensor_tensor_scan(bwd[:, ::-1], pen[:, 1:EP + 1][:, ::-1], p_t[0:GT * H, 0:EP][:, ::-1], -BIG,
                                         ALU.add, ALU.max).then_inc(s_scan, 1)
                    v.wait_ge(s_scan, n * 2 + 2)
                    v.tensor_tensor(top[:, :], fwd[:, :], bwd[:, :], ALU.max).then_inc(s_top, 1)
                    v.wait_ge(s_mT, n + 1)
                    v.tensor_tensor(below[:, :, :], alpha[:, :, :], p_m[0:EP, 0:GT * H].rearrange("p (c h) -> p c h", h=H),
                                    ALU.subtract).then_inc(s_below, 1)
                    v.wait_ge(s_exp, n + 1)
                    for c in range(GT):
                        hc = Gs[b][:, c, 0:MSG].rearrange("p (h w) -> p h w", w=HW)
                        last = v.tensor_tensor(hc[:, :, 0:DH], hc[:, :, 0:DH],
                                               hc[:, :, DH:HW].to_broadcast([EP, H, DH]), ALU.mult)
                    last.then_inc(s_msg, 1)


def combine(nc, io, g, layer, totals, firsts, X):
    with Phase(nc, f"combine{layer}") as ph:
        fs = ph.sb("fs", [FQ, FT, ROW + 1])
        dstf = ph.sb("dstf", [FQ, FT])
        dstf_i, prev_i = ph.sb("dstf_i", [FQ, FT], I32), ph.sb("prev_i", [FQ, FT], I32)
        dstx_i, prevx_i = ph.sb("dstx_i", [H, ET], I32), ph.sb("prevx_i", [H, ET], I32)
        isfirst = ph.sb("isfirst", [FQ, FT])
        penf = ph.sb("penf", [H, ET + 1])
        iota = ph.sb("iota", [FQ, NP])
        ones = ph.sb("ones", [FQ, FT])
        fwd, bwd, top = ph.sb("fwd", [H, ET]), ph.sb("bwd", [H, ET]), ph.sb("top", [H, ET])
        scale = ph.sb("scale", [FQ, FT, H])
        tab = ph.sb("tab", [P, NT, ROW])
        hot = ph.sb("hot", [FQ, 2, FT, P])
        far = ph.sb("far", [P, 1])
        m1, m = ph.sb("m1", [P, H]), ph.sb("m", [P, H])
        ex = ph.sb("ex", [P, 3, H])
        low = ph.sb("low", [P, H])
        part = ph.sb("part", [P, H, HW])
        den, rden = ph.sb("den", [P, H]), ph.sb("rden", [P, H])
        biasrow = ph.sb("biasrow", [P, D])
        p_t = ph.ps("p_t", [P, 512])
        p_m = ph.ps("p_m", [P, 512])
        p_n = ph.ps("p_n", [P, 2, 512])
        s_in, s_mT, s_f, s_scan, s_top, s_back = (ph.sem(x) for x in ("in", "mT", "f", "scan", "top", "back"))
        s_scale, s_exp, s_fs, s_hot, s_sum, s_chain, s_e, s_used = (
            ph.sem(x) for x in ("scale", "exp", "fs", "hot", "sum", "chain", "e", "used"))
        block = ph.open()
        loads = [(fs[:, :, 0:ROW], firsts.rearrange("(b q) w -> q b w", q=FQ)), (dstf_i[:, :], io["dst_f"]),
                 (prev_i[:, :], io["prev_f"]), (dstx_i[:, :], io["dst_fx"]), (prevx_i[:, :], io["prev_fx"]),
                 (iota[:, :], io["iota"].partition_broadcast(FQ)),
                 (tab[:, :, :], totals.rearrange("(t p) w -> p t w", p=P)),
                 (biasrow[:, :], io["gnn_bias"].partition_broadcast(P))]

        @block.sync
        def _(sp):
            for out, in_ in loads:
                sp.dma_start(out, in_).then_inc(s_in, 16)

        @block.tensor
        def _(pe):
            pe.wait_ge(s_in, 16 * len(loads))
            for b in range(FT):
                mm = pe.transpose(p_t[0:H, b * FQ:(b + 1) * FQ], fs[:, b, MSG:ROW], g["ident"][0:FQ, 0:FQ])
            mm.then_inc(s_mT, 1)
            pe.wait_ge(s_top, 1)
            for b in range(FT):
                mm = pe.transpose(p_m[0:FQ, b * H:(b + 1) * H], top[:, b * FQ:(b + 1) * FQ], g["ident"][0:H, 0:H])
            mm.then_inc(s_back, 1)
            pe.wait_ge(s_fs, 3)
            for t in range(NT):
                pe.wait_ge(s_hot, t + 1)
                if t >= 2:
                    pe.wait_ge(s_used, t - 1)
                for b in range(FT):
                    mm = pe.matmul(p_n[:, t % 2, 0:ROW + 1], hot[:, t % 2, b, :], fs[:, b, :],
                                   start=(b == 0), stop=(b == FT - 1))
                mm.then_inc(s_sum, 1)

        @block.scalar
        def _(act):
            act.wait_ge(s_scale, 1)
            act.activation(scale[:, :, :], scale[:, :, :], ACT.Exp).then_inc(s_exp, 1)
            for t in range(NT):
                act.wait_ge(s_e, t + 1)
                act.activation(ex[:, :, :], ex[:, :, :], ACT.Exp).then_inc(s_exp, 1)

        @block.vector
        def _(v):
            steps = [0]

            def step(ins):
                steps[0] += 1
                ins.then_inc(s_chain, 1)
                v.wait_ge(s_chain, steps[0])

            v.wait_ge(s_in, 16 * len(loads))
            step(v.memset(ones[:, :], 1.0))
            step(v.tensor_copy(dstf[:, :], dstf_i[:, :]))
            step(v.tensor_tensor(penf[:, 0:ET], dstx_i[:, :], prevx_i[:, :], ALU.not_equal))
            step(v.tensor_scalar(penf[:, 0:ET], penf[:, 0:ET], -BIG, None, ALU.mult))
            step(v.memset(penf[:, ET:ET + 1], 0.0))
            step(v.tensor_tensor(isfirst[:, :], dstf_i[:, :], prev_i[:, :], ALU.not_equal))
            v.wait_ge(s_mT, 1)
            v.tensor_tensor_scan(fwd[:, :], penf[:, 0:ET], p_t[0:H, 0:ET], -BIG, ALU.add, ALU.max).then_inc(s_scan, 1)
            v.tensor_tensor_scan(bwd[:, ::-1], penf[:, 1:ET + 1][:, ::-1], p_t[0:H, 0:ET][:, ::-1], -BIG,
                                 ALU.add, ALU.max).then_inc(s_scan, 1)
            v.wait_ge(s_scan, 2)
            v.tensor_tensor(top[:, :], fwd[:, :], bwd[:, :], ALU.max).then_inc(s_top, 1)
            v.wait_ge(s_back, 1)
            mf = p_m[0:FQ, 0:FT * H].rearrange("p (b h) -> p b h", h=H)
            v.tensor_tensor(scale[:, :, :], fs[:, :, MSG:ROW], mf, ALU.subtract).then_inc(s_scale, 1)
            v.wait_ge(s_scale, 1)
            v.tensor_tensor(fs[:, :, MSG:ROW], isfirst[:, :, None].to_broadcast([FQ, FT, H]), mf,
                            ALU.mult).then_inc(s_fs, 1)
            v.tensor_tensor(fs[:, :, ROW], isfirst[:, :], ones[:, :], ALU.mult).then_inc(s_fs, 1)
            v.wait_ge(s_exp, 1)
            for b in range(FT):
                f = fs[:, b, 0:MSG].rearrange("p (h w) -> p h w", w=HW)
                step(v.tensor_tensor(f, f, scale[:, b, :, None].to_broadcast([FQ, H, HW]), ALU.mult))
            v.sem_inc(s_fs, 1)
            for t in range(NT):
                if t >= 2:
                    v.wait_ge(s_sum, t - 1)
                v.tensor_tensor(hot[:, t % 2, :, :], iota[:, None, t * P:(t + 1) * P].to_broadcast([FQ, FT, P]),
                                dstf[:, :, None].to_broadcast([FQ, FT, P]), ALU.is_equal).then_inc(s_hot, 1)
                v.wait_ge(s_sum, t + 1)
                pn = p_n[:, t % 2, :]
                mt = tab[:, t, MSG:ROW]
                tb = tab[:, t, 0:MSG].rearrange("p (h w) -> p h w", w=HW)
                step(v.tensor_scalar(far[:, :], pn[:, ROW:ROW + 1], BIG, -BIG, ALU.mult, ALU.add))
                step(v.tensor_scalar(m1[:, :], pn[:, MSG:ROW], far[:, 0:1], None, ALU.add))
                step(v.tensor_tensor(m[:, :], m1[:, :], mt, ALU.max))
                step(v.tensor_tensor(ex[:, 0, :], mt, m[:, :], ALU.subtract))
                step(v.tensor_tensor(ex[:, 1, :], m1[:, :], m[:, :], ALU.subtract))
                v.tensor_scalar(ex[:, 2, :], m[:, :], 0.0, None, ALU.min).then_inc(s_e, 1)
                v.wait_ge(s_exp, t + 2)
                step(v.tensor_tensor(part[:, :, :], pn[:, 0:MSG].rearrange("p (h w) -> p h w", w=HW),
                                     ex[:, 1, :, None].to_broadcast([P, H, HW]), ALU.mult))
                step(v.tensor_tensor(tb, tb, ex[:, 0, :, None].to_broadcast([P, H, HW]), ALU.mult))
                v.tensor_tensor(part[:, :, :], part[:, :, :], tb, ALU.add).then_inc(s_used, 1)
                v.wait_ge(s_used, t + 1)
                if layer == 0:
                    step(v.tensor_scalar(den[:, :], part[:, :, DH], 1e-10, None, ALU.max))
                    step(v.reciprocal(rden[:, :], den[:, :]))
                else:
                    step(v.tensor_tensor(den[:, :], part[:, :, DH], ex[:, 2, :], ALU.mult))
                    step(v.tensor_scalar(den[:, :], den[:, :], 1e-12, None, ALU.add))
                    step(v.reciprocal(rden[:, :], den[:, :]))
                    step(v.tensor_tensor(rden[:, :], rden[:, :], ex[:, 2, :], ALU.mult))
                step(v.tensor_tensor(part[:, :, 0:DH], part[:, :, 0:DH], rden[:, :, None].to_broadcast([P, H, DH]),
                                     ALU.mult))
                xt = X[:, t, :].rearrange("p (h w) -> p h w", w=DH)
                step(v.tensor_tensor(xt, xt, part[:, :, 0:DH], ALU.add))
                if layer == 0:
                    step(v.tensor_tensor(X[:, t, :], X[:, t, :], biasrow[:, :], ALU.add))


DEPTH = 4
FF = 4 * D
FC = FF // P
KB = 10
KW = NP // KB
QK_SCALE = float(DH) ** -0.25
A_T, B_T = 2, 3
A_N, B_N = A_T * P, B_T * P


def attention(nc, g, w, S, turned, spare, ahead):
    wq, wk, wv, wo, bo = w
    qt = spare[:, :, :].rearrange("p t f -> p (t f)").rearrange("p (a n) -> p a n", a=HALF)
    with Phase(nc, "attn") as ph:
        kmx = ph.sb("kmx", [P, HALF, KB])
        kmax = ph.sb("kmax", [P, HALF])
        krow = ph.sb("krow", [1, D])
        ones = ph.sb("ones", [P, P])
        qmax, qsum, qrec = ph.sb("qmax", [P, 2, H]), ph.sb("qsum", [P, 2, H]), ph.sb("qrec", [P, 2, H])
        qs = ph.sb("qs", [P, 2, H, DH])
        ek = ph.sb("ek", [P, 2, D])
        vs = ph.sb("vs", [P, 2, D])
        ctx = ph.sb("ctx", [P, HALF, P])
        rk = ph.sb("rk", [P, HALF])
        M = ph.sb("M", [P, HALF, D])
        p_q = ph.ps("q", [P, 2, 512])
        p_kv = ph.ps("kv", [P, 2, 512])
        p_t = ph.ps("t", [P, 2, 512])
        p_c = ph.ps("c", [P, 512])
        p_s = ph.ps("s", [P, 512])
        names = ("ahead ones kT kmx kmax kTurned krow q kv v_done qmax qs qexp qsum qrec qn qt qt_out "
                 "ek vs ctx ctxm rk m mo o added")
        s = {n: ph.sem(n) for n in names.split()}
        block = ph.open()
        load_ahead(block, s["ahead"], ahead)

        def rows(t):
            return P if t < NT - 1 else LAST

        @block.tensor
        def _(pe):
            for c in range(KB):
                if c >= 2:
                    pe.wait_ge(s["kmx"], 2 * (c - 1))
                for a in range(HALF):
                    for i in range(HALF):
                        mm = pe.matmul((p_q, p_kv)[a][:, c % 2, 0:KW], wk[:, i, a * P:(a + 1) * P],
                                       turned[:, i, c * KW:(c + 1) * KW], start=(i == 0), stop=(i == HALF - 1))
                    mm.then_inc(s["kT"], 1)
            pe.wait_ge(s["kmax"], 1)
            for a in range(HALF):
                mm = pe.transpose(p_s[0:1, a * P:(a + 1) * P], kmax[:, a:a + 1], g["ident"][:, :])
            mm.then_inc(s["kTurned"], 1)
            pe.wait_ge(s["krow"], 1)
            pe.wait_ge(s["ones"], 1)

            def project(t):
                b = t % 2
                if t >= 2:
                    pe.wait_ge(s["qs"], t - 1)
                    pe.wait_ge(s["vs"], t - 1)
                at = slice(t * P, (t + 1) * P)
                for i in range(HALF):
                    mm = pe.matmul(p_q[:, b, 0:D], turned[:, i, at], wq[:, i, :], start=(i == 0), stop=(i == HALF - 1))
                mm.then_inc(s["q"], 1)
                for i in range(HALF):
                    pe.matmul(p_kv[:, b, 0:D], turned[:, i, at], wk[:, i, :], start=(i == 0), stop=False)
                pe.matmul(p_kv[:, b, 0:D], ones[0:1, :], krow[:, :], start=False, stop=True)
                for i in range(HALF):
                    mm = pe.matmul(p_kv[:, b, D:2 * D], turned[:, i, at], wv[:, i, :], start=(i == 0), stop=(i == HALF - 1))
                mm.then_inc(s["kv"], 1)

            def contract(t):
                b, r = t % 2, rows(t)
                pe.wait_ge(s["vs"], t + 1)
                for a in range(HALF):
                    pe.matmul(p_c[:, a * P:(a + 1) * P], vs[0:r, b, a * P:(a + 1) * P], ek[0:r, b, a * P:(a + 1) * P],
                              start=(t == 0 and a == 0), stop=(t == NT - 1), skip_group_check=True)
                for a in range(HALF):
                    mm = pe.matmul(p_c[:, D + a:D + a + 1], ek[0:r, b, a * P:(a + 1) * P], ones[0:r, 0:1],
                                   start=False, stop=(t == NT - 1), skip_group_check=True)
                mm.then_inc(s["ctx"], 1)
                pe.wait_ge(s["qn"], t + 1)
                if t >= 2:
                    pe.wait_ge(s["qt_out"], t - 1)
                for a in range(HALF):
                    mm = pe.transpose(p_t[:, b, a * P:(a + 1) * P],
                                      qs[:, b, :, :].rearrange("p h w -> p (h w)")[:, a * P:(a + 1) * P], g["ident"][:, :])
                mm.then_inc(s["qt"], 1)

            for t in range(NT):
                project(t)
                if t:
                    contract(t - 1)
            contract(NT - 1)
            pe.wait_ge(s["ctxm"], 2)
            for a in range(HALF):
                mm = pe.matmul(p_s[:, a * D:(a + 1) * D], ctx[:, a, :], wo[:, a, :], start=True, stop=True)
            mm.then_inc(s["m"], 1)
            pe.wait_ge(s["mo"], 2)
            pe.wait_ge(s["qt_out"], NT)
            for t in range(NT):
                if t >= 2:
                    pe.wait_ge(s["added"], t - 1)
                for a in range(HALF):
                    pe.matmul(p_q[:, t % 2, 0:D], qt[:, a, t * P:(t + 1) * P], M[:, a, :], start=(a == 0), stop=False)
                pe.matmul(p_q[:, t % 2, 0:D], ones[0:1, :], bo[:, :], start=False, stop=True).then_inc(s["o"], 1)

        @block.scalar
        def _(act):
            def keys(t):
                b = t % 2
                act.wait_ge(s["kv"], t + 1)
                if t >= 2:
                    act.wait_ge(s["ctx"], t - 1)
                act.activation(ek[:, b, :], p_kv[:, b, 0:D], ACT.Exp, scale=QK_SCALE).then_inc(s["ek"], 1)
                act.activation(vs[:, b, :], p_kv[:, b, D:2 * D], ACT.Copy).then_inc(s["vs"], 1)

            def turned_queries(t):
                act.wait_ge(s["qt"], t + 1)
                act.activation(qt[:, :, t * P:(t + 1) * P], p_t[:, t % 2, 0:D].rearrange("p (a n) -> p a n", a=HALF),
                               ACT.Copy).then_inc(s["qt_out"], 1)

            for t in range(NT):
                act.wait_ge(s["qs"], t + 1)
                act.activation(qs[:, t % 2, :, :], qs[:, t % 2, :, :], ACT.Exp, scale=QK_SCALE).then_inc(s["qexp"], 1)
                keys(t)
                if t:
                    turned_queries(t - 1)
            turned_queries(NT - 1)

        @block.vector
        def _(v):
            v.memset(ones[:, :], 1.0).then_inc(s["ones"], 1)
            for c in range(KB):
                w_ = min(KW, N - c * KW)
                for a in range(HALF):
                    v.wait_ge(s["kT"], HALF * c + a + 1)
                    v.tensor_reduce(kmx[:, a, c:c + 1], (p_q, p_kv)[a][:, c % 2, 0:w_], X_AXIS, ALU.max).then_inc(s["kmx"], 1)
            v.wait_ge(s["kmx"], HALF * KB)
            v.tensor_reduce(kmax[:, :], kmx[:, :, :], X_AXIS, ALU.max).then_inc(s["kmax"], 1)
            v.wait_ge(s["kTurned"], 1)
            v.tensor_scalar(krow[:, :], p_s[0:1, 0:D], -1.0, None, ALU.mult).then_inc(s["krow"], 1)

            def shift(t):
                b = t % 2
                v.wait_ge(s["q"], t + 1)
                q = p_q[:, b, 0:D].rearrange("p (h w) -> p h w", w=DH)
                v.tensor_reduce(qmax[:, b, :], q, X_AXIS, ALU.max).then_inc(s["qmax"], 1)
                v.wait_ge(s["qmax"], t + 1)
                if t >= 2:
                    v.wait_ge(s["qt"], t - 1)
                v.tensor_tensor(qs[:, b, :, :], q, qmax[:, b, :, None].to_broadcast([P, H, DH]),
                                ALU.subtract).then_inc(s["qs"], 1)

            def scale(t):
                b = t % 2
                v.wait_ge(s["qexp"], t + 1)
                v.tensor_reduce(qsum[:, b, :], qs[:, b, :, :], X_AXIS, ALU.add).then_inc(s["qsum"], 1)
                v.wait_ge(s["qsum"], t + 1)
                v.reciprocal(qrec[:, b, :], qsum[:, b, :]).then_inc(s["qrec"], 1)
                v.wait_ge(s["qrec"], t + 1)
                v.tensor_tensor(qs[:, b, :, :], qs[:, b, :, :], qrec[:, b, :, None].to_broadcast([P, H, DH]),
                                ALU.mult).then_inc(s["qn"], 1)

            for t in range(NT):
                shift(t)
                scale(t)
            v.wait_ge(s["ctx"], NT)
            v.reciprocal(rk[:, :], p_c[:, D:D + HALF]).then_inc(s["rk"], 1)
            for a in range(HALF):
                v.tensor_tensor(ctx[:, a, :], p_c[:, a * P:(a + 1) * P], g["blocks"][:, :], ALU.mult).then_inc(s["ctxm"], 1)
            v.wait_ge(s["m"], 1)
            v.wait_ge(s["rk"], 1)
            for a in range(HALF):
                v.tensor_scalar(M[:, a, :], p_s[:, a * D:(a + 1) * D], rk[:, a:a + 1], None, ALU.mult).then_inc(s["mo"], 1)
            for t in range(NT):
                v.wait_ge(s["o"], t + 1)
                v.tensor_tensor(S[:, t, :], S[:, t, :], p_q[:, t % 2, 0:D], ALU.add).then_inc(s["added"], 1)


def mlp(nc, g, name, S, turned, weights, ahead=(), experts=1, load=None, gates=None):
    with Phase(nc, name) as ph:
        hid = (ph.sb("hid_a", [P, FC, A_N]), ph.sb("hid_b", [P, FC, B_N]))
        ones = ph.sb("ones", [1, P])
        p_u = ph.ps("u", [P, 4, 512])
        p_d = ph.ps("d", [P, 3, 512])
        p_b = ph.ps("b", [P, 512])
        s_ahead, s_ones, s_up, s_hid, s_down, s_added, s_passed = (
            ph.sem(x) for x in ("ahead", "ones", "up", "hid", "down", "added", "passed"))
        s_w = [ph.sem(f"w{b}") for b in range(2)]
        s_folded, s_pb = ph.sem("folded"), ph.sem("pb")
        block = ph.open()
        load_ahead(block, s_ahead, ahead)
        width, first, tiles = (A_N, B_N), (0, A_N), (A_T, B_T)
        grouped = experts > 1
        UPS, DOWNS = NB * 2 * FC, NT

        def each(eng):
            if not grouped:
                yield 0, 0, 0, False
                return
            with eng.Fori(0, experts // 2 - 1) as pair:
                for b in range(2):
                    yield pair * 2 + b, b, pair, True
            for b in range(2):
                yield experts - 2 + b, b, experts // 2 - 1, b == 0

        n_loads = len(load(0, 0)) if grouped else 0

        def here(eng, b, pair):
            eng.wait_ge(s_w[b], pair * (16 * n_loads) + 16 * n_loads)

        if grouped:
            @block.sync
            def _(sp):
                def fetch(e, b):
                    for out, in_ in load(e, b):
                        sp.dma_start(out, in_).then_inc(s_w[b], 16)

                fetch(0, 0)
                fetch(1, 1)
                with sp.Fori(0, experts // 2 - 1) as pair:
                    for b in range(2):
                        gate(sp, s_down, (pair * 2 + b) * DOWNS + (U + DOWNS), s_passed)
                        fetch(pair * 2 + (b + 2), b)

        @block.tensor
        def _(pe):
            def up(e, b, k, part):
                for f in range(FC):
                    n = part * FC + f
                    pe.wait_ge(s_hid, e * UPS + k * (2 * FC) + (n + 1))
                    for i in range(HALF):
                        mm = pe.matmul(p_u[:, n % 4, 0:width[part]], weights[b]["w1"][:, i, f * P:(f + 1) * P],
                                       turned[:, i, bass.ds(k * (U * P) + first[part], width[part])],
                                       start=(i == 0), stop=(i == HALF - 1))
                    mm.then_inc(s_up, 1)

            def down(e, b, k, part):
                pe.wait_ge(s_hid, e * UPS + k * (2 * FC) + ((part + 1) * FC + 4))
                for j in range(tiles[part]):
                    n = part * A_T + j
                    pe.wait_ge(s_added, e * DOWNS + k * U + (n + 1))
                    for f in range(FC):
                        pe.matmul(p_d[:, n % 3, 0:D], hid[part][:, f, j * P:(j + 1) * P],
                                  weights[b]["w2"][:, f, :], start=(f == 0), stop=False)
                    pe.matmul(p_d[:, n % 3, 0:D], ones[:, :], weights[b]["b2"][:, :], start=False,
                              stop=True).then_inc(s_down, 1)

            def fold(b, pair):
                here(pe, b, pair)
                for f in range(FC):
                    for i in range(HALF):
                        mm = pe.matmul(p_b[:, f:f + 1], weights[b]["w1"][:, i, f * P:(f + 1) * P],
                                       weights[b]["ln_b"][:, i:i + 1], start=(i == 0), stop=(i == HALF - 1))
                mm.then_inc(s_pb, 1)

            pe.sem_inc(s_down, U)
            pe.wait_ge(s_ones, 1)
            if grouped:
                fold(0, 0)
            for e, b, pair, more in each(pe):
                if grouped:
                    pe.wait_ge(s_folded, (HALF + 1) * (e + 1))
                up(e, b, 0, 0)
                with pe.Fori(0, NB - 1) as k:
                    up(e, b, k, 1)
                    down(e, b, k, 0)
                    up(e, b, k + 1, 0)
                    down(e, b, k, 1)
                up(e, b, NB - 1, 1)
                down(e, b, NB - 1, 0)
                if more:
                    fold(1 - b, pair + b)
                down(e, b, NB - 1, 1)

        @block.scalar
        def _(act):
            act.sem_inc(s_hid, 4)
            for e, b, pair, more in each(act):
                if grouped:
                    act.wait_ge(s_folded, (HALF + 1) * (e + 1))
                with act.Fori(0, NB) as k:
                    for part in range(2):
                        act.wait_ge(s_down, e * DOWNS + k * U + (first[part] // P + tiles[part]))
                        for f in range(FC):
                            n = part * FC + f
                            act.wait_ge(s_up, e * UPS + k * (2 * FC) + (n + 1))
                            act.activation(hid[part][:, f, :], p_u[:, n % 4, 0:width[part]], ACT.Gelu,
                                           bias=weights[b]["b1"][:, f:f + 1]).then_inc(s_hid, 1)

        @block.vector
        def _(v):
            v.memset(ones[:, :], 1.0).then_inc(s_ones, 1)
            v.sem_inc(s_added, 2)

            def fold(b, pair, count):
                w = weights[b]
                here(v, b, pair)
                v.wait_ge(s_pb, count)
                v.tensor_tensor(w["b1"][:, :], w["b1"][:, :], p_b[:, 0:FC], ALU.add).then_inc(s_folded, 1)
                for i in range(HALF):
                    v.tensor_scalar(w["w1"][:, i, :], w["w1"][:, i, :], w["ln_g"][:, i:i + 1], None,
                                    ALU.mult).then_inc(s_folded, 1)

            def add(e, k, n):
                v.wait_ge(s_down, e * DOWNS + k * U + (U + n + 1))
                if grouped:
                    v.scalar_tensor_tensor(S[:, k * U + n, :], p_d[:, n % 3, 0:D], gates[:, k * U + n, bass.ds(e, 1)],
                                           S[:, k * U + n, :], ALU.mult, ALU.add).then_inc(s_added, 1)
                else:
                    v.tensor_tensor(S[:, k * U + n, :], S[:, k * U + n, :], p_d[:, n % 3, 0:D],
                                    ALU.add).then_inc(s_added, 1)

            if grouped:
                fold(0, 0, 1)
            for e, b, pair, more in each(v):
                with v.Fori(0, NB - 1) as k:
                    for n in range(U):
                        add(e, k, n)
                for n in range(U):
                    if more and n == A_T:
                        fold(1 - b, pair + b, e + 2)
                    add(e, NB - 1, n)


def mixer(nc, io, g, S, turned, spare):
    with ExitStack() as ctx:
        def sb(name, shape, dtype=F32):
            return ctx.enter_context(nc.sbuf_tensor("mix_" + name, shape, dtype))

        lnp = sb("lnp", [P, 4, HALF])
        wq, wk, wv, wo = (sb(n, [P, HALF, D]) for n in ("wq", "wk", "wv", "wo"))
        bo, b2 = sb("bo", [1, D]), sb("b2", [1, D])
        w1, w2, b1 = sb("w1", [P, HALF, FF]), sb("w2", [P, FC, D]), sb("b1", [P, FC])
        with nc.Fori(0, DEPTH) as layer:
            with Phase(nc, "mixln") as ph:
                loaded = ph.sem("loaded")
                block = ph.open()
                load_ahead(block, loaded, [(lnp[:, :, :], io["mix_ln"][layer])])
            halves = lambda name: io[name][layer].rearrange("(a p) o -> p a o", p=P)
            norm(nc, "mixnorm1", S, spare, turned, g["ident"], lnp[:, 0, :], lnp[:, 1, :],
                 [(wq[:, :, :], halves("wq")), (wk[:, :, :], halves("wk")), (wv[:, :, :], halves("wv")),
                  (wo[:, :, :], halves("wo")), (bo[:, :], io["bo"][bass.ds(layer, 1), :])])
            attention(nc, g, (wq, wk, wv, wo, bo), S, turned, spare,
                      [(w1[:, :, :], halves("w1")), (w2[:, :, :], halves("w2")),
                       (b1[:, :], io["mix_b1"][layer]), (b2[:, :], io["mix_b2"][bass.ds(layer, 1), :])])
            norm(nc, "mixnorm2", S, spare, turned, g["ident"], lnp[:, 2, :], lnp[:, 3, :])
            mlp(nc, g, "mixff", S, turned, [{"w1": w1, "w2": w2, "b1": b1, "b2": b2}])


def add_to(nc, X, S):
    with Phase(nc, "addto") as ph:
        s_done = ph.sem("done")
        block = ph.open()

        @block.vector
        def _(v):
            with v.Fori(0, NB) as k:
                v.tensor_tensor(X[:, bass.ds(k * U, U), :], X[:, bass.ds(k * U, U), :], S[:, bass.ds(k * U, U), :],
                                ALU.add).then_inc(s_done, 1)


def route(nc, g, turned, wr, br, gates, top2, iota8):
    with Phase(nc, "route2" if top2 else "route") as ph:
        logits = ph.sb("logits", [P, NT, R])
        m = ph.sb("m", [P, NT])
        best = ph.sb("best", [P, NT, 8])
        where = ph.sb("where", [P, NT, 8], U32)
        where_f = ph.sb("where_f", [P, NT, 2])
        hot = ph.sb("hot", [P, NT, R])
        den = ph.sb("den", [P, NT])
        ones = ph.sb("ones", [1, P])
        p_l = ph.ps("l", [P, 512])
        s_ones, s_l, s_x, s_e, s_best, s_where = (ph.sem(x) for x in ("ones", "l", "x", "e", "best", "where"))
        block = ph.open()

        @block.tensor
        def _(pe):
            pe.wait_ge(s_ones, 1)
            for t in range(NT):
                for a in range(HALF):
                    pe.matmul(p_l[:, t * R:(t + 1) * R], turned[:, a, t * P:(t + 1) * P], wr[:, a, :],
                              start=(a == 0), stop=False)
                mm = pe.matmul(p_l[:, t * R:(t + 1) * R], ones[:, :], br[:, :], start=False, stop=True)
            mm.then_inc(s_l, 1)

        @block.scalar
        def _(act):
            act.wait_ge(s_x, 2)
            act.activation(logits[:, :, :], logits[:, :, :], ACT.Exp).then_inc(s_e, 1)

        @block.vector
        def _(v):
            steps = [0]

            def step(ins):
                steps[0] += 1
                ins.then_inc(s_x, 1)
                v.wait_ge(s_x, steps[0])

            v.memset(ones[:, :], 1.0).then_inc(s_ones, 1)
            v.wait_ge(s_l, 1)
            lg = p_l[:, 0:NT * R].rearrange("p (t e) -> p t e", e=R)
            step(v.tensor_reduce(m[:, :], lg, X_AXIS, ALU.max))
            step(v.tensor_tensor(logits[:, :, :], lg, m[:, :, None].to_broadcast([P, NT, R]), ALU.subtract))
            v.wait_ge(s_e, 1)
            step(v.tensor_reduce(den[:, :], logits[:, :, :], X_AXIS, ALU.add))
            step(v.reciprocal(m[:, :], den[:, :]))
            probs = logits if top2 else gates
            step(v.tensor_tensor(probs[:, :, :], logits[:, :, :], m[:, :, None].to_broadcast([P, NT, R]), ALU.mult))
            if top2:
                for t in range(NT):
                    v.max(best[:, t, :], probs[:, t, :]).then_inc(s_best, 1)
                v.wait_ge(s_best, NT)
                for t in range(NT):
                    v.max_index(where[:, t, :], best[:, t, :], probs[:, t, :]).then_inc(s_where, 1)
                v.wait_ge(s_where, NT)
                step(v.tensor_copy(where_f[:, :, :], where[:, :, 0:2]))
                step(v.tensor_tensor(den[:, :], best[:, :, 0], best[:, :, 1], ALU.add))
                step(v.reciprocal(m[:, :], den[:, :]))
                step(v.tensor_tensor(best[:, :, 0:2], best[:, :, 0:2], m[:, :, None].to_broadcast([P, NT, 2]), ALU.mult))
                for n, to in ((0, gates), (1, hot)):
                    step(v.tensor_tensor(to[:, :, :], where_f[:, :, n, None].to_broadcast([P, NT, R]),
                                         iota8[:, None, :].to_broadcast([P, NT, R]), ALU.is_equal))
                    step(v.tensor_tensor(to[:, :, :], to[:, :, :], best[:, :, n, None].to_broadcast([P, NT, R]), ALU.mult))
                step(v.tensor_tensor(gates[:, :, :], gates[:, :, :], hot[:, :, :], ALU.add))


QS = float(DH) ** 0.25


def taylor_project(nc, g, w, turned, QK, v1, fac, ahead=()):
    wqkv, bqkv, temp, valid = w
    with Phase(nc, "tproj") as ph:
        ones = ph.sb("ones", [1, P])
        sq = ph.sb("sq", [P, 2, 2 * D])
        ssq = ph.sb("ssq", [P, NT, 2, H])
        nrm = ph.sb("nrm", [P, NT, 2, H])
        p_qk = ph.ps("qk", [P, 2, 512])
        p_v = ph.ps("v", [P, 2, 512])
        names = "ahead ones qk v qk_out v_out sq ssq root x"
        s = {n: ph.sem(n) for n in names.split()}
        block = ph.open()
        load_ahead(block, s["ahead"], ahead)

        @block.tensor
        def _(pe):
            pe.wait_ge(s["ones"], 1)
            for t in range(NT):
                if t >= 2:
                    pe.wait_ge(s["v_out"], t - 1)
                at = slice(t * P, (t + 1) * P)
                for out, c0, c1, done in ((p_qk, 0, 2 * D, "qk"), (p_v, 2 * D, 3 * D, "v")):
                    for a in range(HALF):
                        pe.matmul(out[:, t % 2, 0:c1 - c0], turned[:, a, at], wqkv[:, a, c0:c1], start=(a == 0), stop=False)
                    pe.matmul(out[:, t % 2, 0:c1 - c0], ones[:, :], bqkv[:, c0:c1], start=False,
                              stop=True).then_inc(s[done], 1)

        @block.scalar
        def _(act):
            for t in range(NT):
                act.wait_ge(s["qk"], t + 1)
                act.activation(QK[:, t, :], p_qk[:, t % 2, :], ACT.Copy).then_inc(s["qk_out"], 1)
                act.wait_ge(s["v"], t + 1)
                act.activation(v1[:, t, :, 1:HW], p_v[:, t % 2, 0:D].rearrange("p (h w) -> p h w", w=DH),
                               ACT.Copy, scale=valid[:, t:t + 1]).then_inc(s["v_out"], 1)
            act.wait_ge(s["ssq"], NT)
            act.activation(nrm[:, :, :, :], ssq[:, :, :, :], ACT.Sqrt).then_inc(s["root"], 1)

        @block.vector
        def _(v):
            v.memset(ones[:, :], 1.0).then_inc(s["ones"], 1)
            v.tensor_copy(v1[:, :, :, 0], valid[:, :, None].to_broadcast([P, NT, H])).then_inc(s["x"], 1)
            for t in range(NT):
                v.wait_ge(s["qk_out"], t + 1)
                v.tensor_tensor(sq[:, t % 2, :], QK[:, t, :], QK[:, t, :], ALU.mult).then_inc(s["sq"], 1)
                v.wait_ge(s["sq"], t + 1)
                v.tensor_reduce(ssq[:, t, :, :], sq[:, t % 2, :].rearrange("p (s h w) -> p s h w", s=2, w=DH),
                                X_AXIS, ALU.add).then_inc(s["ssq"], 1)
            v.wait_ge(s["root"], 1)
            v.tensor_scalar(nrm[:, :, 0, :], nrm[:, :, 0, :], QS, 1e-12, ALU.mult, ALU.max).then_inc(s["x"], 1)
            v.tensor_scalar(nrm[:, :, 1, :], nrm[:, :, 1, :], 1e-12, None, ALU.max).then_inc(s["x"], 1)
            v.wait_ge(s["x"], 3)
            v.reciprocal(fac[:, :, :, :], nrm[:, :, :, :]).then_inc(s["x"], 1)
            v.wait_ge(s["x"], 4)
            v.tensor_scalar(fac[:, :, 1, :], fac[:, :, 1, :], QS, None, ALU.mult).then_inc(s["x"], 1)
            v.scalar_tensor_tensor(fac[:, :, 0, :], fac[:, :, 0, :], QS * QS,
                                   temp[:, None, :].to_broadcast([P, NT, H]), ALU.mult, ALU.mult).then_inc(s["x"], 1)


PAIRS = DH * DH // P
PER_BANK = 15


def taylor_keys(nc, g, QK, v1, fac, kv2, kv1, kv0):
    with Phase(nc, "tkeys") as ph:
        krow = ph.sb("krow", [P, 1, H, DH])
        kk = ph.sb("kk", [P, 2, DH, DH])
        ones = ph.sb("ones", [P, 1])
        zero = ph.sb("zero", [P, 512])
        p2 = ph.ps("p2", [P, 5, 512])
        p1 = ph.ps("p1", [P, 512])
        p0 = ph.ps("p0", [P, 512])
        names = "init k kk pp lin out"
        s = {n: ph.sem(n) for n in names.split()}
        block = ph.open()
        half_w = H // HALF * HW

        @block.tensor
        def _(pe):
            pe.wait_ge(s["init"], 2)
            pe.sem_inc(s["pp"], 2)
            pe.sem_inc(s["lin"], 1)
            for bank in [p2[:, n, :] for n in range(5)] + [p1[:, :]]:
                pe.matmul(bank, zero[:, 0:P], zero[:, :], start=True, stop=False, skip_group_check=True)
            pe.matmul(p0[0:1, :], zero[:, 0:1], zero[:, :], start=True, stop=False, skip_group_check=True)
            with pe.Fori(0, NT) as t:
                for h in range(H):
                    pe.wait_ge(s["kk"], t * H + (h + 1))
                    for c in range(PAIRS):
                        n = h * PAIRS + c
                        mm = pe.matmul(p2[:, n // PER_BANK, n % PER_BANK * HW:(n % PER_BANK + 1) * HW],
                                       kk[:, h % 2, :, :].rearrange("p i j -> p (i j)")[:, c * P:(c + 1) * P],
                                       v1[:, t, h, :], start=False, stop=False, skip_group_check=True)
                    mm.then_inc(s["pp"], 1)
                for a in range(HALF):
                    pe.matmul(p1[:, a * half_w:(a + 1) * half_w],
                              krow[:, 0, :, :].rearrange("p h w -> p (h w)")[:, a * P:(a + 1) * P],
                              v1[:, t, a * (H // HALF):(a + 1) * (H // HALF), :].rearrange("p h w -> p (h w)"),
                              start=False, stop=False, skip_group_check=True)
                pe.matmul(p0[0:1, 0:MSG], ones[:, :], v1[:, t, :, :].rearrange("p h w -> p (h w)"),
                          start=False, stop=False, skip_group_check=True).then_inc(s["lin"], 1)

        @block.vector
        def _(v):
            v.memset(ones[:, :], 1.0).then_inc(s["init"], 1)
            v.memset(zero[:, :], 0.0).then_inc(s["init"], 1)
            with v.Fori(0, NT) as t:
                v.wait_ge(s["lin"], t + 1)
                v.tensor_tensor(krow[:, 0, :, :], QK[:, t, D:2 * D].rearrange("p (h w) -> p h w", w=DH),
                                fac[:, t, 1, :, None].to_broadcast([P, H, DH]), ALU.mult).then_inc(s["k"], 1)
                v.wait_ge(s["k"], t + 1)
                for h in range(H):
                    v.wait_ge(s["pp"], t * H + (h + 1))
                    v.tensor_tensor(kk[:, h % 2, :, :], krow[:, 0, h, :, None].to_broadcast([P, DH, DH]),
                                    krow[:, 0, h, None, :].to_broadcast([P, DH, DH]), ALU.mult).then_inc(s["kk"], 1)
            v.wait_ge(s["lin"], NT + 1)
            for n0 in range(0, H * PAIRS, PER_BANK):
                n = min(PER_BANK, H * PAIRS - n0)
                v.tensor_scalar(kv2[:, n0:n0 + n, :], p2[:, n0 // PER_BANK, 0:n * HW].rearrange("p (c w) -> p c w", w=HW),
                                0.5 / N, None, ALU.mult).then_inc(s["out"], 1)
            v.scalar_tensor_tensor(kv1[:, :, :], p1[:, 0:MSG].rearrange("p (h w) -> p h w", w=HW),
                                   QS ** 2 / N, g["head4"][:, :, None].to_broadcast([P, H, HW]),
                                   ALU.mult, ALU.mult).then_inc(s["out"], 1)
            v.tensor_scalar(kv0[:, :], p0[0:1, 0:MSG], QS ** 4 / N, None, ALU.mult).then_inc(s["out"], 1)


def taylor_queries(nc, g, w, QK, fac, kv2, kv1, kv0, X):
    wp, bp, sel_i, sel_j = w
    with Phase(nc, "tqueries") as ph:
        qrow = ph.sb("qrow", [P, H, DH])
        qt = ph.sb("qt", [P, HALF, P])
        rj = ph.sb("rj", [P, 2, P])
        qq = ph.sb("qq", [P, 2, PAIRS, P])
        y = ph.sb("y", [P, H, DH])
        rec = ph.sb("rec", [P, H])
        yt = ph.sb("yt", [P, HALF, P])
        ones = ph.sb("ones", [1, P])
        p_m = ph.ps("m", [P, 512])
        p_o = ph.ps("o", [P, 512])
        p_j = ph.ps("j", [P, 512])
        p_i = ph.ps("i", [P, 4, 512])
        p_y = ph.ps("y", [P, 512])
        names = "ones q qT qt j rj i qq yy rec y yT yt o added passed"
        s = {n: ph.sem(n) for n in names.split()}
        block = ph.open()
        per_half = H // HALF

        @block.tensor
        def _(pe):
            pe.wait_ge(s["ones"], 1)

            with pe.Fori(0, NT) as t:
                def select(h):
                    a, r = h // per_half, slice(h % per_half * DH, (h % per_half + 1) * DH)
                    pe.wait_ge(s["rj"], t * H + (h + 1))
                    pe.matmul(p_j[:, 0:P], sel_j[r, :], qt[r, a, :], start=True, stop=True).then_inc(s["j"], 1)
                    for half in range(2):
                        pe.wait_ge(s["qq"], t * (2 * H) + (2 * h + half + 1))
                        for c in range(PAIRS // 2):
                            mm = pe.matmul(p_i[:, h % 2 * 2 + half, c * P:(c + 1) * P],
                                           sel_i[r, half * (PAIRS // 2) + c, :], qt[r, a, :], start=True, stop=True)
                        mm.then_inc(s["i"], 1)

                def sums(h):
                    for half in range(2):
                        pe.wait_ge(s["qq"], t * (2 * H) + (2 * h + half + 5))
                        for c in range(half * (PAIRS // 2), (half + 1) * (PAIRS // 2)):
                            mm = pe.matmul(p_y[:, h * HW:(h + 1) * HW], qq[:, h % 2, c, :], kv2[:, h * PAIRS + c, :],
                                           start=False, stop=False, skip_group_check=True)
                    mm.then_inc(s["yy"], 1)

                gate(pe, s["q"], t + 1, s["passed"])
                for a in range(HALF):
                    mm = pe.transpose(p_m[:, a * P:(a + 1) * P],
                                      qrow[:, :, :].rearrange("p h w -> p (h w)")[:, a * P:(a + 1) * P], g["ident"][:, :])
                mm.then_inc(s["qT"], 1)
                gate(pe, s["qt"], t + 1, s["passed"])
                gate(pe, s["y"], t + 1, s["passed"])
                pe.matmul(p_y[:, 0:MSG], ones[:, :], kv0[:, :], start=True, stop=False, skip_group_check=True)
                for a in range(HALF):
                    at = slice(a * per_half, (a + 1) * per_half)
                    pe.matmul(p_y[:, a * per_half * HW:(a + 1) * per_half * HW], qt[:, a, :],
                              kv1[:, at, :].rearrange("p h w -> p (h w)"), start=False, stop=False, skip_group_check=True)
                select(0)
                for h in range(H):
                    if h + 1 < H:
                        select(h + 1)
                    sums(h)
                gate(pe, s["y"], t + 2, s["passed"])
                for a in range(HALF):
                    mm = pe.transpose(p_m[:, D + a * P:D + (a + 1) * P],
                                      y[:, :, :].rearrange("p h w -> p (h w)")[:, a * P:(a + 1) * P], g["ident"][:, :])
                mm.then_inc(s["yT"], 1)
                gate(pe, s["yt"], t + 1, s["passed"])
                gate(pe, s["added"], t + 1, s["passed"])
                for a in range(HALF):
                    pe.matmul(p_o[:, 0:D], yt[:, a, :], wp[:, a, :], start=(a == 0), stop=False)
                pe.matmul(p_o[:, 0:D], ones[:, :], bp[:, :], start=False, stop=True).then_inc(s["o"], 1)

        @block.scalar
        def _(act):
            act.sem_inc(s["rj"], 1)
            with act.Fori(0, NT) as t:
                act.wait_ge(s["qT"], t + 1)
                act.activation(qt[:, :, :], p_m[:, 0:D].rearrange("p (a n) -> p a n", a=HALF), ACT.Copy).then_inc(s["qt"], 1)
                for h in range(H):
                    act.wait_ge(s["j"], t * H + (h + 1))
                    act.wait_ge(s["qq"], t * (2 * H) + (2 * h + 2))
                    act.activation(rj[:, h % 2, :], p_j[:, 0:P], ACT.Copy).then_inc(s["rj"], 1)
                act.wait_ge(s["yT"], t + 1)
                act.activation(yt[:, :, :], p_m[:, D:2 * D].rearrange("p (a n) -> p a n", a=HALF), ACT.Copy).then_inc(s["yt"], 1)

        @block.vector
        def _(v):
            v.memset(ones[:, :], 1.0).then_inc(s["ones"], 1)
            v.sem_inc(s["qq"], 4)
            v.sem_inc(s["y"], 1)
            v.sem_inc(s["added"], 1)
            with v.Fori(0, NT) as t:
                v.wait_ge(s["y"], t + 1)
                v.tensor_tensor(qrow[:, :, :], QK[:, t, 0:D].rearrange("p (h w) -> p h w", w=DH),
                                fac[:, t, 0, :, None].to_broadcast([P, H, DH]), ALU.mult).then_inc(s["q"], 1)
                for h in range(H):
                    v.wait_ge(s["rj"], t * H + (h + 2))
                    if h >= 2:
                        v.wait_ge(s["yy"], t * H + (h - 1))
                    for half in range(2):
                        v.wait_ge(s["i"], t * (2 * H) + (2 * h + half + 1))
                        at = slice(half * (PAIRS // 2), (half + 1) * (PAIRS // 2))
                        v.tensor_tensor(qq[:, h % 2, at, :], p_i[:, h % 2 * 2 + half, :].rearrange("p (c n) -> p c n", n=P),
                                        rj[:, h % 2, None, :].to_broadcast([P, PAIRS // 2, P]), ALU.mult).then_inc(s["qq"], 1)
                v.wait_ge(s["yy"], t * H + H)
                yy = p_y[:, 0:MSG].rearrange("p (h w) -> p h w", w=HW)
                v.reciprocal(rec[:, :], yy[:, :, 0]).then_inc(s["rec"], 1)
                v.wait_ge(s["rec"], t + 1)
                v.tensor_tensor(y[:, :, :], yy[:, :, 1:HW], rec[:, :, None].to_broadcast([P, H, DH]), ALU.mult).then_inc(s["y"], 1)
                v.wait_ge(s["o"], t + 1)
                v.tensor_tensor(X[:, t, :], X[:, t, :], p_o[:, 0:D], ALU.add).then_inc(s["added"], 1)


def experts3(nc, g, X, turned, gates, ws, cols, bo):
    EX = R
    with Phase(nc, "experts3") as ph:
        h1 = ph.sb("h1", [P, 2, HALF, B_N])
        h2 = ph.sb("h2", [P, 2, HALF, B_N])
        scale, bias = ph.sb("scale", [P, 2, EX * HALF]), ph.sb("bias", [P, 2, EX * HALF])
        root = ph.sb("root", [P, 2, EX * HALF])
        ones = ph.sb("ones", [1, P])
        p_1 = ph.ps("p1", [P, 2, 512])
        p_2 = ph.ps("p2", [P, 2, 512])
        p_y = ph.ps("py", [P, 4, 512])
        names = "ones x root cols u1 h1 u2 h2 y added"
        s = {n: ph.sem(n) for n in names.split()}
        block = ph.open()
        width, first, tiles = (A_N, B_N), (0, A_N), (A_T, B_T)
        items = [(e, part) for e in range(EX) for part in range(2)]
        n_items = len(items)

        def per_item(k, m):
            return k * (HALF * n_items) + HALF * m

        @block.tensor
        def _(pe):
            pe.wait_ge(s["ones"], 1)
            with pe.Fori(0, NB) as k:
                def one(m):
                    e, part = items[m]
                    for f in range(HALF):
                        pe.wait_ge(s["h1"], per_item(k, m) + (f + 1))
                        for i in range(HALF):
                            mm = pe.matmul(p_1[:, f, 0:width[part]], ws[0][:, e, i, f * P:(f + 1) * P],
                                           turned[:, i, bass.ds(k * (U * P) + first[part], width[part])],
                                           start=(i == 0), stop=(i == HALF - 1))
                        mm.then_inc(s["u1"], 1)

                def two(m):
                    e, part = items[m]
                    pe.wait_ge(s["h1"], per_item(k, m) + 2 * HALF)
                    for f in range(HALF):
                        pe.wait_ge(s["h2"], per_item(k, m) + (f + 1))
                        for i in range(HALF):
                            mm = pe.matmul(p_2[:, f, 0:width[part]], ws[1][:, e, i, f * P:(f + 1) * P],
                                           h1[:, m % 2, i, 0:width[part]], start=(i == 0), stop=(i == HALF - 1))
                        mm.then_inc(s["u2"], 1)

                def three(m):
                    e, part = items[m]
                    pe.wait_ge(s["h2"], per_item(k, m) + 2 * HALF)
                    for j in range(tiles[part]):
                        n = e * U + part * A_T + j
                        pe.wait_ge(s["added"], k * (EX * U) + (n + 1))
                        for i in range(HALF):
                            pe.matmul(p_y[:, n % 4, 0:D], h2[:, m % 2, i, j * P:(j + 1) * P], ws[2][:, e, i, :],
                                      start=(i == 0), stop=False)
                        pe.matmul(p_y[:, n % 4, 0:D], ones[:, :], bo[:, e * D:(e + 1) * D], start=False,
                                  stop=True).then_inc(s["y"], 1)

                for m in range(n_items + 2):
                    if m < n_items:
                        one(m)
                    if 1 <= m <= n_items:
                        two(m - 1)
                    if m >= 2:
                        three(m - 2)

        @block.scalar
        def _(act):
            act.sem_inc(s["h1"], HALF)
            act.sem_inc(s["h2"], HALF)
            act.wait_ge(s["x"], 1)
            act.activation(root[:, :, :], root[:, :, :], ACT.Sqrt).then_inc(s["root"], 1)
            act.wait_ge(s["cols"], 2)
            with act.Fori(0, NB) as k:
                def relu(m, layer):
                    e, part = items[m]
                    up, out, hid, p_ = (("u1", "h1", h1, p_1), ("u2", "h2", h2, p_2))[layer]
                    for f in range(HALF):
                        act.wait_ge(s[up], per_item(k, m) + (f + 1))
                        act.activation(hid[:, m % 2, f, 0:width[part]], p_[:, f, 0:width[part]], ACT.Relu,
                                       bias=bias[:, layer, e * HALF + f:e * HALF + f + 1],
                                       scale=scale[:, layer, e * HALF + f:e * HALF + f + 1]).then_inc(s[out], 1)

                for m in range(n_items + 1):
                    if m < n_items:
                        relu(m, 0)
                    if m:
                        relu(m - 1, 1)

        @block.vector
        def _(v):
            v.memset(ones[:, :], 1.0).then_inc(s["ones"], 1)
            v.sem_inc(s["added"], 4)
            v.tensor_scalar(root[:, :, :], cols[:, :, 4, :], 0.001, None, ALU.add).then_inc(s["x"], 1)
            v.wait_ge(s["root"], 1)
            v.reciprocal(root[:, :, :], root[:, :, :]).then_inc(s["x"], 1)
            v.tensor_tensor(bias[:, :, :], cols[:, :, 0, :], cols[:, :, 3, :], ALU.subtract).then_inc(s["x"], 1)
            v.wait_ge(s["x"], 3)
            v.tensor_tensor(scale[:, :, :], cols[:, :, 1, :], root[:, :, :], ALU.mult).then_inc(s["cols"], 1)
            v.wait_ge(s["cols"], 1)
            v.tensor_tensor(bias[:, :, :], bias[:, :, :], scale[:, :, :], ALU.mult).then_inc(s["x"], 1)
            v.wait_ge(s["x"], 4)
            v.tensor_tensor(bias[:, :, :], bias[:, :, :], cols[:, :, 2, :], ALU.add).then_inc(s["cols"], 1)
            with v.Fori(0, NB) as k:
                for e, part in items:
                    for j in range(tiles[part]):
                        n = e * U + part * A_T + j
                        t = k * U + (part * A_T + j)
                        v.wait_ge(s["y"], k * (EX * U) + (n + 1))
                        v.scalar_tensor_tensor(X[:, t, :], p_y[:, n % 4, 0:D], gates[:, t, e:e + 1], X[:, t, :],
                                               ALU.mult, ALU.add).then_inc(s["added"], 1)


def build(nc, io, out, dbg=None):
    with ExitStack() as ctx:
        def sb(name, shape, dtype=F32, to=ctx):
            return to.enter_context(nc.sbuf_tensor(name, shape, dtype))

        def dram(name, shape):
            return nc.dram_tensor(name, shape, F32).ap()

        def halves(name, n=None):
            a = io[name] if n is None else io[name][n]
            return a.rearrange("(a p) o -> p a o", p=P)

        g = {n: sb("idx_" + n, [EP, ET + 2 * GT], I32) for n in ("src0", "dst0", "src1", "dst1", "put")}
        for layer in range(2):
            for n in ("got", "scattered"):
                g[f"{n}{layer}"] = [ctx.enter_context(nc.semaphore(f"{n}{layer}{b}")) for b in range(2)]
        g["dst"] = sb("idx_dst", [EP, ET], I32)
        g["ident"] = sb("ident", [P, P])
        g["blocks"] = sb("blocks", [P, P])
        g["head4"] = sb("head4", [P, H])
        iota8 = sb("iota8", [P, R])
        X = sb("X", [P, NT, D])
        XN = sb("XN", [P, NT, D])
        table0, table1 = dram("table0", [NP, ROW]), dram("table1", [R * NP, ROW])
        dtable1 = dram("dtable1", [R * NP, H])
        totals0, totals1 = dram("totals0", [NP, ROW]), dram("totals1", [NP, ROW])
        firsts0, firsts1 = dram("firsts0", [ET, ROW]), dram("firsts1", [ET, ROW])
        load_x(nc, io, X)
        edge_prep(nc, io, g, [(g["head4"][:, :], io["head4"]), (iota8[:, :], io["iota"][:, 0:R].partition_broadcast(P))])

        with ExitStack() as part:
            HT = sb("HT_g0", [P, HALF, NP], to=part)
            norm(nc, "norm0", X, XN, HT, g["ident"])
            gnn_table(nc, io, g, 0, HT, table0, None)
        edges(nc, io, g, 0, table0, None, totals0, firsts0)
        combine(nc, io, g, 0, totals0, firsts0, X)
        with ExitStack() as part:
            HT = sb("HT_m0", [P, HALF, NP], to=part)
            spare = sb("spare_m0", [P, NT, D], to=part)
            mixer(nc, io, g, XN, HT, spare)
        add_to(nc, X, XN)

        with ExitStack() as part:
            HT = sb("HT_f0", [P, HALF, NP], to=part)
            gates = sb("gates0", [P, NT, R], to=part)
            wr, br = sb("wr0", [P, HALF, R], to=part), sb("br0", [1, R], to=part)
            weights = [{"w1": sb(f"moe_w1{b}", [P, HALF, FF], to=part), "w2": sb(f"moe_w2{b}", [P, FC, D], to=part),
                        "b1": sb(f"moe_b1{b}", [P, FC], to=part), "b2": sb(f"moe_b2{b}", [1, D], to=part),
                        "ln_g": sb(f"moe_g{b}", [P, HALF], to=part), "ln_b": sb(f"moe_b{b}", [P, HALF], to=part)}
                       for b in range(2)]
            norm(nc, "norm1", X, XN, HT, g["ident"], ahead=[(wr[:, :, :], halves("wr0")), (br[:, :], io["br0"])])
            route(nc, g, HT, wr, br, gates, True, iota8)
            norm(nc, "norm2", XN, XN, HT, g["ident"])

            def load(e, b):
                w = weights[b]
                return [(w["w1"][:, :, :], halves("moe_w1", e)), (w["w2"][:, :, :], halves("moe_w2", e)),
                        (w["b1"][:, :], io["moe_b1"][e]), (w["b2"][:, :], io["moe_b2"][e]),
                        (w["ln_g"][:, :], io["moe_g"][e]), (w["ln_b"][:, :], io["moe_b"][e])]

            mlp(nc, g, "moe", X, HT, weights, experts=R, load=load, gates=gates)

        with ExitStack() as part:
            QK = sb("QK", [P, NT, 2 * D], to=part)
            v1 = sb("v1", [P, NT, H, HW], to=part)
            fac = sb("fac", [P, NT, 2, H], to=part)
            with ExitStack() as inner:
                HT = sb("HT_g1", [P, HALF, NP], to=inner)
                wqkv, bqkv = sb("wqkv", [P, HALF, 3 * D], to=inner), sb("bqkv", [1, 3 * D], to=inner)
                temp, valid = sb("temp", [P, H], to=inner), sb("valid", [P, NT], to=inner)
                norm(nc, "norm3", X, XN, HT, g["ident"],
                     ahead=[(wqkv[:, :, :], halves("wqkv")), (bqkv[:, :], io["bqkv"]),
                            (temp[:, :], io["temp"].partition_broadcast(P)), (valid[:, :], io["valid"])])
                taylor_project(nc, g, (wqkv, bqkv, temp, valid), HT, QK, v1, fac)
                with ExitStack() as deep:
                    gnn_table(nc, io, g, 1, HT, table1, dtable1)
            kv2, kv1, kv0 = (sb("kv2", [P, H * PAIRS, HW], to=part), sb("kv1", [P, H, HW], to=part),
                             sb("kv0", [1, MSG], to=part))
            taylor_keys(nc, g, QK, v1, fac, kv2, kv1, kv0)
            wp, bp = sb("wp", [P, HALF, D], to=part), sb("bp", [1, D], to=part)
            sel_i, sel_j = sb("sel_i", [P, PAIRS, P], to=part), sb("sel_j", [P, P], to=part)
            with Phase(nc, "tload") as ph:
                loaded = ph.sem("loaded")
                block = ph.open()
                load_ahead(block, loaded, [(wp[:, :, :], halves("wproj")), (bp[:, :], io["bproj"]),
                                           (sel_i[:, :, :], io["sel_i"]), (sel_j[:, :], io["sel_j"])])
            taylor_queries(nc, g, (wp, bp, sel_i, sel_j), QK, fac, kv2, kv1, kv0, X)
        edges(nc, io, g, 1, table1, dtable1, totals1, firsts1)
        combine(nc, io, g, 1, totals1, firsts1, X)
        if dbg is not None:
            dump(nc, X, dbg)

        with ExitStack() as part:
            HT = sb("HT_f1", [P, HALF, NP], to=part)
            gates = sb("gates1", [P, NT, R], to=part)
            wr, br = sb("wr1", [P, HALF, R], to=part), sb("br1", [1, R], to=part)
            ws = [sb(f"e3_w{n}", [P, R, HALF, D], to=part) for n in range(3)]
            cols = sb("e3_cols", [P, 2, 5, R * HALF], to=part)
            bo = sb("e3_bo", [1, R * D], to=part)
            norm(nc, "norm4", X, XN, HT, g["ident"],
                 ahead=[(wr[:, :, :], halves("wr1")), (br[:, :], io["br1"]), (cols[:, :, :, :], io["e3_cols"]), (bo[:, :], io["e3_bo"])]
                 + [(w[:, e, :, :], halves(f"e3_w{n}", e)) for n, w in enumerate(ws) for e in range(R)])
            route(nc, g, HT, wr, br, gates, False, iota8)
            experts3(nc, g, X, HT, gates, ws, cols, bo)
        dump(nc, X, out)


def dump(nc, X, out):
    with Phase(nc, f"dump{out.name if 0 else nc.next_id()}") as ph:
        saved = ph.sem("saved")
        block = ph.open()

        @block.sync
        def _(sp):
            full = (NT - 1) * P
            sp.dma_start(out[0:full, :].rearrange("(t p) f -> p t f", p=P), X[:, 0:NT - 1, :]).then_inc(saved, 16)
            sp.dma_start(out[full:N, :], X[0:LAST, NT - 1, :]).then_inc(saved, 16)
            sp.wait_ge(saved, 32)


def kernel(**inputs):
    import concourse.bacc as _bacc
    from concourse.bass_utils import run_bass_kernel_spmd as _run

    nc = _bacc.Bacc("TRN2", target_bir_lowering=False, num_devices=1)
    arrays, io = {}, {}

    def give(name, a, dtype=None):
        a = np.ascontiguousarray(a)
        arrays["in_" + name] = a
        io[name] = nc.dram_tensor("in_" + name, a.shape, mybir.dt.from_np(a.dtype), kind="ExternalInput").ap()

    def pad(a, rows):
        return np.concatenate([a, np.zeros((rows - a.shape[0],) + a.shape[1:], a.dtype)])

    i = {k: np.asarray(v) for k, v in inputs.items()}
    give("x", pad(i["x"], NP))
    src, dst, typ = i["src"], i["dst"], i["edge_type_8"]
    tiles = dst.reshape(ET, EP)
    give("src_c", src.reshape(ET, EP).T)
    give("dst_c", tiles.T)
    give("type_c", typ.reshape(ET, EP).T)
    nxt = np.full((ET, EP), -1, dst.dtype)
    nxt[:, :-1] = tiles[:, 1:]
    give("next_c", nxt.T)
    give("first_c", np.broadcast_to(tiles[:, 0], (EP, ET)))
    give("dst_row", pad(dst, E + 2 * GE)[None, :])
    by_head = np.broadcast_to(tiles.reshape(NG, GT, 1, EP), (NG, GT, H, EP)).reshape(NG, GT * H, EP)
    give("dst_x", pad(by_head, NG + 2))
    attr = np.ones((4, E + 2 * GE), np.float32)
    attr[:3, :E] = i["edge_attr_3"].T
    attr[:3, E:] = 0
    give("attr", attr)
    give("enc_w", np.concatenate([i["L0_gnn_edge_W"].T, i["L0_gnn_edge_b"][None]]))
    lead = tiles[:, 0]
    before = np.concatenate([np.array([-1], dst.dtype), lead[:-1]])
    give("dst_f", lead.reshape(FT, FQ).T)
    give("prev_f", before.reshape(FT, FQ).T)
    give("dst_fx", np.broadcast_to(lead, (H, ET)))
    give("prev_fx", np.broadcast_to(before, (H, ET)))
    give("iota", np.arange(NP, dtype=np.float32)[None, :])
    give("ident", np.eye(P, dtype=np.float32))
    give("blocks", (np.arange(P)[:, None] // DH == np.arange(P) // DH).astype(np.float32))
    give("headmask", (np.arange(D).reshape(HALF, P).T[:, :, None] // DH == np.arange(H)).astype(np.float32))
    give("gnn_bias", i["L0_gnn_bias"][None, :])

    def columns(a, parts):
        return np.swapaxes(a.reshape(a.shape[:-1] + (parts, P)), -1, -2)

    lnp = np.stack([columns(i["L0_mix_" + n], HALF) for n in ("ln1_g", "ln1_b", "ln2_g", "ln2_b")], 2)
    give("mix_ln", lnp)
    for n in ("Wq", "Wk", "Wv", "Wo", "W1", "W2", "bo"):
        give(n.lower(), i["L0_mix_" + n])
    give("mix_b1", columns(i["L0_mix_b1"], FC))
    give("mix_b2", i["L0_mix_b2"])

    give("head4", (np.arange(P)[:, None] // DH == np.arange(H) % (P // DH)).astype(np.float32))
    give("wr0", i["L0_ffn_Wr"])
    give("br0", i["L0_ffn_br"][None])
    give("wr1", i["L1_ffn_Wr"])
    give("br1", i["L1_ffn_br"][None])
    give("moe_w1", i["L0_ffn_W1"])
    give("moe_w2", i["L0_ffn_W2"])
    give("moe_b1", columns(i["L0_ffn_b1"], FC))
    give("moe_b2", i["L0_ffn_b2"][:, None])
    give("moe_g", columns(i["L0_ffn_ln_g"], HALF))
    give("moe_b", columns(i["L0_ffn_ln_b"], HALF))
    give("wqkv", i["L1_mix_Wqkv"].T)
    give("bqkv", i["L1_mix_bqkv"][None])
    give("temp", i["L1_mix_temperature"].reshape(1, H))
    give("valid", (np.arange(NP).reshape(NT, P).T < N).astype(np.float32))
    give("wproj", i["L1_mix_Wproj"].T)
    give("bproj", i["L1_mix_bproj"][None])
    row = np.arange(P)
    d = np.arange(P)[:, None] % DH
    give("sel_j", (d == row % DH).astype(np.float32))
    give("sel_i", (d[:, :, None] == (np.arange(PAIRS)[:, None] * (P // DH) + row // DH)[None]).astype(np.float32))
    for n, name in enumerate(("W1", "W2", "Wo")):
        give(f"e3_w{n}", i["L1_ffn_" + name])
    cols = np.stack([np.stack([i[f"L1_ffn_{n}{layer}"] for n in ("b", "g", "be", "m", "v")]) for layer in (1, 2)])
    give("e3_cols", cols.reshape(2, 5, R, HALF, P).transpose(4, 0, 1, 2, 3).reshape(P, 2, 5, R * HALF))
    give("e3_bo", i["L1_ffn_bo"].reshape(1, R * D))

    def with_scores(w):
        w = w.reshape(-1, H, DH, D).transpose(0, 3, 1, 2)
        full = np.zeros((w.shape[0], D, ROW), np.float32)
        full[:, :, :MSG].reshape(w.shape[0], D, H, HW)[:, :, :, :DH] = w
        return full

    for layer, w, names in ((0, i["L0_gnn_W"][None], ("L0_gnn_a_src", "L0_gnn_a_dst")),
                            (1, i["L1_gnn_W"], ("L1_gnn_attn_src", "L1_gnn_attn_dst"))):
        give(f"gnn_w{layer}", w)
        give(f"gnn_wt{layer}", with_scores(w))
        give(f"a{layer}", np.stack([i[n].reshape(HALF, P).T for n in names], 1))

    out = nc.dram_tensor("out_0", (N, D), F32, kind="ExternalOutput").ap()
    dbg = nc.dram_tensor("dbg", (N, D), F32, kind="ExternalOutput").ap() if DEBUG else None
    build(nc, io, out, dbg=dbg)
    r = _run(nc, [arrays], core_ids=[0])
    return r.results[0]["out_0"]


DEBUG = False
```

```python
from contextlib import ExitStack

import numpy as np

import concourse.bass as bass
from concourse import mybir

F32 = mybir.dt.float32
I32 = mybir.dt.int32
U32 = mybir.dt.uint32
BF16 = mybir.dt.bfloat16
ALU = mybir.AluOpType
ACT = mybir.ActivationFunctionType
X_AXIS = mybir.AxisListType.X

P = 128
N, D = 3125, 256
NT = -(-N // P)
NP = NT * P
LAST = N - (NT - 1) * P
U = 5
NB = NT // U
CH = U * P // 2
H, DH = 8, 32
HALF = D // P

E = 50000
EP = 125
ET = E // EP
GT = 8
NG = ET // GT
GE = GT * EP
HW = DH + 1
MSG = H * HW
ROW = MSG + H
SKIP = 4000
BIG = 1e30
NEG_SLOPE = 0.2
FT = 4
FQ = ET // FT
R = 8
SLOTS = U


class Phase:

    def __init__(self, nc, name):
        self.nc, self.name, self.sems, self.ctx = nc, name, [], ExitStack()

    def sb(self, name, shape, dtype=F32):
        return self.ctx.enter_context(self.nc.sbuf_tensor(f"{self.name}_{name}", shape, dtype))

    def ps(self, name, shape):
        return self.ctx.enter_context(self.nc.psum_tensor(f"{self.name}_ps_{name}", shape, F32))

    def sem(self, name):
        self.sems.append(self.ctx.enter_context(self.nc.semaphore(f"{self.name}_{name}")))
        return self.sems[-1]

    def open(self):
        self.inner = ExitStack()
        return self.inner.enter_context(self.nc.Block())

    def __enter__(self):
        return self

    def __exit__(self, *error):
        if error[0] is None:
            self.inner.close()
            for s in self.sems:
                self.nc.sync.sem_clear(s)
            self.nc.all_engine_barrier()
            self.ctx.close()


def gate(eng, sem, value, passed):
    eng.wait_ge(sem, value)
    eng.sem_inc(passed, 1)


def load_ahead(block, loaded, ahead):
    if ahead:
        @block.sync
        def _(sp):
            for out, in_ in ahead:
                sp.dma_start(out, in_).then_inc(loaded, 16)
            sp.wait_ge(loaded, 16 * len(ahead))


def gather_ahead(ph, block, g, job, loaded, ahead):
    layer, n0, count, used, tables, rows = job
    tiles = count * GT
    at = ph.sb("gather_at", [EP, 2, tiles], I32)
    got_rows = [[ph.sb(f"gathered{side}{b}", [EP, GT, tables[side].shape[1]]) for b in range(2)] for side in range(2)]
    s_at, s_passed = ph.sem("gather_at"), ph.sem("gather_passed")
    s_got = g[f"got{layer}"]
    s_saved = [[ph.sem(f"saved{side}{b}") for b in range(2)] for side in range(2)]

    @block.gpsimd
    def _(pool):
        for side, n in enumerate(("src", "dst")):
            pool.tensor_copy(at[:, side, :], g[f"{n}{layer}"][:, bass.ds(n0 * GT, tiles)]).then_inc(s_at, 1)
        gate(pool, s_at, 2, s_passed)
        for n in range(count):
            for side in range(2):
                if n >= 2:
                    gate(pool, s_saved[side][n % 2], 16 * (n // 2), s_passed)
                for c in range(GT):
                    pool.indirect_dma_start(got_rows[side][n % 2][:, c, :], None, tables[side],
                                            bass.IndirectOffsetOnAxis(ap=at[:, side, n * GT + c:n * GT + c + 1], axis=0)
                                            ).then_inc(s_got[side][n % 2], 16)

    @block.sync
    def _(sp):
        for out, in_ in ahead:
            sp.dma_start(out, in_).then_inc(loaded, 16)
        for n in range(count):
            for side in range(2):
                gate(sp, s_got[side][n % 2], (used[n % 2] + (n // 2 + 1)) * (16 * GT), s_passed)
                sp.dma_start(rows[side][bass.ds((n0 + n) * GE, GE), :].rearrange("(c e) w -> e c w", e=EP),
                             got_rows[side][n % 2][:, :, :]).then_inc(s_saved[side][n % 2], 16)
        for side in range(2):
            for b in range(2):
                sp.wait_ge(s_saved[side][b], 16 * ((count + 1 - b) // 2))
        if ahead:
            sp.wait_ge(loaded, 16 * len(ahead))


def load_x(nc, io, X):
    with Phase(nc, "load") as ph:
        loaded = ph.sem("loaded")
        block = ph.open()

        @block.sync
        def _(sp):
            sp.dma_start(X[:, :, :], io["x"].rearrange("(t p) f -> p t f", p=P)).then_inc(loaded, 16)
            sp.wait_ge(loaded, 16)


def norm(nc, name, src, rows, turned, ident, gain=None, bias=None, ahead=()):
    with Phase(nc, name) as ph:
        stats = ph.sb("stats", [P, NT, 6])
        mv = ph.sb("mv", [P, NT, 2])
        var_eps = ph.sb("var_eps", [P, NT])
        std = ph.sb("std", [P, NT])
        rstd = ph.sb("rstd", [P, NT])
        pt = ph.ps("pt", [P, SLOTS, 512])
        s_stats, s_mv, s_var = ph.sem("stats"), ph.sem("mv"), ph.sem("var")
        s_std, s_rstd, s_rows = ph.sem("std"), ph.sem("rstd"), ph.sem("rows")
        s_turned, s_free, s_ahead = ph.sem("turned"), ph.sem("free"), ph.sem("ahead")
        block = ph.open()
        load_ahead(block, s_ahead, ahead)

        @block.vector
        def _(v):
            with v.Fori(0, NT) as t:
                v.bn_stats(stats[:, t, :], src[:, t, :]).then_inc(s_stats, 1)
            v.wait_ge(s_stats, NT)
            for t in range(NT):
                v.bn_aggr(mv[:, t, :], stats[:, t, :]).then_inc(s_mv, 1)
            v.wait_ge(s_mv, NT)
            v.tensor_scalar(var_eps[:, :], mv[:, :, 1], 1e-5, None, ALU.add).then_inc(s_var, 1)
            v.wait_ge(s_std, 1)
            v.reciprocal(rstd[:, :], std[:, :]).then_inc(s_rstd, 1)
            v.wait_ge(s_rstd, 1)
            with v.Fori(0, NT) as t:
                v.tensor_scalar(rows[:, t, :], src[:, t, :], mv[:, t, 0:1], rstd[:, bass.ds(t, 1)],
                                ALU.subtract, ALU.mult).then_inc(s_rows, 1)

        @block.tensor
        def _(pe):
            for t in range(NT):
                pe.wait_ge(s_rows, t + 1)
                pe.wait_ge(s_free, t + 1)
                for a in range(HALF):
                    mm = pe.transpose(pt[:, t % SLOTS, a * P:(a + 1) * P], rows[:, t, a * P:(a + 1) * P], ident[:, :])
                mm.then_inc(s_turned, 1)

        @block.scalar
        def _(act):
            act.sem_inc(s_free, SLOTS)
            act.wait_ge(s_var, 1)
            act.activation(std[:, :], var_eps[:, :], ACT.Sqrt).then_inc(s_std, 1)
            with act.Fori(0, NB) as k:
                for j in range(U):
                    act.wait_ge(s_turned, k * U + j + 1)
                    at = bass.ds(k * (U * P) + j * P, P)
                    if gain is None:
                        last = act.activation(turned[:, :, at], pt[:, j, 0:D].rearrange("p (a n) -> p a n", a=HALF), ACT.Copy)
                    else:
                        for a in range(HALF):
                            last = act.activation(turned[:, a, at], pt[:, j, a * P:(a + 1) * P], ACT.Identity,
                                                  bias=bias[:, a:a + 1], scale=gain[:, a:a + 1])
                    last.then_inc(s_free, 1)


def edge_prep(nc, io, g, more):
    with Phase(nc, "prep") as ph:
        srcc = ph.sb("src", [EP, ET], I32)
        typec = ph.sb("type", [EP, ET], I32)
        nextc = ph.sb("next", [EP, ET], I32)
        firstc = ph.sb("first", [EP, ET], I32)
        base = ph.sb("base", [EP, ET])
        ends = ph.sb("ends", [EP, ET])
        inner = ph.sb("inner", [EP, ET])
        s_in, s_v = ph.sem("in"), ph.sem("v")
        block = ph.open()
        loads = [(g["dst"][:, :], io["dst_c"]), (srcc[:, :], io["src_c"]), (typec[:, :], io["type_c"]),
                 (nextc[:, :], io["next_c"]), (firstc[:, :], io["first_c"]), (g["ident"][:, :], io["ident"]),
                 (g["blocks"][:, :], io["blocks"])] + more

        @block.sync
        def _(sp):
            for out, in_ in loads:
                sp.dma_start(out, in_).then_inc(s_in, 16)

        @block.vector
        def _(v):
            v.wait_ge(s_in, 16 * len(loads))
            for n in ("src0", "dst0", "src1", "dst1", "put"):
                v.memset(g[n][:, :], 0).then_inc(s_v, 1)
            v.tensor_scalar(base[:, :], typec[:, :], float(NP), None, ALU.mult).then_inc(s_v, 1)
            v.tensor_tensor(ends[:, :], g["dst"][:, :], nextc[:, :], ALU.not_equal).then_inc(s_v, 1)
            v.tensor_tensor(inner[:, :], g["dst"][:, :], firstc[:, :], ALU.not_equal).then_inc(s_v, 1)
            v.wait_ge(s_v, 8)
            v.tensor_copy(g["src0"][:, 0:ET], srcc[:, :]).then_inc(s_v, 1)
            v.tensor_copy(g["dst0"][:, 0:ET], g["dst"][:, :]).then_inc(s_v, 1)
            v.tensor_tensor(g["src1"][:, 0:ET], base[:, :], srcc[:, :], ALU.add).then_inc(s_v, 1)
            v.tensor_tensor(g["dst1"][:, 0:ET], base[:, :], g["dst"][:, :], ALU.add).then_inc(s_v, 1)
            v.tensor_tensor(ends[:, :], ends[:, :], inner[:, :], ALU.mult).then_inc(s_v, 1)
            v.wait_ge(s_v, 13)
            v.scalar_tensor_tensor(inner[:, :], g["dst"][:, :], -float(SKIP), ends[:, :],
                                   ALU.add, ALU.mult).then_inc(s_v, 1)
            v.wait_ge(s_v, 14)
            v.tensor_scalar(g["put"][:, 0:ET], inner[:, :], float(SKIP), None, ALU.add).then_inc(s_v, 1)


def gnn_table(nc, io, g, layer, turned, table, dtable):
    rel = R if layer else 1
    with Phase(nc, f"table{layer}") as ph:
        wo = ph.sb("wo", [P, 2, HALF, D])
        wt = ph.sb("wt", [P, 2, HALF, ROW])
        acol = ph.sb("acol", [P, 2, HALF])
        mask = ph.sb("mask", [P, HALF, H])
        ablk = ph.sb("ablk", [P, HALF, 2, H])
        rows = ph.sb("rows", [P, NB, U, ROW])
        pa = ph.ps("pa", [P, HALF, 512])
        ph_ = ph.ps("ph", [P, SLOTS, 512])
        s_w = [ph.sem(f"w{b}") for b in range(2)]
        s_c, s_ab, s_pa, s_wt = ph.sem("c"), ph.sem("ab"), ph.sem("pa"), ph.sem("wt")
        s_h, s_rows = ph.sem("h"), ph.sem("rows")
        s_saved = [ph.sem(f"saved{k}") for k in range(NB)]
        block = ph.open()
        per_store = 1 if dtable is None else 2

        def store(sp, r):
            for k in range(NB):
                sp.wait_ge(s_rows, SLOTS + r * NT + (k + 1) * U)
                at = slice(r * NP + k * U * P, r * NP + (k + 1) * U * P)
                sp.dma_start(table[at, :].rearrange("(t p) w -> p t w", p=P), rows[:, k, :, :]).then_inc(s_saved[k], 16)
                if dtable is not None:
                    sp.dma_start(dtable[at, :].rearrange("(t p) w -> p t w", p=P),
                                 rows[:, k, :, MSG:ROW]).then_inc(s_saved[k], 16)

        @block.sync
        def _(sp):
            sp.dma_start(acol[:, :, :], io[f"a{layer}"]).then_inc(s_c, 16)
            sp.dma_start(mask[:, :, :], io["headmask"]).then_inc(s_c, 16)
            for k in range(NB):
                sp.sem_inc(s_saved[k], 16 * per_store)
            for r in range(rel):
                if r >= 2:
                    sp.wait_ge(s_h, NT * (r - 1))
                sp.dma_start(wo[:, r % 2, :, :], io[f"gnn_w{layer}"][r].rearrange("(a p) i -> p a i", p=P)).then_inc(s_w[r % 2], 16)
                sp.dma_start(wt[:, r % 2, :, :], io[f"gnn_wt{layer}"][r].rearrange("(a p) o -> p a o", p=P)).then_inc(s_w[r % 2], 16)
                if r:
                    store(sp, r - 1)
            store(sp, rel - 1)
            for k in range(NB):
                sp.wait_ge(s_saved[k], 16 * per_store * (rel + 1))

        @block.vector
        def _(v):
            v.wait_ge(s_c, 32)
            for s in range(2):
                for a in range(HALF):
                    v.tensor_scalar(ablk[:, a, s, :], mask[:, a, :], acol[:, s, a:a + 1], None,
                                    ALU.mult).then_inc(s_ab, 1)
            for r in range(rel):
                v.wait_ge(s_w[r % 2], 32 * (r // 2 + 1))
                v.wait_ge(s_pa, r + 1)
                for a in range(HALF):
                    v.tensor_copy(wt[:, r % 2, a, 0:MSG].rearrange("p (h w) -> p h w", w=HW)[:, :, DH],
                                  pa[:, a, 0:H]).then_inc(s_wt, 1)
                    v.tensor_copy(wt[:, r % 2, a, MSG:ROW], pa[:, a, H:2 * H]).then_inc(s_wt, 1)

        @block.tensor
        def _(pe):
            pe.wait_ge(s_ab, 2 * HALF)
            for r in range(rel):
                pe.wait_ge(s_w[r % 2], 32 * (r // 2 + 1))
                if r:
                    pe.wait_ge(s_wt, 4 * r)
                for a in range(HALF):
                    for o in range(HALF):
                        mm = pe.matmul(pa[:, a, 0:2 * H], wo[:, r % 2, o, a * P:(a + 1) * P],
                                       ablk[:, o, :, :].rearrange("p s h -> p (s h)"),
                                       start=(o == 0), stop=(o == HALF - 1))
                mm.then_inc(s_pa, 1)
                pe.wait_ge(s_wt, 4 * (r + 1))
                for t in range(NT):
                    pe.wait_ge(s_rows, r * NT + t + 1)
                    for a in range(HALF):
                        mm = pe.matmul(ph_[:, t % SLOTS, 0:ROW], turned[:, a, t * P:(t + 1) * P],
                                       wt[:, r % 2, a, :], start=(a == 0), stop=(a == HALF - 1))
                    mm.then_inc(s_h, 1)

        @block.scalar
        def _(act):
            act.sem_inc(s_rows, SLOTS)
            with act.Fori(0, rel) as r:
                for k in range(NB):
                    act.wait_ge(s_saved[k], r * (16 * per_store) + 16 * per_store)
                    for j in range(U):
                        act.wait_ge(s_h, r * NT + (k * U + j + 1))
                        act.activation(rows[:, k, j, :], ph_[:, j, 0:ROW], ACT.Copy).then_inc(s_rows, 1)



SLOTS_O = 4


def edges(nc, io, g, layer, src_rows, dst_rows, totals, firsts):
    encoded = layer == 0
    dw = ROW if encoded else H
    with Phase(nc, f"edges{layer}") as ph:
        Gs = [ph.sb(f"rows_src{b}", [EP, GT, ROW]) for b in range(2)]
        Gd = [ph.sb(f"rows_dst{b}", [EP, GT, dw]) for b in range(2)]
        O = [ph.sb(f"out{b}", [EP, GT, ROW]) for b in range(2)]
        same = [ph.sb(f"same{b}", [EP, GT, EP]) for b in range(2)]
        dstb = [ph.sb(f"dstb{b}", [EP, GT, EP], I32) for b in range(2)]
        dstx = [ph.sb(f"dstx{b}", [GT * H, EP], I32) for b in range(2)]
        slot_o = [ph.sb(f"slot_o{b}", [EP, GT], I32) for b in range(2)]
        blank = ph.sb("blank", [P, ROW])
        pen = ph.sb("pen", [GT * H, EP + 1])
        fwd = ph.sb("fwd", [GT * H, EP])
        bwd = ph.sb("bwd", [GT * H, EP])
        top = ph.sb("top", [GT * H, EP])
        alpha = ph.sb("alpha", [EP, GT, H])
        alpha0 = ph.sb("alpha0", [EP, GT, H])
        below = ph.sb("below", [EP, GT, H])
        p_t = ph.ps("p_t", [P, 512])
        p_m = ph.ps("p_m", [P, 512])
        p_o = ph.ps("p_o", [P, SLOTS_O, 512])
        if encoded:
            attr = [ph.sb(f"attr{b}", [4, GE]) for b in range(2)]
            enc_w = ph.sb("enc_w", [4, D])
            enc = ph.sb("enc", [EP, 2, 2, D])
            dot = ph.sb("dot", [EP, GT, H])
            p_e = ph.ps("p_e", [P, 2, 2, D])
        s_blank, s_clear, s_w = ph.sem("blank"), ph.sem("clear"), ph.sem("w")
        s_chunk = [ph.sem(f"chunk{b}") for b in range(2)]
        s_used = [ph.sem(f"used{b}") for b in range(2)]
        s_rows = [ph.sem(f"rows{b}") for b in range(2)]
        s_put = [ph.sem(f"put{b}") for b in range(2)]
        s_scattered = g[f"scattered{layer}"]
        s_ofree = [ph.sem(f"ofree{b}") for b in range(2)]
        s_firsts = [ph.sem(f"firsts{b}") for b in range(2)]
        s_passed, s_pe, s_penc = ph.sem("passed"), ph.sem("pe"), ph.sem("penc")
        s_enc, s_prod, s_encfree, s_pencfree = ph.sem("enc"), ph.sem("prod"), ph.sem("encfree"), ph.sem("pencfree")
        s_chain, s_alpha, s_aT, s_top, s_mT = ph.sem("chain"), ph.sem("alpha"), ph.sem("aT"), ph.sem("top"), ph.sem("mT")
        s_below, s_exp, s_msg, s_same = ph.sem("below"), ph.sem("exp"), ph.sem("msg"), ph.sem("same")
        s_scan = ph.sem("scan")
        s_sum, s_out, s_pen, s_mcopy = ph.sem("sum"), ph.sem("out"), ph.sem("pen"), ph.sem("mcopy")
        block = ph.open()

        def weight(b):
            return Gs[b][:, :, 0:MSG].rearrange("p c (h w) -> p c h w", w=HW)[:, :, :, DH]

        loads = 3 if encoded else 2

        def load_chunk(sp, n, b):
            sp.dma_start(dstb[b][:, :, :].rearrange("p c e -> p (c e)"),
                         io["dst_row"][:, bass.ds(n * GE, GE)].partition_broadcast(EP)).then_inc(s_chunk[b], 16)
            sp.dma_start(dstx[b][:, :], io["dst_x"][n]).then_inc(s_chunk[b], 16)
            if encoded:
                sp.dma_start(attr[b][:, :], io["attr"][:, bass.ds(n * GE, GE)]).then_inc(s_chunk[b], 16)

        def load_rows(sp, n, b):
            for to, rows in ((Gs[b], src_rows), (Gd[b], dst_rows)):
                sp.dma_start(to[:, :, :], rows[bass.ds(n * GE, GE), :].rearrange("(c e) w -> e c w", e=EP)).then_inc(s_rows[b], 16)

        @block.sync
        def _(sp):
            if encoded:
                sp.dma_start(enc_w[:, :], io["enc_w"]).then_inc(s_w, 16)
            for b in range(2):
                sp.sem_inc(s_ofree[b], 1)
                load_chunk(sp, b, b)
                load_rows(sp, b, b)
            sp.wait_ge(s_blank, 2)
            sp.dma_start(totals.rearrange("(t p) w -> p t w", p=P),
                         blank[:, None, :].to_broadcast([P, NT, ROW])).then_inc(s_clear, 16)
            with sp.Fori(0, NG // 2) as k:
                for b in range(2):
                    n = k * 2 + b
                    gate(sp, s_out, n * GT + (SLOTS_O + GT), s_passed)
                    gate(sp, s_mcopy, n + 2, s_passed)
                    sp.dma_start(firsts[bass.ds(n * GT, GT), :].rearrange("(a t) w -> a t w", a=1),
                                 O[b][0:1, :, :]).then_inc(s_firsts[b], 16)
                    load_rows(sp, n + 2, b)
                    gate(sp, s_used[b], 2 * (k + 1), s_passed)
                    if encoded:
                        gate(sp, s_enc, n * (GT // 2) + (2 + GT // 2), s_passed)
                    load_chunk(sp, n + 2, b)
                    gate(sp, s_scattered[b], 16 * GT * (k + 1), s_passed)
                    gate(sp, s_firsts[b], 16 * (k + 1), s_passed)
                    sp.sem_inc(s_ofree[b], 1)
            for b in range(2):
                sp.wait_ge(s_chunk[b], 16 * loads * (NG // 2 + 1))
                sp.wait_ge(s_rows[b], 32 * (NG // 2 + 1))

        @block.gpsimd
        def _(pool):
            pool.memset(blank[:, 0:MSG], 0.0).then_inc(s_blank, 1)
            pool.memset(blank[:, MSG:ROW], -BIG).then_inc(s_blank, 1)

            def scatter(k, b):
                gate(pool, s_put[b], k + 1, s_passed)
                gate(pool, s_out, k * (2 * GT) + (SLOTS_O + GT * (b + 1)), s_passed)
                gate(pool, s_mcopy, 2 * k + (b + 2), s_passed)
                for c in range(GT):
                    pool.indirect_dma_start(totals, bass.IndirectOffsetOnAxis(ap=slot_o[b][:, c:c + 1], axis=0),
                                            O[b][:, c, :], None, bounds_check=NP - 1,
                                            oob_is_err=False).then_inc(s_scattered[b], 16)

            pool.wait_ge(s_clear, 16)
            with pool.Fori(0, NG // 2) as k:
                scatter(k, 0)
                scatter(k, 1)

        @block.tensor
        def _(pe):
            pe.sem_inc(s_sum, 2 * GT)
            if encoded:
                pe.wait_ge(s_w, 16)
            with pe.Fori(0, NG // 2) as k:
                for b in range(2):
                    n = k * 2 + b
                    if encoded:
                        pe.wait_ge(s_chunk[b], 16 * loads * (k + 1))
                        for q in range(GT // 2):
                            pe.wait_ge(s_enc, n * (GT // 2) + (q + 1))
                            for c in range(2):
                                mm = pe.matmul(p_e[0:EP, q % 2, c, :], attr[b][:, (2 * q + c) * EP:(2 * q + c + 1) * EP],
                                               enc_w[:, :], start=True, stop=True)
                            mm.then_inc(s_penc, 1)
                    gate(pe, s_alpha, n + 1, s_passed)
                    pe.transpose(p_t[0:GT * H, 0:EP], alpha[:, :, :].rearrange("p c h -> p (c h)"),
                                 g["ident"][0:EP, 0:EP]).then_inc(s_aT, 1)
                    gate(pe, s_top, n + 2, s_passed)
                    gate(pe, s_mcopy, n + 1, s_passed)
                    gate(pe, s_below, n + 1, s_passed)
                    pe.transpose(p_m[0:EP, 0:GT * H], top[:, :], g["ident"][0:GT * H, 0:GT * H]).then_inc(s_mT, 1)
                    pe.wait_ge(s_msg, n + 1)
                    for c in range(GT):
                        pe.wait_ge(s_out, n * GT + (c + 1))
                        pe.matmul(p_o[0:EP, c % SLOTS_O, 0:MSG], same[b][:, c, :], Gs[b][:, c, 0:MSG],
                                  start=True, stop=True).then_inc(s_sum, 1)

        @block.scalar
        def _(act):
            act.sem_inc(s_out, SLOTS_O)
            act.sem_inc(s_enc, 2)
            act.sem_inc(s_mcopy, 1)
            with act.Fori(0, NG // 2) as k:
                for b in range(2):
                    n = k * 2 + b
                    if encoded:
                        for q in range(GT // 2):
                            act.wait_ge(s_penc, n * (GT // 2) + (q + 1))
                            act.wait_ge(s_encfree, n * (GT // 2) + (q + 1))
                            act.activation(enc[:, q % 2, :, :], p_e[0:EP, q % 2, :, :], ACT.Relu).then_inc(s_enc, 1)
                    act.wait_ge(s_ofree[b], k + 1)
                    act.wait_ge(s_below, n + 2)
                    act.activation(weight(b), below[:, :, :], ACT.Exp).then_inc(s_exp, 1)
                    act.activation(O[b][:, :, MSG:ROW], p_m[0:EP, 0:GT * H].rearrange("p (c h) -> p c h", h=H),
                                   ACT.Copy).then_inc(s_mcopy, 1)
                    for c in range(GT):
                        act.wait_ge(s_sum, n * GT + (2 * GT + c + 1))
                        act.activation(O[b][:, c, 0:MSG], p_o[0:EP, c % SLOTS_O, 0:MSG], ACT.Copy).then_inc(s_out, 1)

        @block.vector
        def _(v):
            v.memset(pen[:, :], 0.0).then_inc(s_pen, 1)
            v.sem_inc(s_top, 1)
            v.sem_inc(s_below, 1)
            if encoded:
                v.sem_inc(s_encfree, 2)
            v.wait_ge(s_pen, 1)
            with v.Fori(0, NG // 2) as k:
                for b in range(2):
                    n = k * 2 + b
                    v.wait_ge(s_chunk[b], 16 * loads * (k + 1))
                    v.wait_ge(s_top, n + 1)
                    v.tensor_tensor(pen[:, 1:EP], dstx[b][:, 1:EP], dstx[b][:, 0:EP - 1],
                                    ALU.not_equal).then_inc(s_used[b], 1)
                    v.wait_ge(s_sum, n * GT + GT)
                    v.tensor_tensor(same[b][:, :, :], dstb[b][:, :, :],
                                    g["dst"][:, bass.ds(n * GT, GT)][:, :, None].to_broadcast([EP, GT, EP]),
                                    ALU.is_equal).then_inc(s_used[b], 1)
                    v.wait_ge(s_used[b], 2 * (k + 1))
                    v.tensor_scalar(pen[:, 1:EP], pen[:, 1:EP], -BIG, None, ALU.mult).then_inc(s_pen, 1)
                    v.wait_ge(s_rows[b], 32 * (k + 1))
                    v.wait_ge(s_ofree[b], k + 1)
                    v.tensor_copy(slot_o[b][:, :], g["put"][:, bass.ds(n * GT, GT)]).then_inc(s_put[b], 1)
                    if encoded:
                        v.tensor_tensor(alpha0[:, :, :], weight(b), Gd[b][:, :, MSG:ROW], ALU.add).then_inc(s_chain, 1)
                        for q in range(GT // 2):
                            v.wait_ge(s_enc, n * (GT // 2) + (q + 3))
                            e4 = enc[:, q % 2, :, :].rearrange("p c (h w) -> p c h w", w=DH)
                            for c in range(2):
                                v.tensor_tensor(e4[:, c], e4[:, c],
                                                Gd[b][:, 2 * q + c, 0:MSG].rearrange("p (h w) -> p h w", w=HW)[:, :, 0:DH],
                                                ALU.mult).then_inc(s_prod, 1)
                            v.wait_ge(s_prod, n * GT + (2 * q + 2))
                            v.tensor_reduce(dot[:, 2 * q:2 * q + 2, :], e4, X_AXIS, ALU.add).then_inc(s_encfree, 1)
                        v.wait_ge(s_encfree, n * (GT // 2) + (GT // 2 + 2))
                        v.wait_ge(s_chain, n * 2 + 1)
                        v.tensor_tensor(alpha0[:, :, :], alpha0[:, :, :], dot[:, :, :], ALU.add).then_inc(s_chain, 1)
                        v.wait_ge(s_chain, n * 2 + 2)
                    else:
                        v.tensor_tensor(alpha0[:, :, :], weight(b), Gd[b][:, :, :], ALU.add).then_inc(s_chain, 1)
                        v.wait_ge(s_chain, n + 1)
                    v.wait_ge(s_below, n + 1)
                    v.scalar_tensor_tensor(alpha[:, :, :], alpha0[:, :, :], NEG_SLOPE, alpha0[:, :, :],
                                           ALU.mult, ALU.max).then_inc(s_alpha, 1)
                    v.wait_ge(s_aT, n + 1)
                    v.wait_ge(s_pen, n + 2)
                    v.tensor_tensor_scan(fwd[:, :], pen[:, 0:EP], p_t[0:GT * H, 0:EP], -BIG,
                                         ALU.add, ALU.max).then_inc(s_scan, 1)
                    v.tensor_tensor_scan(bwd[:, ::-1], pen[:, 1:EP + 1][:, ::-1], p_t[0:GT * H, 0:EP][:, ::-1], -BIG,
                                         ALU.add, ALU.max).then_inc(s_scan, 1)
                    v.wait_ge(s_scan, n * 2 + 2)
                    v.tensor_tensor(top[:, :], fwd[:, :], bwd[:, :], ALU.max).then_inc(s_top, 1)
                    v.wait_ge(s_mT, n + 1)
                    v.tensor_tensor(below[:, :, :], alpha[:, :, :], p_m[0:EP, 0:GT * H].rearrange("p (c h) -> p c h", h=H),
                                    ALU.subtract).then_inc(s_below, 1)
                    v.wait_ge(s_exp, n + 1)
                    for c in range(GT):
                        hc = Gs[b][:, c, 0:MSG].rearrange("p (h w) -> p h w", w=HW)
                        last = v.tensor_tensor(hc[:, :, 0:DH], hc[:, :, 0:DH],
                                               hc[:, :, DH:HW].to_broadcast([EP, H, DH]), ALU.mult)
                    last.then_inc(s_msg, 1)


def combine(nc, io, g, layer, totals, firsts, X):
    with Phase(nc, f"combine{layer}") as ph:
        fs = ph.sb("fs", [FQ, FT, ROW + 1])
        dstf = ph.sb("dstf", [FQ, FT])
        dstf_i, prev_i = ph.sb("dstf_i", [FQ, FT], I32), ph.sb("prev_i", [FQ, FT], I32)
        dstx_i, prevx_i = ph.sb("dstx_i", [H, ET], I32), ph.sb("prevx_i", [H, ET], I32)
        isfirst = ph.sb("isfirst", [FQ, FT])
        penf = ph.sb("penf", [H, ET + 1])
        iota = ph.sb("iota", [FQ, NP])
        ones = ph.sb("ones", [FQ, FT])
        fwd, bwd, top = ph.sb("fwd", [H, ET]), ph.sb("bwd", [H, ET]), ph.sb("top", [H, ET])
        scale = ph.sb("scale", [FQ, FT, H])
        tab = ph.sb("tab", [P, NT, ROW])
        hot = ph.sb("hot", [FQ, 2, FT, P])
        far = ph.sb("far", [P, 1])
        m1, m = ph.sb("m1", [P, H]), ph.sb("m", [P, H])
        ex = ph.sb("ex", [P, 3, H])
        low = ph.sb("low", [P, H])
        part = ph.sb("part", [P, H, HW])
        den, rden = ph.sb("den", [P, H]), ph.sb("rden", [P, H])
        biasrow = ph.sb("biasrow", [P, D])
        p_t = ph.ps("p_t", [P, 512])
        p_m = ph.ps("p_m", [P, 512])
        p_n = ph.ps("p_n", [P, 2, 512])
        s_in, s_mT, s_f, s_scan, s_top, s_back = (ph.sem(x) for x in ("in", "mT", "f", "scan", "top", "back"))
        s_scale, s_exp, s_fs, s_hot, s_sum, s_chain, s_e, s_used = (
            ph.sem(x) for x in ("scale", "exp", "fs", "hot", "sum", "chain", "e", "used"))
        block = ph.open()
        loads = [(fs[:, :, 0:ROW], firsts.rearrange("(b q) w -> q b w", q=FQ)), (dstf_i[:, :], io["dst_f"]),
                 (prev_i[:, :], io["prev_f"]), (dstx_i[:, :], io["dst_fx"]), (prevx_i[:, :], io["prev_fx"]),
                 (iota[:, :], io["iota"].partition_broadcast(FQ)),
                 (tab[:, :, :], totals.rearrange("(t p) w -> p t w", p=P)),
                 (biasrow[:, :], io["gnn_bias"].partition_broadcast(P))]

        @block.sync
        def _(sp):
            for out, in_ in loads:
                sp.dma_start(out, in_).then_inc(s_in, 16)

        @block.tensor
        def _(pe):
            pe.wait_ge(s_in, 16 * len(loads))
            for b in range(FT):
                mm = pe.transpose(p_t[0:H, b * FQ:(b + 1) * FQ], fs[:, b, MSG:ROW], g["ident"][0:FQ, 0:FQ])
            mm.then_inc(s_mT, 1)
            pe.wait_ge(s_top, 1)
            for b in range(FT):
                mm = pe.transpose(p_m[0:FQ, b * H:(b + 1) * H], top[:, b * FQ:(b + 1) * FQ], g["ident"][0:H, 0:H])
            mm.then_inc(s_back, 1)
            pe.wait_ge(s_fs, 3)
            for t in range(NT):
                pe.wait_ge(s_hot, t + 1)
                if t >= 2:
                    pe.wait_ge(s_used, t - 1)
                for b in range(FT):
                    mm = pe.matmul(p_n[:, t % 2, 0:ROW + 1], hot[:, t % 2, b, :], fs[:, b, :],
                                   start=(b == 0), stop=(b == FT - 1))
                mm.then_inc(s_sum, 1)

        @block.scalar
        def _(act):
            act.wait_ge(s_scale, 1)
            act.activation(scale[:, :, :], scale[:, :, :], ACT.Exp).then_inc(s_exp, 1)
            for t in range(NT):
                act.wait_ge(s_e, t + 1)
                act.activation(ex[:, :, :], ex[:, :, :], ACT.Exp).then_inc(s_exp, 1)

        @block.vector
        def _(v):
            steps = [0]

            def step(ins):
                steps[0] += 1
                ins.then_inc(s_chain, 1)
                v.wait_ge(s_chain, steps[0])

            v.wait_ge(s_in, 16 * len(loads))
            step(v.memset(ones[:, :], 1.0))
            step(v.tensor_copy(dstf[:, :], dstf_i[:, :]))
            step(v.tensor_tensor(penf[:, 0:ET], dstx_i[:, :], prevx_i[:, :], ALU.not_equal))
            step(v.tensor_scalar(penf[:, 0:ET], penf[:, 0:ET], -BIG, None, ALU.mult))
            step(v.memset(penf[:, ET:ET + 1], 0.0))
            step(v.tensor_tensor(isfirst[:, :], dstf_i[:, :], prev_i[:, :], ALU.not_equal))
            v.wait_ge(s_mT, 1)
            v.tensor_tensor_scan(fwd[:, :], penf[:, 0:ET], p_t[0:H, 0:ET], -BIG, ALU.add, ALU.max).then_inc(s_scan, 1)
            v.tensor_tensor_scan(bwd[:, ::-1], penf[:, 1:ET + 1][:, ::-1], p_t[0:H, 0:ET][:, ::-1], -BIG,
                                 ALU.add, ALU.max).then_inc(s_scan, 1)
            v.wait_ge(s_scan, 2)
            v.tensor_tensor(top[:, :], fwd[:, :], bwd[:, :], ALU.max).then_inc(s_top, 1)
            v.wait_ge(s_back, 1)
            mf = p_m[0:FQ, 0:FT * H].rearrange("p (b h) -> p b h", h=H)
            v.tensor_tensor(scale[:, :, :], fs[:, :, MSG:ROW], mf, ALU.subtract).then_inc(s_scale, 1)
            v.wait_ge(s_scale, 1)
            v.tensor_tensor(fs[:, :, MSG:ROW], isfirst[:, :, None].to_broadcast([FQ, FT, H]), mf,
                            ALU.mult).then_inc(s_fs, 1)
            v.tensor_tensor(fs[:, :, ROW], isfirst[:, :], ones[:, :], ALU.mult).then_inc(s_fs, 1)
            v.wait_ge(s_exp, 1)
            for b in range(FT):
                f = fs[:, b, 0:MSG].rearrange("p (h w) -> p h w", w=HW)
                step(v.tensor_tensor(f, f, scale[:, b, :, None].to_broadcast([FQ, H, HW]), ALU.mult))
            v.sem_inc(s_fs, 1)
            for t in range(NT):
                if t >= 2:
                    v.wait_ge(s_sum, t - 1)
                v.tensor_tensor(hot[:, t % 2, :, :], iota[:, None, t * P:(t + 1) * P].to_broadcast([FQ, FT, P]),
                                dstf[:, :, None].to_broadcast([FQ, FT, P]), ALU.is_equal).then_inc(s_hot, 1)
                v.wait_ge(s_sum, t + 1)
                pn = p_n[:, t % 2, :]
                mt = tab[:, t, MSG:ROW]
                tb = tab[:, t, 0:MSG].rearrange("p (h w) -> p h w", w=HW)
                step(v.tensor_scalar(far[:, :], pn[:, ROW:ROW + 1], BIG, -BIG, ALU.mult, ALU.add))
                step(v.tensor_scalar(m1[:, :], pn[:, MSG:ROW], far[:, 0:1], None, ALU.add))
                step(v.tensor_tensor(m[:, :], m1[:, :], mt, ALU.max))
                step(v.tensor_tensor(ex[:, 0, :], mt, m[:, :], ALU.subtract))
                step(v.tensor_tensor(ex[:, 1, :], m1[:, :], m[:, :], ALU.subtract))
                v.tensor_scalar(ex[:, 2, :], m[:, :], 0.0, None, ALU.min).then_inc(s_e, 1)
                v.wait_ge(s_exp, t + 2)
                step(v.tensor_tensor(part[:, :, :], pn[:, 0:MSG].rearrange("p (h w) -> p h w", w=HW),
                                     ex[:, 1, :, None].to_broadcast([P, H, HW]), ALU.mult))
                step(v.tensor_tensor(tb, tb, ex[:, 0, :, None].to_broadcast([P, H, HW]), ALU.mult))
                v.tensor_tensor(part[:, :, :], part[:, :, :], tb, ALU.add).then_inc(s_used, 1)
                v.wait_ge(s_used, t + 1)
                if layer == 0:
                    step(v.tensor_scalar(den[:, :], part[:, :, DH], 1e-10, None, ALU.max))
                    step(v.reciprocal(rden[:, :], den[:, :]))
                else:
                    step(v.tensor_tensor(den[:, :], part[:, :, DH], ex[:, 2, :], ALU.mult))
                    step(v.tensor_scalar(den[:, :], den[:, :], 1e-12, None, ALU.add))
                    step(v.reciprocal(rden[:, :], den[:, :]))
                    step(v.tensor_tensor(rden[:, :], rden[:, :], ex[:, 2, :], ALU.mult))
                step(v.tensor_tensor(part[:, :, 0:DH], part[:, :, 0:DH], rden[:, :, None].to_broadcast([P, H, DH]),
                                     ALU.mult))
                xt = X[:, t, :].rearrange("p (h w) -> p h w", w=DH)
                step(v.tensor_tensor(xt, xt, part[:, :, 0:DH], ALU.add))
                if layer == 0:
                    step(v.tensor_tensor(X[:, t, :], X[:, t, :], biasrow[:, :], ALU.add))


DEPTH = 4
FF = 4 * D
FC = FF // P
KB = 10
KW = NP // KB
ATTN_GROUPS, FF_GROUPS = 6, 7


def halved(*counts):
    return [sum((n + 1 - b) // 2 for n in counts) for b in range(2)]


assert DEPTH * (ATTN_GROUPS + FF_GROUPS) == NG + 2
QK_SCALE = float(DH) ** -0.25
A_T, B_T = 2, 3
A_N, B_N = A_T * P, B_T * P


def attention(nc, g, w, S, turned, spare, ahead, job):
    wq, wk, wv, wo, bo = w
    qt = spare[:, :, :].rearrange("p t f -> p (t f)").rearrange("p (a n) -> p a n", a=HALF)
    with Phase(nc, "attn") as ph:
        kmx = ph.sb("kmx", [P, HALF, KB])
        kmax = ph.sb("kmax", [P, HALF])
        krow = ph.sb("krow", [1, D])
        ones = ph.sb("ones", [P, P])
        qmax, qsum, qrec = ph.sb("qmax", [P, 2, H]), ph.sb("qsum", [P, 2, H]), ph.sb("qrec", [P, 2, H])
        qs = ph.sb("qs", [P, 2, H, DH])
        ek = ph.sb("ek", [P, 2, D])
        vs = ph.sb("vs", [P, 2, D])
        ctx = ph.sb("ctx", [P, HALF, P])
        rk = ph.sb("rk", [P, HALF])
        M = ph.sb("M", [P, HALF, D])
        p_q = ph.ps("q", [P, 2, 512])
        p_kv = ph.ps("kv", [P, 2, 512])
        p_t = ph.ps("t", [P, 2, 512])
        p_c = ph.ps("c", [P, 512])
        p_s = ph.ps("s", [P, 512])
        names = ("ahead ones kT kmx kmax kTurned krow q kv v_done qmax qs qexp qsum qrec qn qt qt_out "
                 "ek vs ctx ctxm rk m mo o added")
        s = {n: ph.sem(n) for n in names.split()}
        block = ph.open()
        gather_ahead(ph, block, g, job, s["ahead"], ahead)

        def rows(t):
            return P if t < NT - 1 else LAST

        @block.tensor
        def _(pe):
            for c in range(KB):
                if c >= 2:
                    pe.wait_ge(s["kmx"], 2 * (c - 1))
                for a in range(HALF):
                    for i in range(HALF):
                        mm = pe.matmul((p_q, p_kv)[a][:, c % 2, 0:KW], wk[:, i, a * P:(a + 1) * P],
                                       turned[:, i, c * KW:(c + 1) * KW], start=(i == 0), stop=(i == HALF - 1))
                    mm.then_inc(s["kT"], 1)
            pe.wait_ge(s["kmax"], 1)
            for a in range(HALF):
                mm = pe.transpose(p_s[0:1, a * P:(a + 1) * P], kmax[:, a:a + 1], g["ident"][:, :])
            mm.then_inc(s["kTurned"], 1)
            pe.wait_ge(s["krow"], 1)
            pe.wait_ge(s["ones"], 1)

            def project(t):
                b = t % 2
                if t >= 2:
                    pe.wait_ge(s["qs"], t - 1)
                    pe.wait_ge(s["vs"], t - 1)
                at = slice(t * P, (t + 1) * P)
                for i in range(HALF):
                    mm = pe.matmul(p_q[:, b, 0:D], turned[:, i, at], wq[:, i, :], start=(i == 0), stop=(i == HALF - 1))
                mm.then_inc(s["q"], 1)
                for i in range(HALF):
                    pe.matmul(p_kv[:, b, 0:D], turned[:, i, at], wk[:, i, :], start=(i == 0), stop=False)
                pe.matmul(p_kv[:, b, 0:D], ones[0:1, :], krow[:, :], start=False, stop=True)
                for i in range(HALF):
                    mm = pe.matmul(p_kv[:, b, D:2 * D], turned[:, i, at], wv[:, i, :], start=(i == 0), stop=(i == HALF - 1))
                mm.then_inc(s["kv"], 1)

            def contract(t):
                b, r = t % 2, rows(t)
                pe.wait_ge(s["vs"], t + 1)
                for a in range(HALF):
                    pe.matmul(p_c[:, a * P:(a + 1) * P], vs[0:r, b, a * P:(a + 1) * P], ek[0:r, b, a * P:(a + 1) * P],
                              start=(t == 0 and a == 0), stop=(t == NT - 1), skip_group_check=True)
                for a in range(HALF):
                    mm = pe.matmul(p_c[:, D + a:D + a + 1], ek[0:r, b, a * P:(a + 1) * P], ones[0:r, 0:1],
                                   start=False, stop=(t == NT - 1), skip_group_check=True)
                mm.then_inc(s["ctx"], 1)
                pe.wait_ge(s["qn"], t + 1)
                if t >= 2:
                    pe.wait_ge(s["qt_out"], t - 1)
                for a in range(HALF):
                    mm = pe.transpose(p_t[:, b, a * P:(a + 1) * P],
                                      qs[:, b, :, :].rearrange("p h w -> p (h w)")[:, a * P:(a + 1) * P], g["ident"][:, :])
                mm.then_inc(s["qt"], 1)

            for t in range(NT):
                project(t)
                if t:
                    contract(t - 1)
            contract(NT - 1)
            pe.wait_ge(s["ctxm"], 2)
            for a in range(HALF):
                mm = pe.matmul(p_s[:, a * D:(a + 1) * D], ctx[:, a, :], wo[:, a, :], start=True, stop=True)
            mm.then_inc(s["m"], 1)
            pe.wait_ge(s["mo"], 2)
            pe.wait_ge(s["qt_out"], NT)
            for t in range(NT):
                if t >= 2:
                    pe.wait_ge(s["added"], t - 1)
                for a in range(HALF):
                    pe.matmul(p_q[:, t % 2, 0:D], qt[:, a, t * P:(t + 1) * P], M[:, a, :], start=(a == 0), stop=False)
                pe.matmul(p_q[:, t % 2, 0:D], ones[0:1, :], bo[:, :], start=False, stop=True).then_inc(s["o"], 1)

        @block.scalar
        def _(act):
            def keys(t):
                b = t % 2
                act.wait_ge(s["kv"], t + 1)
                if t >= 2:
                    act.wait_ge(s["ctx"], t - 1)
                act.activation(ek[:, b, :], p_kv[:, b, 0:D], ACT.Exp, scale=QK_SCALE).then_inc(s["ek"], 1)
                act.activation(vs[:, b, :], p_kv[:, b, D:2 * D], ACT.Copy).then_inc(s["vs"], 1)

            def turned_queries(t):
                act.wait_ge(s["qt"], t + 1)
                act.activation(qt[:, :, t * P:(t + 1) * P], p_t[:, t % 2, 0:D].rearrange("p (a n) -> p a n", a=HALF),
                               ACT.Copy).then_inc(s["qt_out"], 1)

            for t in range(NT):
                act.wait_ge(s["qs"], t + 1)
                act.activation(qs[:, t % 2, :, :], qs[:, t % 2, :, :], ACT.Exp, scale=QK_SCALE).then_inc(s["qexp"], 1)
                keys(t)
                if t:
                    turned_queries(t - 1)
            turned_queries(NT - 1)

        @block.vector
        def _(v):
            v.memset(ones[:, :], 1.0).then_inc(s["ones"], 1)
            for c in range(KB):
                w_ = min(KW, N - c * KW)
                for a in range(HALF):
                    v.wait_ge(s["kT"], HALF * c + a + 1)
                    v.tensor_reduce(kmx[:, a, c:c + 1], (p_q, p_kv)[a][:, c % 2, 0:w_], X_AXIS, ALU.max).then_inc(s["kmx"], 1)
            v.wait_ge(s["kmx"], HALF * KB)
            v.tensor_reduce(kmax[:, :], kmx[:, :, :], X_AXIS, ALU.max).then_inc(s["kmax"], 1)
            v.wait_ge(s["kTurned"], 1)
            v.tensor_scalar(krow[:, :], p_s[0:1, 0:D], -1.0, None, ALU.mult).then_inc(s["krow"], 1)

            def shift(t):
                b = t % 2
                v.wait_ge(s["q"], t + 1)
                q = p_q[:, b, 0:D].rearrange("p (h w) -> p h w", w=DH)
                v.tensor_reduce(qmax[:, b, :], q, X_AXIS, ALU.max).then_inc(s["qmax"], 1)
                v.wait_ge(s["qmax"], t + 1)
                if t >= 2:
                    v.wait_ge(s["qt"], t - 1)
                v.tensor_tensor(qs[:, b, :, :], q, qmax[:, b, :, None].to_broadcast([P, H, DH]),
                                ALU.subtract).then_inc(s["qs"], 1)

            def scale(t):
                b = t % 2
                v.wait_ge(s["qexp"], t + 1)
                v.tensor_reduce(qsum[:, b, :], qs[:, b, :, :], X_AXIS, ALU.add).then_inc(s["qsum"], 1)
                v.wait_ge(s["qsum"], t + 1)
                v.reciprocal(qrec[:, b, :], qsum[:, b, :]).then_inc(s["qrec"], 1)
                v.wait_ge(s["qrec"], t + 1)
                v.tensor_tensor(qs[:, b, :, :], qs[:, b, :, :], qrec[:, b, :, None].to_broadcast([P, H, DH]),
                                ALU.mult).then_inc(s["qn"], 1)

            for t in range(NT):
                shift(t)
                scale(t)
            v.wait_ge(s["ctx"], NT)
            v.reciprocal(rk[:, :], p_c[:, D:D + HALF]).then_inc(s["rk"], 1)
            for a in range(HALF):
                v.tensor_tensor(ctx[:, a, :], p_c[:, a * P:(a + 1) * P], g["blocks"][:, :], ALU.mult).then_inc(s["ctxm"], 1)
            v.wait_ge(s["m"], 1)
            v.wait_ge(s["rk"], 1)
            for a in range(HALF):
                v.tensor_scalar(M[:, a, :], p_s[:, a * D:(a + 1) * D], rk[:, a:a + 1], None, ALU.mult).then_inc(s["mo"], 1)
            for t in range(NT):
                v.wait_ge(s["o"], t + 1)
                v.tensor_tensor(S[:, t, :], S[:, t, :], p_q[:, t % 2, 0:D], ALU.add).then_inc(s["added"], 1)


def mlp(nc, g, name, S, turned, weights, ahead=(), experts=1, load=None, gates=None, job=None):
    with Phase(nc, name) as ph:
        hid = (ph.sb("hid_a", [P, FC, A_N]), ph.sb("hid_b", [P, FC, B_N]))
        ones = ph.sb("ones", [1, P])
        p_u = ph.ps("u", [P, 4, 512])
        p_d = ph.ps("d", [P, 3, 512])
        p_b = ph.ps("b", [P, 512])
        s_ahead, s_ones, s_up, s_hid, s_down, s_added, s_passed = (
            ph.sem(x) for x in ("ahead", "ones", "up", "hid", "down", "added", "passed"))
        s_w = [ph.sem(f"w{b}") for b in range(2)]
        s_folded, s_pb = ph.sem("folded"), ph.sem("pb")
        block = ph.open()
        if job is not None:
            gather_ahead(ph, block, g, job, s_ahead, ahead)
        width, first, tiles = (A_N, B_N), (0, A_N), (A_T, B_T)
        grouped = experts > 1
        UPS, DOWNS = NB * 2 * FC, NT

        def each(eng):
            if not grouped:
                yield 0, 0, 0, False
                return
            with eng.Fori(0, experts // 2 - 1) as pair:
                for b in range(2):
                    yield pair * 2 + b, b, pair, True
            for b in range(2):
                yield experts - 2 + b, b, experts // 2 - 1, b == 0

        n_loads = len(load(0, 0)) if grouped else 0

        def here(eng, b, pair):
            eng.wait_ge(s_w[b], pair * (16 * n_loads) + 16 * n_loads)

        if grouped:
            @block.sync
            def _(sp):
                def fetch(e, b):
                    for out, in_ in load(e, b):
                        sp.dma_start(out, in_).then_inc(s_w[b], 16)

                fetch(0, 0)
                fetch(1, 1)
                with sp.Fori(0, experts // 2 - 1) as pair:
                    for b in range(2):
                        gate(sp, s_down, (pair * 2 + b) * DOWNS + (U + DOWNS), s_passed)
                        fetch(pair * 2 + (b + 2), b)

        @block.tensor
        def _(pe):
            def up(e, b, k, part):
                for f in range(FC):
                    n = part * FC + f
                    pe.wait_ge(s_hid, e * UPS + k * (2 * FC) + (n + 1))
                    for i in range(HALF):
                        mm = pe.matmul(p_u[:, n % 4, 0:width[part]], weights[b]["w1"][:, i, f * P:(f + 1) * P],
                                       turned[:, i, bass.ds(k * (U * P) + first[part], width[part])],
                                       start=(i == 0), stop=(i == HALF - 1))
                    mm.then_inc(s_up, 1)

            def down(e, b, k, part):
                pe.wait_ge(s_hid, e * UPS + k * (2 * FC) + ((part + 1) * FC + 4))
                for j in range(tiles[part]):
                    n = part * A_T + j
                    pe.wait_ge(s_added, e * DOWNS + k * U + (n + 1))
                    for f in range(FC):
                        pe.matmul(p_d[:, n % 3, 0:D], hid[part][:, f, j * P:(j + 1) * P],
                                  weights[b]["w2"][:, f, :], start=(f == 0), stop=False)
                    pe.matmul(p_d[:, n % 3, 0:D], ones[:, :], weights[b]["b2"][:, :], start=False,
                              stop=True).then_inc(s_down, 1)

            def fold(b, pair):
                here(pe, b, pair)
                for f in range(FC):
                    for i in range(HALF):
                        mm = pe.matmul(p_b[:, f:f + 1], weights[b]["w1"][:, i, f * P:(f + 1) * P],
                                       weights[b]["ln_b"][:, i:i + 1], start=(i == 0), stop=(i == HALF - 1))
                mm.then_inc(s_pb, 1)

            pe.sem_inc(s_down, U)
            pe.wait_ge(s_ones, 1)
            if grouped:
                fold(0, 0)
            for e, b, pair, more in each(pe):
                if grouped:
                    pe.wait_ge(s_folded, (HALF + 1) * (e + 1))
                up(e, b, 0, 0)
                with pe.Fori(0, NB - 1) as k:
                    up(e, b, k, 1)
                    down(e, b, k, 0)
                    up(e, b, k + 1, 0)
                    down(e, b, k, 1)
                up(e, b, NB - 1, 1)
                down(e, b, NB - 1, 0)
                if more:
                    fold(1 - b, pair + b)
                down(e, b, NB - 1, 1)

        @block.scalar
        def _(act):
            act.sem_inc(s_hid, 4)
            for e, b, pair, more in each(act):
                if grouped:
                    act.wait_ge(s_folded, (HALF + 1) * (e + 1))
                with act.Fori(0, NB) as k:
                    for part in range(2):
                        act.wait_ge(s_down, e * DOWNS + k * U + (first[part] // P + tiles[part]))
                        for f in range(FC):
                            n = part * FC + f
                            act.wait_ge(s_up, e * UPS + k * (2 * FC) + (n + 1))
                            act.activation(hid[part][:, f, :], p_u[:, n % 4, 0:width[part]], ACT.Gelu,
                                           bias=weights[b]["b1"][:, f:f + 1]).then_inc(s_hid, 1)

        @block.vector
        def _(v):
            v.memset(ones[:, :], 1.0).then_inc(s_ones, 1)
            v.sem_inc(s_added, 2)

            def fold(b, pair, count):
                w = weights[b]
                here(v, b, pair)
                v.wait_ge(s_pb, count)
                v.tensor_tensor(w["b1"][:, :], w["b1"][:, :], p_b[:, 0:FC], ALU.add).then_inc(s_folded, 1)
                for i in range(HALF):
                    v.tensor_scalar(w["w1"][:, i, :], w["w1"][:, i, :], w["ln_g"][:, i:i + 1], None,
                                    ALU.mult).then_inc(s_folded, 1)

            def add(e, k, n):
                v.wait_ge(s_down, e * DOWNS + k * U + (U + n + 1))
                if grouped:
                    v.scalar_tensor_tensor(S[:, k * U + n, :], p_d[:, n % 3, 0:D], gates[:, k * U + n, bass.ds(e, 1)],
                                           S[:, k * U + n, :], ALU.mult, ALU.add).then_inc(s_added, 1)
                else:
                    v.tensor_tensor(S[:, k * U + n, :], S[:, k * U + n, :], p_d[:, n % 3, 0:D],
                                    ALU.add).then_inc(s_added, 1)

            if grouped:
                fold(0, 0, 1)
            for e, b, pair, more in each(v):
                with v.Fori(0, NB - 1) as k:
                    for n in range(U):
                        add(e, k, n)
                for n in range(U):
                    if more and n == A_T:
                        fold(1 - b, pair + b, e + 2)
                    add(e, NB - 1, n)


def mixer(nc, io, g, S, turned, spare, tables):
    with ExitStack() as ctx:
        def sb(name, shape, dtype=F32):
            return ctx.enter_context(nc.sbuf_tensor("mix_" + name, shape, dtype))

        lnp = sb("lnp", [P, 4, HALF])
        wq, wk, wv, wo = (sb(n, [P, HALF, D]) for n in ("wq", "wk", "wv", "wo"))
        bo, b2 = sb("bo", [1, D]), sb("b2", [1, D])
        w1, w2, b1 = sb("w1", [P, HALF, FF]), sb("w2", [P, FC, D]), sb("b1", [P, FC])
        with nc.Fori(0, DEPTH) as layer:
            with Phase(nc, "mixln") as ph:
                loaded = ph.sem("loaded")
                block = ph.open()
                load_ahead(block, loaded, [(lnp[:, :, :], io["mix_ln"][layer])])
            halves = lambda name: io[name][layer].rearrange("(a p) o -> p a o", p=P)
            norm(nc, "mixnorm1", S, spare, turned, g["ident"], lnp[:, 0, :], lnp[:, 1, :],
                 [(wq[:, :, :], halves("wq")), (wk[:, :, :], halves("wk")), (wv[:, :, :], halves("wv")),
                  (wo[:, :, :], halves("wo")), (bo[:, :], io["bo"][bass.ds(layer, 1), :])])
            attention(nc, g, (wq, wk, wv, wo, bo), S, turned, spare,
                      [(w1[:, :, :], halves("w1")), (w2[:, :, :], halves("w2")),
                       (b1[:, :], io["mix_b1"][layer]), (b2[:, :], io["mix_b2"][bass.ds(layer, 1), :])],
                      (0, layer * (ATTN_GROUPS + FF_GROUPS), ATTN_GROUPS, [layer * n for n in halved(ATTN_GROUPS, FF_GROUPS)])
                      + tables)
            norm(nc, "mixnorm2", S, spare, turned, g["ident"], lnp[:, 2, :], lnp[:, 3, :])
            mlp(nc, g, "mixff", S, turned, [{"w1": w1, "w2": w2, "b1": b1, "b2": b2}],
                job=(0, layer * (ATTN_GROUPS + FF_GROUPS) + ATTN_GROUPS, FF_GROUPS,
                     [layer * n + m for n, m in zip(halved(ATTN_GROUPS, FF_GROUPS), halved(ATTN_GROUPS))]) + tables)


def add_to(nc, X, S):
    with Phase(nc, "addto") as ph:
        s_done = ph.sem("done")
        block = ph.open()

        @block.vector
        def _(v):
            with v.Fori(0, NB) as k:
                v.tensor_tensor(X[:, bass.ds(k * U, U), :], X[:, bass.ds(k * U, U), :], S[:, bass.ds(k * U, U), :],
                                ALU.add).then_inc(s_done, 1)


def route(nc, g, turned, wr, br, gates, top2, iota8):
    with Phase(nc, "route2" if top2 else "route") as ph:
        logits = ph.sb("logits", [P, NT, R])
        m = ph.sb("m", [P, NT])
        best = ph.sb("best", [P, NT, 8])
        where = ph.sb("where", [P, NT, 8], U32)
        where_f = ph.sb("where_f", [P, NT, 2])
        hot = ph.sb("hot", [P, NT, R])
        den = ph.sb("den", [P, NT])
        ones = ph.sb("ones", [1, P])
        p_l = ph.ps("l", [P, 512])
        s_ones, s_l, s_x, s_e, s_best, s_where = (ph.sem(x) for x in ("ones", "l", "x", "e", "best", "where"))
        block = ph.open()

        @block.tensor
        def _(pe):
            pe.wait_ge(s_ones, 1)
            for t in range(NT):
                for a in range(HALF):
                    pe.matmul(p_l[:, t * R:(t + 1) * R], turned[:, a, t * P:(t + 1) * P], wr[:, a, :],
                              start=(a == 0), stop=False)
                mm = pe.matmul(p_l[:, t * R:(t + 1) * R], ones[:, :], br[:, :], start=False, stop=True)
            mm.then_inc(s_l, 1)

        @block.scalar
        def _(act):
            act.wait_ge(s_x, 2)
            act.activation(logits[:, :, :], logits[:, :, :], ACT.Exp).then_inc(s_e, 1)

        @block.vector
        def _(v):
            steps = [0]

            def step(ins):
                steps[0] += 1
                ins.then_inc(s_x, 1)
                v.wait_ge(s_x, steps[0])

            v.memset(ones[:, :], 1.0).then_inc(s_ones, 1)
            v.wait_ge(s_l, 1)
            lg = p_l[:, 0:NT * R].rearrange("p (t e) -> p t e", e=R)
            step(v.tensor_reduce(m[:, :], lg, X_AXIS, ALU.max))
            step(v.tensor_tensor(logits[:, :, :], lg, m[:, :, None].to_broadcast([P, NT, R]), ALU.subtract))
            v.wait_ge(s_e, 1)
            step(v.tensor_reduce(den[:, :], logits[:, :, :], X_AXIS, ALU.add))
            step(v.reciprocal(m[:, :], den[:, :]))
            probs = logits if top2 else gates
            step(v.tensor_tensor(probs[:, :, :], logits[:, :, :], m[:, :, None].to_broadcast([P, NT, R]), ALU.mult))
            if top2:
                for t in range(NT):
                    v.max(best[:, t, :], probs[:, t, :]).then_inc(s_best, 1)
                v.wait_ge(s_best, NT)
                for t in range(NT):
                    v.max_index(where[:, t, :], best[:, t, :], probs[:, t, :]).then_inc(s_where, 1)
                v.wait_ge(s_where, NT)
                step(v.tensor_copy(where_f[:, :, :], where[:, :, 0:2]))
                step(v.tensor_tensor(den[:, :], best[:, :, 0], best[:, :, 1], ALU.add))
                step(v.reciprocal(m[:, :], den[:, :]))
                step(v.tensor_tensor(best[:, :, 0:2], best[:, :, 0:2], m[:, :, None].to_broadcast([P, NT, 2]), ALU.mult))
                for n, to in ((0, gates), (1, hot)):
                    step(v.tensor_tensor(to[:, :, :], where_f[:, :, n, None].to_broadcast([P, NT, R]),
                                         iota8[:, None, :].to_broadcast([P, NT, R]), ALU.is_equal))
                    step(v.tensor_tensor(to[:, :, :], to[:, :, :], best[:, :, n, None].to_broadcast([P, NT, R]), ALU.mult))
                step(v.tensor_tensor(gates[:, :, :], gates[:, :, :], hot[:, :, :], ALU.add))


QS = float(DH) ** 0.25


def taylor_project(nc, g, w, turned, QK, v1, fac, ahead=()):
    wqkv, bqkv, temp, valid = w
    with Phase(nc, "tproj") as ph:
        ones = ph.sb("ones", [1, P])
        sq = ph.sb("sq", [P, 2, 2 * D])
        ssq = ph.sb("ssq", [P, NT, 2, H])
        nrm = ph.sb("nrm", [P, NT, 2, H])
        p_qk = ph.ps("qk", [P, 2, 512])
        p_v = ph.ps("v", [P, 2, 512])
        names = "ahead ones qk v qk_out v_out sq ssq root x"
        s = {n: ph.sem(n) for n in names.split()}
        block = ph.open()
        load_ahead(block, s["ahead"], ahead)

        @block.tensor
        def _(pe):
            pe.wait_ge(s["ones"], 1)
            for t in range(NT):
                if t >= 2:
                    pe.wait_ge(s["v_out"], t - 1)
                at = slice(t * P, (t + 1) * P)
                for out, c0, c1, done in ((p_qk, 0, 2 * D, "qk"), (p_v, 2 * D, 3 * D, "v")):
                    for a in range(HALF):
                        pe.matmul(out[:, t % 2, 0:c1 - c0], turned[:, a, at], wqkv[:, a, c0:c1], start=(a == 0), stop=False)
                    pe.matmul(out[:, t % 2, 0:c1 - c0], ones[:, :], bqkv[:, c0:c1], start=False,
                              stop=True).then_inc(s[done], 1)

        @block.scalar
        def _(act):
            for t in range(NT):
                act.wait_ge(s["qk"], t + 1)
                act.activation(QK[:, t, :], p_qk[:, t % 2, :], ACT.Copy).then_inc(s["qk_out"], 1)
                act.wait_ge(s["v"], t + 1)
                act.activation(v1[:, t, :, 1:HW], p_v[:, t % 2, 0:D].rearrange("p (h w) -> p h w", w=DH),
                               ACT.Copy, scale=valid[:, t:t + 1]).then_inc(s["v_out"], 1)
            act.wait_ge(s["ssq"], NT)
            act.activation(nrm[:, :, :, :], ssq[:, :, :, :], ACT.Sqrt).then_inc(s["root"], 1)

        @block.vector
        def _(v):
            v.memset(ones[:, :], 1.0).then_inc(s["ones"], 1)
            v.tensor_copy(v1[:, :, :, 0], valid[:, :, None].to_broadcast([P, NT, H])).then_inc(s["x"], 1)
            for t in range(NT):
                v.wait_ge(s["qk_out"], t + 1)
                v.tensor_tensor(sq[:, t % 2, :], QK[:, t, :], QK[:, t, :], ALU.mult).then_inc(s["sq"], 1)
                v.wait_ge(s["sq"], t + 1)
                v.tensor_reduce(ssq[:, t, :, :], sq[:, t % 2, :].rearrange("p (s h w) -> p s h w", s=2, w=DH),
                                X_AXIS, ALU.add).then_inc(s["ssq"], 1)
            v.wait_ge(s["root"], 1)
            v.tensor_scalar(nrm[:, :, 0, :], nrm[:, :, 0, :], QS, 1e-12, ALU.mult, ALU.max).then_inc(s["x"], 1)
            v.tensor_scalar(nrm[:, :, 1, :], nrm[:, :, 1, :], 1e-12, None, ALU.max).then_inc(s["x"], 1)
            v.wait_ge(s["x"], 3)
            v.reciprocal(fac[:, :, :, :], nrm[:, :, :, :]).then_inc(s["x"], 1)
            v.wait_ge(s["x"], 4)
            v.tensor_scalar(fac[:, :, 1, :], fac[:, :, 1, :], QS, None, ALU.mult).then_inc(s["x"], 1)
            v.scalar_tensor_tensor(fac[:, :, 0, :], fac[:, :, 0, :], QS * QS,
                                   temp[:, None, :].to_broadcast([P, NT, H]), ALU.mult, ALU.mult).then_inc(s["x"], 1)


OFFSETS = DH // 2
PAIRS = OFFSETS * DH // P
KEYS_GROUPS = 20
PER_BANK = 15
SPLIT = 3


def window(x, n):
    return bass.AP(tensor=x.tensor, offset=x.offset, ap=[x.ap[0], [1, n], x.ap[1]])


def taylor_keys(nc, g, w, QK, v1, fac, kv2, kv_half, kv1, kv0, job):
    pair_scale, half_mask = w
    with Phase(nc, "tkeys") as ph:
        krow = ph.sb("krow", [P, H, DH + OFFSETS])
        kk = ph.sb("kk", [P, H, OFFSETS, DH])
        kk_half = ph.sb("kk_half", [P, H, OFFSETS])
        ones = ph.sb("ones", [P, 1])
        zero = ph.sb("zero", [P, 512])
        p2 = ph.ps("p2", [P, 3, 512])
        p_half = ph.ps("half", [P, 512])
        p1 = ph.ps("p1", [P, 512])
        p0 = ph.ps("p0", [P, 512])
        names = "init k kk pp lin out"
        s = {n: ph.sem(n) for n in names.split()}
        block = ph.open()
        gather_ahead(ph, block, g, job, None, [])

        @block.tensor
        def _(pe):
            pe.wait_ge(s["init"], 2)
            pe.sem_inc(s["pp"], H // 2)
            pe.sem_inc(s["lin"], 1)
            for bank in [p2[:, n, :] for n in range(3)] + [p_half[:, :]]:
                pe.matmul(bank, zero[:, 0:P], zero[:, :], start=True, stop=False, skip_group_check=True)
            pe.matmul(p1[0:DH, :], zero[:, 0:DH], zero[:, :], start=True, stop=False, skip_group_check=True)
            pe.matmul(p0[0:1, :], zero[:, 0:1], zero[:, :], start=True, stop=False, skip_group_check=True)
            with pe.Fori(0, NT) as t:
                pe.wait_ge(s["k"], t * 3 + 3)
                for h in range(H):
                    pe.matmul(p1[0:DH, h * HW:(h + 1) * HW], krow[:, h, 0:DH], v1[:, t, h, :],
                              start=False, stop=False, skip_group_check=True)
                pe.matmul(p_half[:, 0:MSG], kk_half[:, :, :].rearrange("p h d -> p (h d)"),
                          v1[:, t, :, :].rearrange("p h w -> p (h w)"), start=False, stop=False, skip_group_check=True)
                pe.matmul(p0[0:1, 0:MSG], ones[:, :], v1[:, t, :, :].rearrange("p h w -> p (h w)"),
                          start=False, stop=False, skip_group_check=True).then_inc(s["lin"], 1)
                for h in range(H):
                    if h % 2 == 0:
                        pe.wait_ge(s["kk"], t * (H // 2) + (h // 2 + 2))
                    for c in range(PAIRS):
                        n = h * PAIRS + c
                        mm = pe.matmul(p2[:, n // PER_BANK, n % PER_BANK * HW:(n % PER_BANK + 1) * HW],
                                       kk[:, h, :, :].rearrange("p d i -> p (d i)")[:, c * P:(c + 1) * P],
                                       v1[:, t, h, :], start=False, stop=False, skip_group_check=True)
                    if h % 2:
                        mm.then_inc(s["pp"], 1)

        @block.vector
        def _(v):
            v.memset(ones[:, :], 1.0).then_inc(s["init"], 1)
            v.memset(zero[:, :], 0.0).then_inc(s["init"], 1)
            v.sem_inc(s["kk"], 1)
            with v.Fori(0, NT) as t:
                v.wait_ge(s["lin"], t + 1)
                v.wait_ge(s["kk"], t * (H // 2) + 1)
                for to, width in ((0, DH), (DH, OFFSETS)):
                    v.tensor_tensor(krow[:, :, to:to + width],
                                    QK[:, t, D:2 * D].rearrange("p (h w) -> p h w", w=DH)[:, :, 0:width],
                                    fac[:, t, 1, :, None].to_broadcast([P, H, width]), ALU.mult).then_inc(s["k"], 1)
                v.wait_ge(s["k"], t * 3 + 2)
                v.tensor_tensor(kk_half[:, :, :], krow[:, :, 0:OFFSETS], krow[:, :, OFFSETS:DH], ALU.mult).then_inc(s["k"], 1)
                for h in range(H):
                    if h % 2 == 0:
                        v.wait_ge(s["pp"], t * (H // 2) + (h // 2 + 1))
                    last = v.tensor_tensor(kk[:, h, :, :], krow[:, h, None, 0:DH].to_broadcast([P, OFFSETS, DH]),
                                           window(krow[:, h, 0:DH], OFFSETS), ALU.mult)
                    if h % 2:
                        last.then_inc(s["kk"], 1)
            v.wait_ge(s["lin"], NT + 1)
            v.wait_ge(s["pp"], (NT + 1) * (H // 2))
            for h in range(H):
                for c in range(PAIRS):
                    n = h * PAIRS + c
                    v.tensor_scalar(kv2[:, n, :], p2[:, n // PER_BANK, n % PER_BANK * HW:(n % PER_BANK + 1) * HW],
                                    pair_scale[:, min(c, 1):min(c, 1) + 1], None, ALU.mult).then_inc(s["out"], 1)
            v.tensor_tensor(kv_half[:, :, :], p_half[:, 0:MSG].rearrange("p (h w) -> p h w", w=HW),
                            half_mask[:, :, None].to_broadcast([P, H, HW]), ALU.mult).then_inc(s["out"], 1)
            v.tensor_scalar(kv1[:, :], p1[0:DH, 0:MSG], QS ** 2 / N, None, ALU.mult).then_inc(s["out"], 1)
            v.tensor_scalar(kv0[:, :], p0[0:1, 0:MSG], QS ** 4 / N, None, ALU.mult).then_inc(s["out"], 1)


JR = 4
GH = H // 2


def taylor_queries(nc, g, w, QK, fac, kv2, kv_half, kv1, kv0, X, spare, job):
    wp, bp, select = w
    with Phase(nc, "tqueries") as ph:
        qrow = ph.sb("qrow", [P, H, DH])
        q_half = ph.sb("q_half", [P, U, H, OFFSETS])
        rest = ph.sb("rest", [P, H, DH])
        parts = ph.sb("parts", [P, H, SPLIT, DH], BF16)
        ident = ph.sb("ident", [P, P], BF16)
        sel = ph.sb("sel", [SPLIT * DH, PAIRS + 1, P], BF16)
        qt = ph.sb("qt", [SPLIT * DH, U, H, P], BF16)
        qi = spare[:, 0:U * H * P // D, :].rearrange("p t f -> p (t f)").rearrange("p (u h n) -> p u h n", u=U, h=H)
        qq = ph.sb("qq", [P, JR, PAIRS, P])
        qq_half = ph.sb("qq_half", [P, P])
        y = ph.sb("y", [P, H, DH])
        rec = ph.sb("rec", [P, H])
        yt = ph.sb("yt", [P, HALF, P])
        ones = ph.sb("ones", [1, P])
        p_t = ph.ctx.enter_context(nc.psum_tensor("tqueries_ps_t", [P, 1024], BF16))
        p_o = ph.ps("o", [P, 512])
        p_i = ph.ps("i", [P, 512])
        p_j = ph.ps("j", [P, JR, 512])
        p_y = ph.ps("y", [P, 512])
        names = ("ones init q hi rest mid parts turned qt i qi j qq yy sum rec y yT yt half o added")
        s = {n: ph.sem(n) for n in names.split()}
        block = ph.open()
        DIFF = DH * SPLIT
        gather_ahead(ph, block, g, job, None, [])

        def passes(eng, body):
            for j in range(U):
                body(0, j, j)
            with eng.Fori(1, NB - 1) as k:
                for j in range(U):
                    body(k * U + j, j, None)
            for j in range(U):
                body((NB - 1) * U + j, j, (NB - 1) * U + j)

        def body_for(step):
            return lambda t, j, n: step(j if n is not None and n < U else t, j, n is None or n >= 1,
                                        n is None or n + 1 < NT, n is None or n + 2 < NT)

        @block.tensor
        def _(pe):
            def turn(t, j):
                pe.wait_ge(s["parts"], t + 1)
                pe.wait_ge(s["qt"], t + 1)
                for h in range(H):
                    mm = pe.transpose(p_t[0:DIFF, h * P:(h + 1) * P], parts[:, h, :, :].rearrange("p s w -> p (s w)"),
                                      ident[:, :])
                mm.then_inc(s["turned"], 1)

            def select_i(t, j, group):
                pe.wait_ge(s["qt"], t + 2)
                pe.wait_ge(s["qi"], t * 2 + (group + 1))
                pe.matmul(p_i[:, :], sel[:, PAIRS, :],
                          qt[:, j, group * GH:(group + 1) * GH, :].rearrange("p h n -> p (h n)"),
                          start=True, stop=True).then_inc(s["i"], 1)

            def select_j(t, j, h):
                pe.wait_ge(s["qq"], t * H + (h + 1))
                for c in range(PAIRS):
                    mm = pe.matmul(p_j[:, h % JR, c * P:(c + 1) * P], sel[:, c, :], qt[:, j, h, :], start=True, stop=True)
                mm.then_inc(s["j"], 1)

            def linear(t, j):
                pe.wait_ge(s["y"], t + 1)
                pe.wait_ge(s["qi"], t * 2 + 3)
                pe.matmul(p_y[:, 0:MSG], ones[:, :], kv0[:, :], start=True, stop=False, skip_group_check=True)
                for h in range(H):
                    pe.matmul(p_y[:, h * HW:(h + 1) * HW], qi[0:DH, j, h, :], kv1[:, h * HW:(h + 1) * HW],
                              start=False, stop=False, skip_group_check=True)

            def sums(t, h):
                pe.wait_ge(s["qq"], t * H + (h + JR + 1))
                for c in range(PAIRS):
                    mm = pe.matmul(p_y[:, h * HW:(h + 1) * HW], qq[:, h % JR, c, :], kv2[:, h * PAIRS + c, :],
                                   start=False, stop=False, skip_group_check=True)
                mm.then_inc(s["yy"], 1)

            def turn_half(j):
                return pe.transpose(p_o[:, D:D + P], q_half[:, j, :, :].rearrange("p h d -> p (h d)"), g["ident"][:, :])

            def turn_y(t, j, after):
                pe.wait_ge(s["y"], t + 2)
                pe.wait_ge(s["added"], t + 1)
                for a in range(HALF):
                    mm = pe.transpose(p_o[:, a * P:(a + 1) * P],
                                      y[:, :, :].rearrange("p h w -> p (h w)")[:, a * P:(a + 1) * P], g["ident"][:, :])
                if after:
                    mm = turn_half((j + 1) % U)
                mm.then_inc(s["yT"], 1)

            def project(t, after):
                pe.wait_ge(s["yt"], t + 1)
                if after:
                    pe.wait_ge(s["half"], t + 2)
                for a in range(HALF):
                    pe.matmul(p_o[:, 0:D], yt[:, a, :], wp[:, a, :], start=(a == 0), stop=False)
                pe.matmul(p_o[:, 0:D], ones[:, :], bp[:, :], start=False, stop=True).then_inc(s["o"], 1)

            def step(t, j, before, after, _):
                nj = (j + 1) % U
                if after:
                    turn(t + 1, nj)
                linear(t, j)
                for h in range(H):
                    if h == 0 and before:
                        turn_y(t - 1, (j - 1) % U, True)
                    if h == 2 and before:
                        project(t - 1, True)
                    sums(t, h)
                    if after and h in (3, 4):
                        select_i(t + 1, nj, h - 3)
                    if h + 3 < H:
                        select_j(t, j, h + 3)
                    elif after:
                        select_j(t + 1, nj, h + 3 - H)
                pe.wait_ge(s["half"], t + 1)
                pe.matmul(p_y[:, 0:MSG], qq_half[:, :], kv_half[:, :, :].rearrange("p h w -> p (h w)"),
                          start=False, stop=False, skip_group_check=True).then_inc(s["sum"], 1)

            pe.wait_ge(s["init"], 2)
            pe.wait_ge(s["ones"], 1)
            turn(0, 0)
            turn_half(0).then_inc(s["yT"], 1)
            for group in range(2):
                select_i(0, 0, group)
            for h in range(3):
                select_j(0, 0, h)
            passes(pe, body_for(step))
            turn_y(NT - 1, U - 1, False)
            project(NT - 1, False)

        @block.scalar
        def _(act):
            def turned(t, j):
                act.wait_ge(s["turned"], t + 1)
                act.activation(qt[:, j, :, :], p_t[0:DIFF, :].rearrange("p (h n) -> p h n", h=H), ACT.Copy).then_inc(s["qt"], 1)

            def half(t):
                act.wait_ge(s["yT"], t + 1)
                act.activation(qq_half[:, :], p_o[:, D:D + P], ACT.Copy).then_inc(s["half"], 1)

            def turned_y(t):
                act.wait_ge(s["yT"], t + 2)
                act.activation(yt[:, :, :], p_o[:, 0:D].rearrange("p (a n) -> p a n", a=HALF), ACT.Copy).then_inc(s["yt"], 1)

            def high(t):
                act.wait_ge(s["q"], 2 * t + 1)
                act.activation(parts[:, :, 0, :], qrow[:, :, :], ACT.Copy).then_inc(s["hi"], 1)

            def middle(t):
                act.wait_ge(s["rest"], t + 1)
                act.activation(parts[:, :, 1, :], rest[:, :, :], ACT.Copy).then_inc(s["mid"], 1)

            def selected(t, j, group):
                act.wait_ge(s["i"], t * 2 + (group + 1))
                act.activation(qi[:, j, group * GH:(group + 1) * GH, :], p_i[:, :].rearrange("p (h n) -> p h n", h=GH),
                               ACT.Copy).then_inc(s["qi"], 1)

            def step(t, j, before, after, after2):
                if after:
                    turned(t + 1, (j + 1) % U)
                if before:
                    half(t)
                    turned_y(t - 1)
                if after2:
                    high(t + 2)
                    middle(t + 2)
                if after:
                    for group in range(2):
                        selected(t + 1, (j + 1) % U, group)

            act.sem_inc(s["qt"], 1)
            act.sem_inc(s["qi"], 1)
            high(0)
            middle(0)
            turned(0, 0)
            half(0)
            high(1)
            middle(1)
            for group in range(2):
                selected(0, 0, group)
            passes(act, body_for(step))
            turned_y(NT - 1)

        @block.vector
        def _(v):
            def scaled(t, j, first=False):
                if not first:
                    v.wait_ge(s["parts"], t)
                    v.wait_ge(s["q"], 2 * t)
                v.tensor_tensor(qrow[:, :, :], QK[:, t, 0:D].rearrange("p (h w) -> p h w", w=DH),
                                fac[:, t, 0, :, None].to_broadcast([P, H, DH]), ALU.mult).then_inc(s["q"], 1)
                v.wait_ge(s["q"], 2 * t + 1)
                v.tensor_tensor(q_half[:, j, :, :], qrow[:, :, 0:OFFSETS], qrow[:, :, OFFSETS:DH], ALU.mult).then_inc(s["q"], 1)

            def middle(t):
                v.wait_ge(s["hi"], t + 1)
                v.tensor_tensor(rest[:, :, :], qrow[:, :, :], parts[:, :, 0, :], ALU.subtract).then_inc(s["rest"], 1)

            def low(t):
                v.wait_ge(s["mid"], t + 1)
                v.tensor_tensor(parts[:, :, 2, :], rest[:, :, :], parts[:, :, 1, :], ALU.subtract).then_inc(s["parts"], 1)

            def products(t, j, h):
                v.wait_ge(s["qi"], t * 2 + (h // GH + 2))
                v.wait_ge(s["yy"], t * H + (h + 1))
                v.wait_ge(s["j"], t * H + (h + 1))
                v.tensor_tensor(qq[:, h % JR, :, :], p_j[:, h % JR, :].rearrange("p (c n) -> p c n", n=P),
                                qi[:, j, h, None, :].to_broadcast([P, PAIRS, P]), ALU.mult).then_inc(s["qq"], 1)

            def quotient(t):
                v.wait_ge(s["sum"], t + 1)
                yy = p_y[:, 0:MSG].rearrange("p (h w) -> p h w", w=HW)
                v.reciprocal(rec[:, :], yy[:, :, 0]).then_inc(s["rec"], 1)
                v.wait_ge(s["rec"], t + 1)
                v.tensor_tensor(y[:, :, :], yy[:, :, 1:HW], rec[:, :, None].to_broadcast([P, H, DH]), ALU.mult).then_inc(s["y"], 1)

            def add(t):
                v.wait_ge(s["o"], t + 1)
                v.tensor_tensor(X[:, t, :], X[:, t, :], p_o[:, 0:D], ALU.add).then_inc(s["added"], 1)

            def step(t, j, before, after, after2):
                for h in range(H):
                    products(t, j, h)
                    if h == 1 and before:
                        quotient(t - 1)
                    if h == 2 and after2:
                        scaled(t + 2, (j + 2) % U)
                    if h == 3 and after2:
                        middle(t + 2)
                    if h == 4 and after2:
                        low(t + 2)
                    if h == 5 and before:
                        add(t - 1)

            v.memset(ones[:, :], 1.0).then_inc(s["ones"], 1)
            v.tensor_copy(ident[:, :], g["ident"][:, :]).then_inc(s["init"], 1)
            v.tensor_copy(sel[:, :, :], select[:, :, :]).then_inc(s["init"], 1)
            v.sem_inc(s["yy"], JR)
            v.sem_inc(s["qq"], JR)
            v.sem_inc(s["y"], 1)
            v.sem_inc(s["added"], 1)
            for t in range(2):
                scaled(t, t, t == 0)
                middle(t)
                low(t)
            passes(v, body_for(step))
            quotient(NT - 1)
            add(NT - 1)


def experts3(nc, g, X, turned, gates, ws, cols, bo):
    EX = R
    with Phase(nc, "experts3") as ph:
        h1 = ph.sb("h1", [P, 2, HALF, B_N])
        h2 = ph.sb("h2", [P, 2, HALF, B_N])
        scale, bias = ph.sb("scale", [P, 2, EX * HALF]), ph.sb("bias", [P, 2, EX * HALF])
        root = ph.sb("root", [P, 2, EX * HALF])
        ones = ph.sb("ones", [1, P])
        p_1 = ph.ps("p1", [P, 2, 512])
        p_2 = ph.ps("p2", [P, 2, 512])
        p_y = ph.ps("py", [P, 4, 512])
        names = "ones x root cols u1 h1 u2 h2 y added"
        s = {n: ph.sem(n) for n in names.split()}
        block = ph.open()
        width, first, tiles = (A_N, B_N), (0, A_N), (A_T, B_T)
        items = [(e, part) for e in range(EX) for part in range(2)]
        n_items = len(items)

        def per_item(k, m):
            return k * (HALF * n_items) + HALF * m

        @block.tensor
        def _(pe):
            pe.wait_ge(s["ones"], 1)
            with pe.Fori(0, NB) as k:
                def one(m):
                    e, part = items[m]
                    for f in range(HALF):
                        pe.wait_ge(s["h1"], per_item(k, m) + (f + 1))
                        for i in range(HALF):
                            mm = pe.matmul(p_1[:, f, 0:width[part]], ws[0][:, e, i, f * P:(f + 1) * P],
                                           turned[:, i, bass.ds(k * (U * P) + first[part], width[part])],
                                           start=(i == 0), stop=(i == HALF - 1))
                        mm.then_inc(s["u1"], 1)

                def two(m):
                    e, part = items[m]
                    pe.wait_ge(s["h1"], per_item(k, m) + 2 * HALF)
                    for f in range(HALF):
                        pe.wait_ge(s["h2"], per_item(k, m) + (f + 1))
                        for i in range(HALF):
                            mm = pe.matmul(p_2[:, f, 0:width[part]], ws[1][:, e, i, f * P:(f + 1) * P],
                                           h1[:, m % 2, i, 0:width[part]], start=(i == 0), stop=(i == HALF - 1))
                        mm.then_inc(s["u2"], 1)

                def three(m):
                    e, part = items[m]
                    pe.wait_ge(s["h2"], per_item(k, m) + 2 * HALF)
                    for j in range(tiles[part]):
                        n = e * U + part * A_T + j
                        pe.wait_ge(s["added"], k * (EX * U) + (n + 1))
                        for i in range(HALF):
                            pe.matmul(p_y[:, n % 4, 0:D], h2[:, m % 2, i, j * P:(j + 1) * P], ws[2][:, e, i, :],
                                      start=(i == 0), stop=False)
                        pe.matmul(p_y[:, n % 4, 0:D], ones[:, :], bo[:, e * D:(e + 1) * D], start=False,
                                  stop=True).then_inc(s["y"], 1)

                for m in range(n_items + 2):
                    if m < n_items:
                        one(m)
                    if 1 <= m <= n_items:
                        two(m - 1)
                    if m >= 2:
                        three(m - 2)

        @block.scalar
        def _(act):
            act.sem_inc(s["h1"], HALF)
            act.sem_inc(s["h2"], HALF)
            act.wait_ge(s["x"], 1)
            act.activation(root[:, :, :], root[:, :, :], ACT.Sqrt).then_inc(s["root"], 1)
            act.wait_ge(s["cols"], 2)
            with act.Fori(0, NB) as k:
                def relu(m, layer):
                    e, part = items[m]
                    up, out, hid, p_ = (("u1", "h1", h1, p_1), ("u2", "h2", h2, p_2))[layer]
                    for f in range(HALF):
                        act.wait_ge(s[up], per_item(k, m) + (f + 1))
                        act.activation(hid[:, m % 2, f, 0:width[part]], p_[:, f, 0:width[part]], ACT.Relu,
                                       bias=bias[:, layer, e * HALF + f:e * HALF + f + 1],
                                       scale=scale[:, layer, e * HALF + f:e * HALF + f + 1]).then_inc(s[out], 1)

                for m in range(n_items + 1):
                    if m < n_items:
                        relu(m, 0)
                    if m:
                        relu(m - 1, 1)

        @block.vector
        def _(v):
            v.memset(ones[:, :], 1.0).then_inc(s["ones"], 1)
            v.sem_inc(s["added"], 4)
            v.tensor_scalar(root[:, :, :], cols[:, :, 4, :], 0.001, None, ALU.add).then_inc(s["x"], 1)
            v.wait_ge(s["root"], 1)
            v.reciprocal(root[:, :, :], root[:, :, :]).then_inc(s["x"], 1)
            v.tensor_tensor(bias[:, :, :], cols[:, :, 0, :], cols[:, :, 3, :], ALU.subtract).then_inc(s["x"], 1)
            v.wait_ge(s["x"], 3)
            v.tensor_tensor(scale[:, :, :], cols[:, :, 1, :], root[:, :, :], ALU.mult).then_inc(s["cols"], 1)
            v.wait_ge(s["cols"], 1)
            v.tensor_tensor(bias[:, :, :], bias[:, :, :], scale[:, :, :], ALU.mult).then_inc(s["x"], 1)
            v.wait_ge(s["x"], 4)
            v.tensor_tensor(bias[:, :, :], bias[:, :, :], cols[:, :, 2, :], ALU.add).then_inc(s["cols"], 1)
            with v.Fori(0, NB) as k:
                for e, part in items:
                    for j in range(tiles[part]):
                        n = e * U + part * A_T + j
                        t = k * U + (part * A_T + j)
                        v.wait_ge(s["y"], k * (EX * U) + (n + 1))
                        v.scalar_tensor_tensor(X[:, t, :], p_y[:, n % 4, 0:D], gates[:, t, e:e + 1], X[:, t, :],
                                               ALU.mult, ALU.add).then_inc(s["added"], 1)


def build(nc, io, out, dbg=None):
    with ExitStack() as ctx:
        def sb(name, shape, dtype=F32, to=ctx):
            return to.enter_context(nc.sbuf_tensor(name, shape, dtype))

        def dram(name, shape):
            return nc.dram_tensor(name, shape, F32).ap()

        def halves(name, n=None):
            a = io[name] if n is None else io[name][n]
            return a.rearrange("(a p) o -> p a o", p=P)

        g = {n: sb("idx_" + n, [EP, ET + 2 * GT], I32) for n in ("src0", "dst0", "src1", "dst1", "put")}
        for layer in range(2):
            g[f"got{layer}"] = [[ctx.enter_context(nc.semaphore(f"got{layer}{side}{b}")) for b in range(2)] for side in range(2)]
            for n in ("scattered",):
                g[f"{n}{layer}"] = [ctx.enter_context(nc.semaphore(f"{n}{layer}{b}")) for b in range(2)]
        g["dst"] = sb("idx_dst", [EP, ET], I32)
        g["ident"] = sb("ident", [P, P])
        g["blocks"] = sb("blocks", [P, P])
        iota8 = sb("iota8", [P, R])
        X = sb("X", [P, NT, D])
        XN = sb("XN", [P, NT, D])
        table0, table1 = dram("table0", [NP, ROW]), dram("table1", [R * NP, ROW])
        dtable1 = dram("dtable1", [R * NP, H])
        totals0, totals1 = dram("totals0", [NP, ROW]), dram("totals1", [NP, ROW])
        firsts0, firsts1 = dram("firsts0", [ET, ROW]), dram("firsts1", [ET, ROW])
        rows0 = tuple(dram(f"{n}_rows0", [(NG + 2) * GE, ROW]) for n in ("src", "dst"))
        rows1 = (dram("src_rows1", [(NG + 2) * GE, ROW]), dram("dst_rows1", [(NG + 2) * GE, H]))
        load_x(nc, io, X)
        edge_prep(nc, io, g, [(iota8[:, :], io["iota"][:, 0:R].partition_broadcast(P))])

        with ExitStack() as part:
            HT = sb("HT_g0", [P, HALF, NP], to=part)
            norm(nc, "norm0", X, XN, HT, g["ident"])
            gnn_table(nc, io, g, 0, HT, table0, None)
        with ExitStack() as part:
            HT = sb("HT_m0", [P, HALF, NP], to=part)
            spare = sb("spare_m0", [P, NT, D], to=part)
            mixer(nc, io, g, XN, HT, spare, ((table0, table0), rows0))
        edges(nc, io, g, 0, *rows0, totals0, firsts0)
        combine(nc, io, g, 0, totals0, firsts0, X)
        add_to(nc, X, XN)

        with ExitStack() as part:
            HT = sb("HT_f0", [P, HALF, NP], to=part)
            gates = sb("gates0", [P, NT, R], to=part)
            wr, br = sb("wr0", [P, HALF, R], to=part), sb("br0", [1, R], to=part)
            weights = [{"w1": sb(f"moe_w1{b}", [P, HALF, FF], to=part), "w2": sb(f"moe_w2{b}", [P, FC, D], to=part),
                        "b1": sb(f"moe_b1{b}", [P, FC], to=part), "b2": sb(f"moe_b2{b}", [1, D], to=part),
                        "ln_g": sb(f"moe_g{b}", [P, HALF], to=part), "ln_b": sb(f"moe_b{b}", [P, HALF], to=part)}
                       for b in range(2)]
            norm(nc, "norm1", X, XN, HT, g["ident"], ahead=[(wr[:, :, :], halves("wr0")), (br[:, :], io["br0"])])
            route(nc, g, HT, wr, br, gates, True, iota8)
            norm(nc, "norm2", XN, XN, HT, g["ident"])

            def load(e, b):
                w = weights[b]
                return [(w["w1"][:, :, :], halves("moe_w1", e)), (w["w2"][:, :, :], halves("moe_w2", e)),
                        (w["b1"][:, :], io["moe_b1"][e]), (w["b2"][:, :], io["moe_b2"][e]),
                        (w["ln_g"][:, :], io["moe_g"][e]), (w["ln_b"][:, :], io["moe_b"][e])]

            mlp(nc, g, "moe", X, HT, weights, experts=R, load=load, gates=gates)

        with ExitStack() as part:
            QK = sb("QK", [P, NT, 2 * D], to=part)
            v1 = sb("v1", [P, NT, H, HW], to=part)
            fac = sb("fac", [P, NT, 2, H], to=part)
            with ExitStack() as inner:
                HT = sb("HT_g1", [P, HALF, NP], to=inner)
                wqkv, bqkv = sb("wqkv", [P, HALF, 3 * D], to=inner), sb("bqkv", [1, 3 * D], to=inner)
                temp, valid = sb("temp", [P, H], to=inner), sb("valid", [P, NT], to=inner)
                norm(nc, "norm3", X, XN, HT, g["ident"],
                     ahead=[(wqkv[:, :, :], halves("wqkv")), (bqkv[:, :], io["bqkv"]),
                            (temp[:, :], io["temp"].partition_broadcast(P)), (valid[:, :], io["valid"])])
                taylor_project(nc, g, (wqkv, bqkv, temp, valid), HT, QK, v1, fac)
                with ExitStack() as deep:
                    gnn_table(nc, io, g, 1, HT, table1, dtable1)
            kv2, kv_half = sb("kv2", [P, H * PAIRS, HW], to=part), sb("kv_half", [P, H, HW], to=part)
            kv1, kv0 = sb("kv1", [DH, MSG], to=part), sb("kv0", [1, MSG], to=part)
            wp, bp = sb("wp", [P, HALF, D], to=part), sb("bp", [1, D], to=part)
            select = sb("select", [SPLIT * DH, PAIRS + 1, P], to=part)
            pair_scale, half_mask = sb("pair_scale", [P, 2], to=part), sb("half_mask", [P, H], to=part)
            with Phase(nc, "tload") as ph:
                loaded = ph.sem("loaded")
                block = ph.open()
                load_ahead(block, loaded, [(wp[:, :, :], halves("wproj")), (bp[:, :], io["bproj"]), (select[:, :, :], io["select"]),
                                           (pair_scale[:, :], io["pair_scale"]), (half_mask[:, :], io["half_mask"])])
            taylor_keys(nc, g, (pair_scale, half_mask), QK, v1, fac, kv2, kv_half, kv1, kv0,
                        (1, 0, KEYS_GROUPS, [0, 0], (table1, dtable1), rows1))
            taylor_queries(nc, g, (wp, bp, select), QK, fac, kv2, kv_half, kv1, kv0, X, XN,
                           (1, KEYS_GROUPS, NG + 2 - KEYS_GROUPS, halved(KEYS_GROUPS), (table1, dtable1), rows1))
        edges(nc, io, g, 1, *rows1, totals1, firsts1)
        combine(nc, io, g, 1, totals1, firsts1, X)
        if dbg is not None:
            dump(nc, X, dbg)

        with ExitStack() as part:
            HT = sb("HT_f1", [P, HALF, NP], to=part)
            gates = sb("gates1", [P, NT, R], to=part)
            wr, br = sb("wr1", [P, HALF, R], to=part), sb("br1", [1, R], to=part)
            ws = [sb(f"e3_w{n}", [P, R, HALF, D], to=part) for n in range(3)]
            cols = sb("e3_cols", [P, 2, 5, R * HALF], to=part)
            bo = sb("e3_bo", [1, R * D], to=part)
            norm(nc, "norm4", X, XN, HT, g["ident"],
                 ahead=[(wr[:, :, :], halves("wr1")), (br[:, :], io["br1"]), (cols[:, :, :, :], io["e3_cols"]), (bo[:, :], io["e3_bo"])]
                 + [(w[:, e, :, :], halves(f"e3_w{n}", e)) for n, w in enumerate(ws) for e in range(R)])
            route(nc, g, HT, wr, br, gates, False, iota8)
            experts3(nc, g, X, HT, gates, ws, cols, bo)
        dump(nc, X, out)


def dump(nc, X, out):
    with Phase(nc, f"dump{out.name if 0 else nc.next_id()}") as ph:
        saved = ph.sem("saved")
        block = ph.open()

        @block.sync
        def _(sp):
            full = (NT - 1) * P
            sp.dma_start(out[0:full, :].rearrange("(t p) f -> p t f", p=P), X[:, 0:NT - 1, :]).then_inc(saved, 16)
            sp.dma_start(out[full:N, :], X[0:LAST, NT - 1, :]).then_inc(saved, 16)
            sp.wait_ge(saved, 32)


def kernel(**inputs):
    import concourse.bacc as _bacc
    from concourse.bass_utils import run_bass_kernel_spmd as _run

    nc = _bacc.Bacc("TRN2", target_bir_lowering=False, num_devices=1)
    arrays, io = {}, {}

    def give(name, a, dtype=None):
        a = np.ascontiguousarray(a)
        arrays["in_" + name] = a
        io[name] = nc.dram_tensor("in_" + name, a.shape, mybir.dt.from_np(a.dtype), kind="ExternalInput").ap()

    def pad(a, rows):
        return np.concatenate([a, np.zeros((rows - a.shape[0],) + a.shape[1:], a.dtype)])

    i = {k: np.asarray(v) for k, v in inputs.items()}
    give("x", pad(i["x"], NP))
    src, dst, typ = i["src"], i["dst"], i["edge_type_8"]
    tiles = dst.reshape(ET, EP)
    give("src_c", src.reshape(ET, EP).T)
    give("dst_c", tiles.T)
    give("type_c", typ.reshape(ET, EP).T)
    nxt = np.full((ET, EP), -1, dst.dtype)
    nxt[:, :-1] = tiles[:, 1:]
    give("next_c", nxt.T)
    give("first_c", np.broadcast_to(tiles[:, 0], (EP, ET)))
    give("dst_row", pad(dst, E + 2 * GE)[None, :])
    by_head = np.broadcast_to(tiles.reshape(NG, GT, 1, EP), (NG, GT, H, EP)).reshape(NG, GT * H, EP)
    give("dst_x", pad(by_head, NG + 2))
    attr = np.ones((4, E + 2 * GE), np.float32)
    attr[:3, :E] = i["edge_attr_3"].T
    attr[:3, E:] = 0
    give("attr", attr)
    give("enc_w", np.concatenate([i["L0_gnn_edge_W"].T, i["L0_gnn_edge_b"][None]]))
    lead = tiles[:, 0]
    before = np.concatenate([np.array([-1], dst.dtype), lead[:-1]])
    give("dst_f", lead.reshape(FT, FQ).T)
    give("prev_f", before.reshape(FT, FQ).T)
    give("dst_fx", np.broadcast_to(lead, (H, ET)))
    give("prev_fx", np.broadcast_to(before, (H, ET)))
    give("iota", np.arange(NP, dtype=np.float32)[None, :])
    give("ident", np.eye(P, dtype=np.float32))
    give("blocks", (np.arange(P)[:, None] // DH == np.arange(P) // DH).astype(np.float32))
    give("headmask", (np.arange(D).reshape(HALF, P).T[:, :, None] // DH == np.arange(H)).astype(np.float32))
    give("gnn_bias", i["L0_gnn_bias"][None, :])

    def columns(a, parts):
        return np.swapaxes(a.reshape(a.shape[:-1] + (parts, P)), -1, -2)

    lnp = np.stack([columns(i["L0_mix_" + n], HALF) for n in ("ln1_g", "ln1_b", "ln2_g", "ln2_b")], 2)
    give("mix_ln", lnp)
    for n in ("Wq", "Wk", "Wv", "Wo", "W1", "W2", "bo"):
        give(n.lower(), i["L0_mix_" + n])
    give("mix_b1", columns(i["L0_mix_b1"], FC))
    give("mix_b2", i["L0_mix_b2"])

    give("wr0", i["L0_ffn_Wr"])
    give("br0", i["L0_ffn_br"][None])
    give("wr1", i["L1_ffn_Wr"])
    give("br1", i["L1_ffn_br"][None])
    give("moe_w1", i["L0_ffn_W1"])
    give("moe_w2", i["L0_ffn_W2"])
    give("moe_b1", columns(i["L0_ffn_b1"], FC))
    give("moe_b2", i["L0_ffn_b2"][:, None])
    give("moe_g", columns(i["L0_ffn_ln_g"], HALF))
    give("moe_b", columns(i["L0_ffn_ln_b"], HALF))
    give("wqkv", i["L1_mix_Wqkv"].T)
    give("bqkv", i["L1_mix_bqkv"][None])
    give("temp", i["L1_mix_temperature"].reshape(1, H))
    give("valid", (np.arange(NP).reshape(NT, P).T < N).astype(np.float32))
    give("wproj", i["L1_mix_Wproj"].T)
    give("bproj", i["L1_mix_bproj"][None])
    row = np.arange(P)
    takes = [(row % DH + c * (P // DH) + row // DH) % DH for c in range(PAIRS)] + [row % DH]
    feature = np.arange(SPLIT * DH)[:, None] % DH
    give("select", np.stack([feature == n for n in takes], 1).astype(np.float32))
    once = np.where(row < DH, 0.5, 1.0) / N
    give("pair_scale", np.stack([once, np.full(P, 1.0 / N)], 1).astype(np.float32))
    give("half_mask", ((row[:, None] // OFFSETS == np.arange(H)) / N).astype(np.float32))
    for n, name in enumerate(("W1", "W2", "Wo")):
        give(f"e3_w{n}", i["L1_ffn_" + name])
    cols = np.stack([np.stack([i[f"L1_ffn_{n}{layer}"] for n in ("b", "g", "be", "m", "v")]) for layer in (1, 2)])
    give("e3_cols", cols.reshape(2, 5, R, HALF, P).transpose(4, 0, 1, 2, 3).reshape(P, 2, 5, R * HALF))
    give("e3_bo", i["L1_ffn_bo"].reshape(1, R * D))

    def with_scores(w):
        w = w.reshape(-1, H, DH, D).transpose(0, 3, 1, 2)
        full = np.zeros((w.shape[0], D, ROW), np.float32)
        full[:, :, :MSG].reshape(w.shape[0], D, H, HW)[:, :, :, :DH] = w
        return full

    for layer, w, names in ((0, i["L0_gnn_W"][None], ("L0_gnn_a_src", "L0_gnn_a_dst")),
                            (1, i["L1_gnn_W"], ("L1_gnn_attn_src", "L1_gnn_attn_dst"))):
        give(f"gnn_w{layer}", w)
        give(f"gnn_wt{layer}", with_scores(w))
        give(f"a{layer}", np.stack([i[n].reshape(HALF, P).T for n in names], 1))

    out = nc.dram_tensor("out_0", (N, D), F32, kind="ExternalOutput").ap()
    dbg = nc.dram_tensor("dbg", (N, D), F32, kind="ExternalOutput").ap() if DEBUG else None
    build(nc, io, out, dbg=dbg)
    r = _run(nc, [arrays], core_ids=[0])
    return r.results[0]["out_0"]


DEBUG = False
```

```python
from contextlib import ExitStack

import numpy as np

import concourse.bass as bass
from concourse import mybir

F32 = mybir.dt.float32
I32 = mybir.dt.int32
U32 = mybir.dt.uint32
BF16 = mybir.dt.bfloat16
ALU = mybir.AluOpType
ACT = mybir.ActivationFunctionType
X_AXIS = mybir.AxisListType.X

P = 128
N, D = 3125, 256
NT = -(-N // P)
NP = NT * P
LAST = N - (NT - 1) * P
U = 5
NB = NT // U
CH = U * P // 2
H, DH = 8, 32
HALF = D // P

E = 50000
EP = 125
ET = E // EP
GT = 8
NG = ET // GT
GE = GT * EP
HW = DH + 1
MSG = H * HW
ROW = MSG + H
SKIP = 4000
BIG = 1e30
NEG_SLOPE = 0.2
FT = 4
FQ = ET // FT
R = 8
SPLIT = 3
SLOTS = U


class Phase:

    def __init__(self, nc, name):
        self.nc, self.name, self.sems, self.ctx = nc, name, [], ExitStack()

    def sb(self, name, shape, dtype=F32):
        return self.ctx.enter_context(self.nc.sbuf_tensor(f"{self.name}_{name}", shape, dtype))

    def ps(self, name, shape):
        return self.ctx.enter_context(self.nc.psum_tensor(f"{self.name}_ps_{name}", shape, F32))

    def sem(self, name):
        self.sems.append(self.ctx.enter_context(self.nc.semaphore(f"{self.name}_{name}")))
        return self.sems[-1]

    def open(self):
        self.inner = ExitStack()
        return self.inner.enter_context(self.nc.Block())

    def __enter__(self):
        return self

    def __exit__(self, *error):
        if error[0] is None:
            self.inner.close()
            for s in self.sems:
                self.nc.sync.sem_clear(s)
            self.nc.all_engine_barrier()
            self.ctx.close()


def gate(eng, sem, value, passed):
    eng.wait_ge(sem, value)
    eng.sem_inc(passed, 1)


def load_ahead(block, loaded, ahead):
    if ahead:
        @block.sync
        def _(sp):
            for out, in_ in ahead:
                sp.dma_start(out, in_).then_inc(loaded, 16)
            sp.wait_ge(loaded, 16 * len(ahead))


def gather_ahead(ph, block, g, job, loaded, ahead):
    layer, n0, count, used, tables, rows = job
    tiles = count * GT
    at = ph.sb("gather_at", [EP, 2, tiles], I32)
    got_rows = [[ph.sb(f"gathered{side}{b}", [EP, GT, tables[side].shape[1]]) for b in range(2)] for side in range(2)]
    s_at, s_passed = ph.sem("gather_at"), ph.sem("gather_passed")
    s_got = g[f"got{layer}"]
    s_saved = [[ph.sem(f"saved{side}{b}") for b in range(2)] for side in range(2)]

    @block.gpsimd
    def _(pool):
        for side, n in enumerate(("src", "dst")):
            pool.tensor_copy(at[:, side, :], g[f"{n}{layer}"][:, bass.ds(n0 * GT, tiles)]).then_inc(s_at, 1)
        gate(pool, s_at, 2, s_passed)
        for n in range(count):
            for side in range(2):
                if n >= 2:
                    gate(pool, s_saved[side][n % 2], 16 * (n // 2), s_passed)
                for c in range(GT):
                    pool.indirect_dma_start(got_rows[side][n % 2][:, c, :], None, tables[side],
                                            bass.IndirectOffsetOnAxis(ap=at[:, side, n * GT + c:n * GT + c + 1], axis=0)
                                            ).then_inc(s_got[side][n % 2], 16)

    @block.sync
    def _(sp):
        for out, in_ in ahead:
            sp.dma_start(out, in_).then_inc(loaded, 16)
        for n in range(count):
            for side in range(2):
                gate(sp, s_got[side][n % 2], (used[n % 2] + (n // 2 + 1)) * (16 * GT), s_passed)
                sp.dma_start(rows[side][bass.ds((n0 + n) * GE, GE), :].rearrange("(c e) w -> e c w", e=EP),
                             got_rows[side][n % 2][:, :, :]).then_inc(s_saved[side][n % 2], 16)
        for side in range(2):
            for b in range(2):
                sp.wait_ge(s_saved[side][b], 16 * ((count + 1 - b) // 2))
        if ahead:
            sp.wait_ge(loaded, 16 * len(ahead))


def norm(nc, name, src, rows, turned, ident, gain=None, bias=None, ahead=()):
    with Phase(nc, name) as ph:
        stats = ph.sb("stats", [P, NT, 6])
        mv = ph.sb("mv", [P, NT, 2])
        var_eps = ph.sb("var_eps", [P, NT])
        std = ph.sb("std", [P, NT])
        rstd = ph.sb("rstd", [P, NT])
        pt = ph.ps("pt", [P, SLOTS, 512])
        s_stats, s_mv, s_var = ph.sem("stats"), ph.sem("mv"), ph.sem("var")
        s_std, s_rstd, s_rows = ph.sem("std"), ph.sem("rstd"), ph.sem("rows")
        s_turned, s_free, s_ahead = ph.sem("turned"), ph.sem("free"), ph.sem("ahead")
        parts = [(0, U), (U, 3 * U), (3 * U, NT)]
        block = ph.open()
        load_ahead(block, s_ahead, ahead)

        @block.vector
        def _(v):
            def statistics(t0, t1):
                for t in range(t0, t1):
                    v.bn_stats(stats[:, t, :], src[:, t, :]).then_inc(s_stats, 1)
                v.wait_ge(s_stats, t1)
                for t in range(t0, t1):
                    v.bn_aggr(mv[:, t, :], stats[:, t, :]).then_inc(s_mv, 1)
                v.wait_ge(s_mv, t1)
                v.tensor_scalar(var_eps[:, t0:t1], mv[:, t0:t1, 1], 1e-5, None, ALU.add).then_inc(s_var, 1)

            def normalised(n, t0, t1):
                v.wait_ge(s_std, n + 1)
                v.reciprocal(rstd[:, t0:t1], std[:, t0:t1]).then_inc(s_rstd, 1)
                v.wait_ge(s_rstd, n + 1)
                for t in range(t0, t1):
                    v.tensor_scalar(rows[:, t, :], src[:, t, :], mv[:, t, 0:1], rstd[:, t:t + 1],
                                    ALU.subtract, ALU.mult).then_inc(s_rows, 1)

            statistics(*parts[0])
            for n, part in enumerate(parts):
                if n + 1 < len(parts):
                    statistics(*parts[n + 1])
                normalised(n, *part)

        @block.tensor
        def _(pe):
            for t in range(NT):
                pe.wait_ge(s_rows, t + 1)
                pe.wait_ge(s_free, t + 1)
                for a in range(HALF):
                    mm = pe.transpose(pt[:, t % SLOTS, a * P:(a + 1) * P], rows[:, t, a * P:(a + 1) * P], ident[:, :])
                mm.then_inc(s_turned, 1)

        @block.scalar
        def _(act):
            act.sem_inc(s_free, SLOTS)
            def roots(n):
                t0, t1 = parts[n]
                act.wait_ge(s_var, n + 1)
                act.activation(std[:, t0:t1], var_eps[:, t0:t1], ACT.Sqrt).then_inc(s_std, 1)

            def turned_out(k0, k1):
                with act.Fori(k0, k1) as k:
                    for j in range(U):
                        act.wait_ge(s_turned, k * U + j + 1)
                        at = bass.ds(k * (U * P) + j * P, P)
                        if gain is None:
                            last = act.activation(turned[:, :, at], pt[:, j, 0:D].rearrange("p (a n) -> p a n", a=HALF), ACT.Copy)
                        else:
                            for a in range(HALF):
                                last = act.activation(turned[:, a, at], pt[:, j, a * P:(a + 1) * P], ACT.Identity,
                                                      bias=bias[:, a:a + 1], scale=gain[:, a:a + 1])
                        last.then_inc(s_free, 1)

            roots(0)
            roots(1)
            turned_out(0, 1)
            roots(2)
            turned_out(1, NB)


def edge_prep(nc, io, g, more):
    with Phase(nc, "prep") as ph:
        srcc = ph.sb("src", [EP, ET], I32)
        typec = ph.sb("type", [EP, ET], I32)
        nextc = ph.sb("next", [EP, ET], I32)
        firstc = ph.sb("first", [EP, ET], I32)
        base = ph.sb("base", [EP, ET])
        ends = ph.sb("ends", [EP, ET])
        inner = ph.sb("inner", [EP, ET])
        s_in, s_v = ph.sem("in"), ph.sem("v")
        block = ph.open()
        loads = [(g["dst"][:, :], io["dst_c"]), (srcc[:, :], io["src_c"]), (typec[:, :], io["type_c"]),
                 (nextc[:, :], io["next_c"]), (firstc[:, :], io["first_c"]), (g["ident"][:, :], io["ident"]),
                 (g["blocks"][:, :], io["blocks"])] + more

        @block.sync
        def _(sp):
            for out, in_ in loads:
                sp.dma_start(out, in_).then_inc(s_in, 16)

        @block.vector
        def _(v):
            v.wait_ge(s_in, 16 * len(loads))
            for n in ("src0", "dst0", "src1", "dst1", "put"):
                v.memset(g[n][:, :], 0).then_inc(s_v, 1)
            v.tensor_scalar(base[:, :], typec[:, :], float(NP), None, ALU.mult).then_inc(s_v, 1)
            v.tensor_tensor(ends[:, :], g["dst"][:, :], nextc[:, :], ALU.not_equal).then_inc(s_v, 1)
            v.tensor_tensor(inner[:, :], g["dst"][:, :], firstc[:, :], ALU.not_equal).then_inc(s_v, 1)
            v.wait_ge(s_v, 8)
            v.tensor_copy(g["src0"][:, 0:ET], srcc[:, :]).then_inc(s_v, 1)
            v.tensor_copy(g["dst0"][:, 0:ET], g["dst"][:, :]).then_inc(s_v, 1)
            v.tensor_tensor(g["src1"][:, 0:ET], base[:, :], srcc[:, :], ALU.add).then_inc(s_v, 1)
            v.tensor_tensor(g["dst1"][:, 0:ET], base[:, :], g["dst"][:, :], ALU.add).then_inc(s_v, 1)
            v.tensor_tensor(ends[:, :], ends[:, :], inner[:, :], ALU.mult).then_inc(s_v, 1)
            v.wait_ge(s_v, 13)
            v.scalar_tensor_tensor(inner[:, :], g["dst"][:, :], -float(SKIP), ends[:, :],
                                   ALU.add, ALU.mult).then_inc(s_v, 1)
            v.wait_ge(s_v, 14)
            v.tensor_scalar(g["put"][:, 0:ET], inner[:, :], float(SKIP), None, ALU.add).then_inc(s_v, 1)


def gnn_table(nc, io, g, layer, turned, table, dtable):
    rel = R if layer else 1
    with Phase(nc, f"table{layer}") as ph:
        wo = ph.sb("wo", [P, 2, HALF, D])
        wt = ph.sb("wt", [P, 2, HALF, ROW])
        acol = ph.sb("acol", [P, 2, HALF])
        mask = ph.sb("mask", [P, HALF, H])
        ablk = ph.sb("ablk", [P, HALF, 2, H])
        rows = ph.sb("rows", [P, NB, U, ROW])
        pa = ph.ps("pa", [P, HALF, 512])
        ph_ = ph.ps("ph", [P, SLOTS, 512])
        s_w = [ph.sem(f"w{b}") for b in range(2)]
        s_c, s_ab, s_pa, s_wt = ph.sem("c"), ph.sem("ab"), ph.sem("pa"), ph.sem("wt")
        s_h, s_rows = ph.sem("h"), ph.sem("rows")
        s_saved = [ph.sem(f"saved{k}") for k in range(NB)]
        block = ph.open()
        per_store = 1 if dtable is None else 2

        def store(sp, r):
            for k in range(NB):
                sp.wait_ge(s_rows, SLOTS + r * NT + (k + 1) * U)
                at = slice(r * NP + k * U * P, r * NP + (k + 1) * U * P)
                sp.dma_start(table[at, :].rearrange("(t p) w -> p t w", p=P), rows[:, k, :, :]).then_inc(s_saved[k], 16)
                if dtable is not None:
                    sp.dma_start(dtable[at, :].rearrange("(t p) w -> p t w", p=P),
                                 rows[:, k, :, MSG:ROW]).then_inc(s_saved[k], 16)

        @block.sync
        def _(sp):
            sp.dma_start(acol[:, :, :], io[f"a{layer}"]).then_inc(s_c, 16)
            sp.dma_start(mask[:, :, :], io["headmask"]).then_inc(s_c, 16)
            for k in range(NB):
                sp.sem_inc(s_saved[k], 16 * per_store)
            for r in range(rel):
                if r >= 2:
                    sp.wait_ge(s_h, NT * (r - 1))
                sp.dma_start(wo[:, r % 2, :, :], io[f"gnn_w{layer}"][r].rearrange("(a p) i -> p a i", p=P)).then_inc(s_w[r % 2], 16)
                sp.dma_start(wt[:, r % 2, :, :], io[f"gnn_wt{layer}"][r].rearrange("(a p) o -> p a o", p=P)).then_inc(s_w[r % 2], 16)
                if r:
                    store(sp, r - 1)
            store(sp, rel - 1)
            for k in range(NB):
                sp.wait_ge(s_saved[k], 16 * per_store * (rel + 1))

        @block.vector
        def _(v):
            v.wait_ge(s_c, 32)
            for s in range(2):
                for a in range(HALF):
                    v.tensor_scalar(ablk[:, a, s, :], mask[:, a, :], acol[:, s, a:a + 1], None,
                                    ALU.mult).then_inc(s_ab, 1)
            for r in range(rel):
                v.wait_ge(s_w[r % 2], 32 * (r // 2 + 1))
                v.wait_ge(s_pa, r + 1)
                for a in range(HALF):
                    v.tensor_copy(wt[:, r % 2, a, 0:MSG].rearrange("p (h w) -> p h w", w=HW)[:, :, DH],
                                  pa[:, a, 0:H]).then_inc(s_wt, 1)
                    v.tensor_copy(wt[:, r % 2, a, MSG:ROW], pa[:, a, H:2 * H]).then_inc(s_wt, 1)

        @block.tensor
        def _(pe):
            pe.wait_ge(s_ab, 2 * HALF)
            for r in range(rel):
                pe.wait_ge(s_w[r % 2], 32 * (r // 2 + 1))
                if r:
                    pe.wait_ge(s_wt, 4 * r)
                for a in range(HALF):
                    for o in range(HALF):
                        mm = pe.matmul(pa[:, a, 0:2 * H], wo[:, r % 2, o, a * P:(a + 1) * P],
                                       ablk[:, o, :, :].rearrange("p s h -> p (s h)"),
                                       start=(o == 0), stop=(o == HALF - 1))
                mm.then_inc(s_pa, 1)
                pe.wait_ge(s_wt, 4 * (r + 1))
                for t in range(NT):
                    pe.wait_ge(s_rows, r * NT + t + 1)
                    for a in range(HALF):
                        mm = pe.matmul(ph_[:, t % SLOTS, 0:ROW], turned[:, a, t * P:(t + 1) * P],
                                       wt[:, r % 2, a, :], start=(a == 0), stop=(a == HALF - 1))
                    mm.then_inc(s_h, 1)

        @block.scalar
        def _(act):
            act.sem_inc(s_rows, SLOTS)
            with act.Fori(0, rel) as r:
                for k in range(NB):
                    act.wait_ge(s_saved[k], r * (16 * per_store) + 16 * per_store)
                    for j in range(U):
                        act.wait_ge(s_h, r * NT + (k * U + j + 1))
                        act.activation(rows[:, k, j, :], ph_[:, j, 0:ROW], ACT.Copy).then_inc(s_rows, 1)



SLOTS_O = 4


def edges(nc, io, g, layer, src_rows, dst_rows, totals, firsts):
    encoded = layer == 0
    dw = ROW if encoded else H
    with Phase(nc, f"edges{layer}") as ph:
        Gs = [ph.sb(f"rows_src{b}", [EP, GT, ROW]) for b in range(2)]
        Gd = [ph.sb(f"rows_dst{b}", [EP, GT, dw]) for b in range(2)]
        msg = [ph.sb(f"msg{b}", [EP, GT, MSG]) for b in range(2)]
        maxima = [ph.sb(f"maxima{b}", [EP, GT, H]) for b in range(2)]
        O = [ph.sb(f"out{b}", [EP, GT, ROW]) for b in range(2)]
        same = [ph.sb(f"same{b}", [EP, GT, EP]) for b in range(2)]
        dstb = [ph.sb(f"dstb{b}", [EP, GT, EP], I32) for b in range(2)]
        dstx = [ph.sb(f"dstx{b}", [GT * H, EP], I32) for b in range(2)]
        slot_o = [ph.sb(f"slot_o{b}", [EP, GT], I32) for b in range(2)]
        blank = ph.sb("blank", [P, ROW])
        pen = ph.sb("pen", [GT * H, EP + 1])
        fwd = ph.sb("fwd", [GT * H, EP])
        bwd = ph.sb("bwd", [GT * H, EP])
        top = ph.sb("top", [GT * H, EP])
        alpha = ph.sb("alpha", [EP, GT, H])
        alpha0 = ph.sb("alpha0", [EP, GT, H])
        below = ph.sb("below", [EP, GT, H])
        p_t = ph.ps("p_t", [P, 512])
        p_m = ph.ps("p_m", [P, 512])
        p_o = ph.ps("p_o", [P, SLOTS_O, 512])
        if encoded:
            attr = [ph.sb(f"attr{b}", [4, GE]) for b in range(2)]
            enc_w = ph.sb("enc_w", [4, D])
            enc = ph.sb("enc", [EP, GT // 2, 2, D])
            dot = ph.sb("dot", [EP, GT, H])
            p_e = ph.ps("p_e", [P, 2, 2, D])
        s_blank, s_clear, s_w = ph.sem("blank"), ph.sem("clear"), ph.sem("w")
        s_chunk = [ph.sem(f"chunk{b}") for b in range(2)]
        s_used = [ph.sem(f"used{b}") for b in range(2)]
        s_rows = [ph.sem(f"rows{b}") for b in range(2)]
        s_put, s_max = ph.sem("put"), ph.sem("max")
        s_scattered = g[f"scattered{layer}"]
        s_ofree = [ph.sem(f"ofree{b}") for b in range(2)]
        s_firsts = [ph.sem(f"firsts{b}") for b in range(2)]
        s_passed, s_pe, s_penc = ph.sem("passed"), ph.sem("pe"), ph.sem("penc")
        s_enc, s_prod, s_encfree = ph.sem("enc"), ph.sem("prod"), ph.sem("encfree")
        s_chain, s_alpha, s_aT, s_top, s_mT = ph.sem("chain"), ph.sem("alpha"), ph.sem("aT"), ph.sem("top"), ph.sem("mT")
        s_below, s_exp, s_msg, s_same = ph.sem("below"), ph.sem("exp"), ph.sem("msg"), ph.sem("same")
        s_scan = ph.sem("scan")
        s_sum, s_out, s_pen, s_mcopy = ph.sem("sum"), ph.sem("out"), ph.sem("pen"), ph.sem("mcopy")
        block = ph.open()

        def score(b):
            return Gs[b][:, :, 0:MSG].rearrange("p c (h w) -> p c h w", w=HW)[:, :, :, DH]

        def groups(eng, body):
            body(0, 0, 0, False, True)
            with eng.Fori(0, NG // 2 - 1) as k:
                body(k * 2 + 1, k, 1, True, True)
                body(k * 2 + 2, k + 1, 0, True, True)
            body(NG - 1, NG // 2 - 1, 1, True, False)

        def score(b):
            return Gs[b][:, :, 0:MSG].rearrange("p c (h w) -> p c h w", w=HW)[:, :, :, DH]

        loads = 3 if encoded else 2

        def load_chunk(sp, n, b):
            sp.dma_start(dstb[b][:, :, :].rearrange("p c e -> p (c e)"),
                         io["dst_row"][:, bass.ds(n * GE, GE)].partition_broadcast(EP)).then_inc(s_chunk[b], 16)
            sp.dma_start(dstx[b][:, :], io["dst_x"][n]).then_inc(s_chunk[b], 16)
            if encoded:
                sp.dma_start(attr[b][:, :], io["attr"][:, bass.ds(n * GE, GE)]).then_inc(s_chunk[b], 16)

        def load_rows(sp, n, b):
            for to, rows in ((Gs[b], src_rows), (Gd[b], dst_rows)):
                sp.dma_start(to[:, :, :], rows[bass.ds(n * GE, GE), :].rearrange("(c e) w -> e c w", e=EP)).then_inc(s_rows[b], 16)

        @block.sync
        def _(sp):
            if encoded:
                sp.dma_start(enc_w[:, :], io["enc_w"]).then_inc(s_w, 16)
            for b in range(2):
                sp.sem_inc(s_ofree[b], 1)
                load_chunk(sp, b, b)
                load_rows(sp, b, b)
            sp.wait_ge(s_blank, 2)
            sp.dma_start(totals.rearrange("(t p) w -> p t w", p=P),
                         blank[:, None, :].to_broadcast([P, NT, ROW])).then_inc(s_clear, 16)
            def firsts_out(n, b):
                gate(sp, s_out, n * GT + (SLOTS_O + GT), s_passed)
                gate(sp, s_max, n + 3, s_passed)
                sp.dma_start(firsts[bass.ds(n * GT, GT), :].rearrange("(a t) w -> a t w", a=1),
                             O[b][0:1, :, :]).then_inc(s_firsts[b], 16)

            def group(n, k, b, before, after):
                gate(sp, s_used[b], 2 * (k + 1), s_passed)
                if encoded:
                    gate(sp, s_enc, n * (GT // 2) + (2 + GT // 2), s_passed)
                load_chunk(sp, n + 2, b)
                gate(sp, s_msg, n + 1, s_passed)
                load_rows(sp, n + 2, b)
                if before:
                    firsts_out(n - 1, 1 - b)

            groups(sp, group)
            firsts_out(NG - 1, 1)
            for b in range(2):
                sp.wait_ge(s_chunk[b], 16 * loads * (NG // 2 + 1))
                sp.wait_ge(s_rows[b], 32 * (NG // 2 + 1))

        @block.gpsimd
        def _(pool):
            pool.memset(blank[:, 0:MSG], 0.0).then_inc(s_blank, 1)
            pool.memset(blank[:, MSG:ROW], -BIG).then_inc(s_blank, 1)

            def release(k, b):
                gate(pool, s_scattered[b], 16 * GT * (k + 1), s_passed)
                gate(pool, s_firsts[b], 16 * (k + 1), s_passed)
                pool.sem_inc(s_ofree[b], 1)

            def group(n, k, b, before, after):
                pool.tensor_copy(slot_o[b][:, :], g["put"][:, bass.ds(n * GT, GT)]).then_inc(s_put, 1)
                gate(pool, s_put, n + 1, s_passed)
                gate(pool, s_out, n * GT + (SLOTS_O + GT), s_passed)
                gate(pool, s_max, n + 3, s_passed)
                for c in range(GT):
                    pool.indirect_dma_start(totals, bass.IndirectOffsetOnAxis(ap=slot_o[b][:, c:c + 1], axis=0),
                                            O[b][:, c, :], None, bounds_check=NP - 1,
                                            oob_is_err=False).then_inc(s_scattered[b], 16)
                if before:
                    release(k if b else k - 1, 1 - b)

            pool.wait_ge(s_clear, 16)
            groups(pool, group)
            release(NG // 2 - 1, 1)

        @block.tensor
        def _(pe):
            def encode(n, k, b):
                pe.wait_ge(s_chunk[b], 16 * loads * (k + 1))
                for q in range(GT // 2):
                    pe.wait_ge(s_enc, n * (GT // 2) + (q + 1))
                    for c in range(2):
                        mm = pe.matmul(p_e[0:EP, q % 2, c, :], attr[b][:, (2 * q + c) * EP:(2 * q + c + 1) * EP],
                                       enc_w[:, :], start=True, stop=True)
                    mm.then_inc(s_penc, 1)

            def sums(n, b):
                pe.wait_ge(s_msg, n + 1)
                for c in range(GT):
                    pe.wait_ge(s_out, n * GT + (c + 1))
                    pe.matmul(p_o[0:EP, c % SLOTS_O, 0:MSG], same[b][:, c, :], msg[b][:, c, :],
                              start=True, stop=True).then_inc(s_sum, 1)

            def group(n, k, b, before, after):
                gate(pe, s_alpha, n + 1, s_passed)
                pe.transpose(p_t[0:GT * H, 0:EP], alpha[:, :, :].rearrange("p c h -> p (c h)"),
                             g["ident"][0:EP, 0:EP]).then_inc(s_aT, 1)
                gate(pe, s_top, n + 2, s_passed)
                gate(pe, s_mcopy, n + 1, s_passed)
                gate(pe, s_below, n + 1, s_passed)
                pe.transpose(p_m[0:EP, 0:GT * H], top[:, :], g["ident"][0:GT * H, 0:GT * H]).then_inc(s_mT, 1)
                if encoded and after:
                    encode(n + 1, k + b, 1 - b)
                if before:
                    sums(n - 1, 1 - b)

            pe.sem_inc(s_sum, 2 * GT)
            if encoded:
                pe.wait_ge(s_w, 16)
                encode(0, 0, 0)
            groups(pe, group)
            sums(NG - 1, 1)

        @block.scalar
        def _(act):
            def encoded_out(n):
                for q in range(GT // 2):
                    act.wait_ge(s_penc, n * (GT // 2) + (q + 1))
                    act.wait_ge(s_encfree, n * (GT // 2) + (q + 1))
                    act.activation(enc[:, q, :, :], p_e[0:EP, q % 2, :, :], ACT.Relu).then_inc(s_enc, 1)

            def out(n, k, b):
                act.wait_ge(s_ofree[b], k + 1)
                act.wait_ge(s_mcopy, n + 2)
                act.activation(O[b][:, :, MSG:ROW], maxima[b][:, :, :], ACT.Copy).then_inc(s_max, 1)
                for c in range(GT):
                    act.wait_ge(s_sum, n * GT + (2 * GT + c + 1))
                    act.activation(O[b][:, c, 0:MSG], p_o[0:EP, c % SLOTS_O, 0:MSG], ACT.Copy).then_inc(s_out, 1)

            def group(n, k, b, before, after):
                act.wait_ge(s_sum, n * GT + GT)
                act.wait_ge(s_below, n + 2)
                act.activation(msg[b][:, :, :].rearrange("p c (h w) -> p c h w", w=HW)[:, :, :, DH], below[:, :, :],
                               ACT.Exp).then_inc(s_exp, 1)
                act.wait_ge(s_max, n + 1)
                act.activation(maxima[b][:, :, :], p_m[0:EP, 0:GT * H].rearrange("p (c h) -> p c h", h=H),
                               ACT.Copy).then_inc(s_mcopy, 1)
                if encoded and after:
                    encoded_out(n + 1)
                if before:
                    out(n - 1, k if b else k - 1, 1 - b)

            act.sem_inc(s_out, SLOTS_O)
            act.sem_inc(s_enc, 2)
            act.sem_inc(s_mcopy, 1)
            act.sem_inc(s_max, 2)
            if encoded:
                encoded_out(0)
            groups(act, group)
            out(NG - 1, NG // 2 - 1, 1)

        @block.vector
        def _(v):
            def same_dst(n, k, b):
                v.wait_ge(s_chunk[b], 16 * loads * (k + 1))
                v.wait_ge(s_sum, n * GT + GT)
                v.tensor_tensor(same[b][:, :, :], dstb[b][:, :, :],
                                g["dst"][:, bass.ds(n * GT, GT)][:, :, None].to_broadcast([EP, GT, EP]),
                                ALU.is_equal).then_inc(s_used[b], 1)

            def borders(n, k, b):
                v.wait_ge(s_chunk[b], 16 * loads * (k + 1))
                v.wait_ge(s_top, n + 1)
                v.tensor_tensor(pen[:, 1:EP], dstx[b][:, 1:EP], dstx[b][:, 0:EP - 1],
                                ALU.not_equal).then_inc(s_used[b], 1)
                v.wait_ge(s_used[b], 2 * k + 1)
                v.tensor_scalar(pen[:, 1:EP], pen[:, 1:EP], -BIG, None, ALU.mult).then_inc(s_pen, 1)

            def group(n, k, b, before, after):
                v.wait_ge(s_rows[b], 32 * (k + 1))
                if encoded:
                    v.tensor_tensor(alpha0[:, :, :], score(b), Gd[b][:, :, MSG:ROW], ALU.add).then_inc(s_chain, 1)
                    for q in range(GT // 2):
                        v.wait_ge(s_enc, n * (GT // 2) + (q + 3))
                        e4 = enc[:, q, :, :].rearrange("p c (h w) -> p c h w", w=DH)
                        for c in range(2):
                            v.tensor_tensor(e4[:, c], e4[:, c],
                                            Gd[b][:, 2 * q + c, 0:MSG].rearrange("p (h w) -> p h w", w=HW)[:, :, 0:DH],
                                            ALU.mult).then_inc(s_prod, 1)
                        if q:
                            v.wait_ge(s_prod, n * GT + 2 * q)
                            dots(q - 1)
                    v.wait_ge(s_prod, n * GT + GT)
                    dots(GT // 2 - 1)
                    v.wait_ge(s_encfree, n * (GT // 2) + GT)
                    v.wait_ge(s_chain, n * 2 + 1)
                    v.tensor_tensor(alpha0[:, :, :], alpha0[:, :, :], dot[:, :, :], ALU.add).then_inc(s_chain, 1)
                    v.wait_ge(s_chain, n * 2 + 2)
                else:
                    v.tensor_tensor(alpha0[:, :, :], score(b), Gd[b][:, :, :], ALU.add).then_inc(s_chain, 1)
                    v.wait_ge(s_chain, n + 1)
                v.wait_ge(s_below, n + 1)
                v.scalar_tensor_tensor(alpha[:, :, :], alpha0[:, :, :], NEG_SLOPE, alpha0[:, :, :],
                                       ALU.mult, ALU.max).then_inc(s_alpha, 1)
                same_dst(n, k, b)
                v.wait_ge(s_aT, n + 1)
                v.wait_ge(s_pen, n + 2)
                v.tensor_tensor_scan(fwd[:, :], pen[:, 0:EP], p_t[0:GT * H, 0:EP], -BIG,
                                     ALU.add, ALU.max).then_inc(s_scan, 1)
                v.tensor_tensor_scan(bwd[:, ::-1], pen[:, 1:EP + 1][:, ::-1], p_t[0:GT * H, 0:EP][:, ::-1], -BIG,
                                     ALU.add, ALU.max).then_inc(s_scan, 1)
                v.wait_ge(s_scan, n * 2 + 2)
                v.tensor_tensor(top[:, :], fwd[:, :], bwd[:, :], ALU.max).then_inc(s_top, 1)
                if after:
                    borders(n + 1, k + b, 1 - b)
                v.wait_ge(s_mT, n + 1)
                v.tensor_tensor(below[:, :, :], alpha[:, :, :], p_m[0:EP, 0:GT * H].rearrange("p (c h) -> p c h", h=H),
                                ALU.subtract).then_inc(s_below, 1)
                v.wait_ge(s_exp, n + 1)
                for c in range(GT):
                    to = msg[b][:, c, :].rearrange("p (h w) -> p h w", w=HW)
                    last = v.tensor_tensor(to[:, :, 0:DH], Gs[b][:, c, 0:MSG].rearrange("p (h w) -> p h w", w=HW)[:, :, 0:DH],
                                           to[:, :, DH:HW].to_broadcast([EP, H, DH]), ALU.mult)
                last.then_inc(s_msg, 1)

            def dots(q):
                v.tensor_reduce(dot[:, 2 * q:2 * q + 2, :], enc[:, q, :, :].rearrange("p c (h w) -> p c h w", w=DH),
                                X_AXIS, ALU.add).then_inc(s_encfree, 1)

            v.memset(pen[:, :], 0.0).then_inc(s_pen, 1)
            v.sem_inc(s_top, 1)
            v.sem_inc(s_below, 1)
            if encoded:
                v.sem_inc(s_encfree, GT // 2)
            v.wait_ge(s_pen, 1)
            borders(0, 0, 0)
            groups(v, group)


def combine(nc, io, g, layer, totals, firsts, X):
    with Phase(nc, f"combine{layer}") as ph:
        fs = ph.sb("fs", [FQ, FT, ROW + 1])
        dstf = ph.sb("dstf", [FQ, FT])
        dstf_i, prev_i = ph.sb("dstf_i", [FQ, FT], I32), ph.sb("prev_i", [FQ, FT], I32)
        dstx_i, prevx_i = ph.sb("dstx_i", [H, ET], I32), ph.sb("prevx_i", [H, ET], I32)
        isfirst = ph.sb("isfirst", [FQ, FT])
        penf = ph.sb("penf", [H, ET + 1])
        iota = ph.sb("iota", [FQ, NP])
        ones = ph.sb("ones", [FQ, FT])
        fwd, bwd, top = ph.sb("fwd", [H, ET]), ph.sb("bwd", [H, ET]), ph.sb("top", [H, ET])
        scale = ph.sb("scale", [FQ, FT, H])
        tab = ph.sb("tab", [P, NT, ROW])
        fs_parts = ph.sb("fs_parts", [FQ, SPLIT, FT, ROW + 1], BF16)
        hot = ph.sb("hot", [FQ, 2, U, FT, P], BF16)
        far = ph.sb("far", [P, U])
        m1, m = ph.sb("m1", [P, U, H]), ph.sb("m", [P, U, H])
        ex = ph.sb("ex", [P, 3, U, H])
        part = ph.sb("part", [P, U, H, HW])
        den, rden = ph.sb("den", [P, U, H]), ph.sb("rden", [P, U, H])
        biasrow = ph.sb("biasrow", [P, D])
        p_t = ph.ps("p_t", [P, 512])
        p_m = ph.ps("p_m", [P, 512])
        p_n = ph.ps("p_n", [P, U, 512])
        s_in, s_mT, s_f, s_scan, s_top, s_back = (ph.sem(x) for x in ("in", "mT", "f", "scan", "top", "back"))
        s_scale, s_exp, s_fs, s_hot, s_sum, s_chain, s_e, s_used = (
            ph.sem(x) for x in ("scale", "exp", "fs", "hot", "sum", "chain", "e", "used"))
        block = ph.open()
        loads = [(fs[:, :, 0:ROW], firsts.rearrange("(b q) w -> q b w", q=FQ)), (dstf_i[:, :], io["dst_f"]),
                 (prev_i[:, :], io["prev_f"]), (dstx_i[:, :], io["dst_fx"]), (prevx_i[:, :], io["prev_fx"]),
                 (iota[:, :], io["iota"].partition_broadcast(FQ)),
                 (tab[:, :, :], totals.rearrange("(t p) w -> p t w", p=P)),
                 (biasrow[:, :], io["gnn_bias"].partition_broadcast(P))]

        @block.sync
        def _(sp):
            for out, in_ in loads:
                sp.dma_start(out, in_).then_inc(s_in, 16)

        @block.tensor
        def _(pe):
            pe.wait_ge(s_in, 16 * len(loads))
            for b in range(FT):
                mm = pe.transpose(p_t[0:H, b * FQ:(b + 1) * FQ], fs[:, b, MSG:ROW], g["ident"][0:FQ, 0:FQ])
            mm.then_inc(s_mT, 1)
            pe.wait_ge(s_top, 1)
            for b in range(FT):
                mm = pe.transpose(p_m[0:FQ, b * H:(b + 1) * H], top[:, b * FQ:(b + 1) * FQ], g["ident"][0:H, 0:H])
            mm.then_inc(s_back, 1)
            pe.wait_ge(s_fs, 1)
            for k in range(NB):
                pe.wait_ge(s_hot, k + 1)
                if k:
                    pe.wait_ge(s_used, k)
                for j in range(U):
                    for s_ in range(SPLIT):
                        for b in range(FT):
                            mm = pe.matmul(p_n[:, j, 0:ROW + 1], hot[:, k % 2, j, b, :], fs_parts[:, s_, b, :],
                                           start=(s_ == 0 and b == 0), stop=(s_ == SPLIT - 1 and b == FT - 1))
                mm.then_inc(s_sum, 1)

        @block.scalar
        def _(act):
            act.wait_ge(s_scale, 1)
            act.activation(scale[:, :, :], scale[:, :, :], ACT.Exp).then_inc(s_exp, 1)
            for k in range(NB):
                act.wait_ge(s_e, k + 1)
                act.activation(ex[:, :, :, :], ex[:, :, :, :], ACT.Exp).then_inc(s_exp, 1)

        @block.vector
        def _(v):
            steps = [0]

            def step(ins):
                steps[0] += 1
                ins.then_inc(s_chain, 1)
                v.wait_ge(s_chain, steps[0])

            v.wait_ge(s_in, 16 * len(loads))
            step(v.memset(ones[:, :], 1.0))
            step(v.tensor_copy(dstf[:, :], dstf_i[:, :]))
            step(v.tensor_tensor(penf[:, 0:ET], dstx_i[:, :], prevx_i[:, :], ALU.not_equal))
            step(v.tensor_scalar(penf[:, 0:ET], penf[:, 0:ET], -BIG, None, ALU.mult))
            step(v.memset(penf[:, ET:ET + 1], 0.0))
            step(v.tensor_tensor(isfirst[:, :], dstf_i[:, :], prev_i[:, :], ALU.not_equal))
            v.wait_ge(s_mT, 1)
            v.tensor_tensor_scan(fwd[:, :], penf[:, 0:ET], p_t[0:H, 0:ET], -BIG, ALU.add, ALU.max).then_inc(s_scan, 1)
            v.tensor_tensor_scan(bwd[:, ::-1], penf[:, 1:ET + 1][:, ::-1], p_t[0:H, 0:ET][:, ::-1], -BIG,
                                 ALU.add, ALU.max).then_inc(s_scan, 1)
            v.wait_ge(s_scan, 2)
            v.tensor_tensor(top[:, :], fwd[:, :], bwd[:, :], ALU.max).then_inc(s_top, 1)
            v.wait_ge(s_back, 1)
            mf = p_m[0:FQ, 0:FT * H].rearrange("p (b h) -> p b h", h=H)
            v.tensor_tensor(scale[:, :, :], fs[:, :, MSG:ROW], mf, ALU.subtract).then_inc(s_scale, 1)
            v.wait_ge(s_scale, 1)
            step(v.tensor_tensor(fs[:, :, MSG:ROW], isfirst[:, :, None].to_broadcast([FQ, FT, H]), mf, ALU.mult))
            step(v.tensor_tensor(fs[:, :, ROW], isfirst[:, :], ones[:, :], ALU.mult))
            v.wait_ge(s_exp, 1)
            for b in range(FT):
                f = fs[:, b, 0:MSG].rearrange("p (h w) -> p h w", w=HW)
                step(v.tensor_tensor(f, f, scale[:, b, :, None].to_broadcast([FQ, H, HW]), ALU.mult))
            for n in range(SPLIT):
                step(v.tensor_copy(fs_parts[:, n, :, :], fs[:, :, :]))
                if n + 1 < SPLIT:
                    step(v.tensor_tensor(fs[:, :, :], fs[:, :, :], fs_parts[:, n, :, :], ALU.subtract))
            v.sem_inc(s_fs, 1)

            def which(k):
                v.wait_ge(s_chain, steps[0])
                for j in range(U):
                    at = slice((k * U + j) * P, (k * U + j + 1) * P)
                    last = v.tensor_tensor(hot[:, k % 2, j, :, :], iota[:, None, at].to_broadcast([FQ, FT, P]),
                                           dstf[:, :, None].to_broadcast([FQ, FT, P]), ALU.is_equal)
                last.then_inc(s_hot, 1)

            def per_head(a):
                return a[:, :, :, None]

            which(0)
            for k in range(NB):
                at = slice(k * U, (k + 1) * U)
                if k + 1 < NB:
                    if k:
                        v.wait_ge(s_sum, k)
                    which(k + 1)
                v.wait_ge(s_sum, k + 1)
                mt = tab[:, at, MSG:ROW]
                tb = tab[:, at, 0:MSG].rearrange("p t (h w) -> p t h w", w=HW)
                step(v.tensor_scalar(far[:, :], p_n[:, :, ROW], BIG, -BIG, ALU.mult, ALU.add))
                step(v.tensor_tensor(m1[:, :, :], p_n[:, :, MSG:ROW], far[:, :, None].to_broadcast([P, U, H]), ALU.add))
                step(v.tensor_tensor(m[:, :, :], m1[:, :, :], mt, ALU.max))
                step(v.tensor_tensor(ex[:, 0, :, :], mt, m[:, :, :], ALU.subtract))
                step(v.tensor_tensor(ex[:, 1, :, :], m1[:, :, :], m[:, :, :], ALU.subtract))
                v.tensor_scalar(ex[:, 2, :, :], m[:, :, :], 0.0, None, ALU.min).then_inc(s_e, 1)
                v.wait_ge(s_exp, k + 2)
                for j in range(U):
                    last = v.tensor_tensor(part[:, j, :, :], p_n[:, j, 0:MSG].rearrange("p (h w) -> p h w", w=HW),
                                           ex[:, 1, j, :, None].to_broadcast([P, H, HW]), ALU.mult)
                last.then_inc(s_used, 1)
                step(v.tensor_tensor(tb, tb, per_head(ex[:, 0, :, :]).to_broadcast([P, U, H, HW]), ALU.mult))
                v.wait_ge(s_used, k + 1)
                step(v.tensor_tensor(part[:, :, :, :], part[:, :, :, :], tb, ALU.add))
                if layer == 0:
                    step(v.tensor_scalar(den[:, :, :], part[:, :, :, DH], 1e-10, None, ALU.max))
                    step(v.reciprocal(rden[:, :, :], den[:, :, :]))
                else:
                    step(v.tensor_tensor(den[:, :, :], part[:, :, :, DH], ex[:, 2, :, :], ALU.mult))
                    step(v.tensor_scalar(den[:, :, :], den[:, :, :], 1e-12, None, ALU.add))
                    step(v.reciprocal(rden[:, :, :], den[:, :, :]))
                    step(v.tensor_tensor(rden[:, :, :], rden[:, :, :], ex[:, 2, :, :], ALU.mult))
                step(v.tensor_tensor(part[:, :, :, 0:DH], part[:, :, :, 0:DH],
                                     per_head(rden[:, :, :]).to_broadcast([P, U, H, DH]), ALU.mult))
                xt = X[:, at, :].rearrange("p t (h w) -> p t h w", w=DH)
                step(v.tensor_tensor(xt, xt, part[:, :, :, 0:DH], ALU.add))
                if layer == 0:
                    step(v.tensor_tensor(X[:, at, :], X[:, at, :], biasrow[:, None, :].to_broadcast([P, U, D]), ALU.add))


DEPTH = 4
FF = 4 * D
FC = FF // P
KB = 10
KW = NP // KB
ATTN_GROUPS, FF_GROUPS = 6, 7


def halved(*counts):
    return [sum((n + 1 - b) // 2 for n in counts) for b in range(2)]


assert DEPTH * (ATTN_GROUPS + FF_GROUPS) == NG + 2
QK_SCALE = float(DH) ** -0.25
A_T, B_T = 2, 3
A_N, B_N = A_T * P, B_T * P


def attention(nc, g, w, S, turned, spare, ahead, job):
    wq, wk, wv, wo, bo = w
    qt = spare[:, :, :].rearrange("p t f -> p (t f)").rearrange("p (a n) -> p a n", a=HALF)
    with Phase(nc, "attn") as ph:
        kmx = ph.sb("kmx", [P, HALF, KB])
        kmax = ph.sb("kmax", [P, HALF])
        krow = ph.sb("krow", [1, D])
        ones = ph.sb("ones", [P, P])
        qmax, qsum, qrec = ph.sb("qmax", [P, 2, H]), ph.sb("qsum", [P, 2, H]), ph.sb("qrec", [P, 2, H])
        qs = ph.sb("qs", [P, 2, H, DH])
        ek = ph.sb("ek", [P, 2, D])
        vs = ph.sb("vs", [P, 2, D])
        ctx = ph.sb("ctx", [P, HALF, P])
        rk = ph.sb("rk", [P, HALF])
        M = ph.sb("M", [P, HALF, D])
        p_q = ph.ps("q", [P, 2, 512])
        p_kv = ph.ps("kv", [P, 2, 512])
        p_t = ph.ps("t", [P, 2, 512])
        p_c = ph.ps("c", [P, 512])
        p_s = ph.ps("s", [P, 512])
        names = ("ahead ones kT kmx kmax kTurned krow q kv v_done qmax qs qexp qsum qrec qn qt qt_out "
                 "ek vs ctx ctxm rk m mo o added")
        s = {n: ph.sem(n) for n in names.split()}
        block = ph.open()
        gather_ahead(ph, block, g, job, s["ahead"], ahead)

        def rows(t):
            return P if t < NT - 1 else LAST

        @block.tensor
        def _(pe):
            for c in range(KB):
                if c >= 2:
                    pe.wait_ge(s["kmx"], 2 * (c - 1))
                for a in range(HALF):
                    for i in range(HALF):
                        mm = pe.matmul((p_q, p_kv)[a][:, c % 2, 0:KW], wk[:, i, a * P:(a + 1) * P],
                                       turned[:, i, c * KW:(c + 1) * KW], start=(i == 0), stop=(i == HALF - 1))
                    mm.then_inc(s["kT"], 1)
            pe.wait_ge(s["kmax"], 1)
            for a in range(HALF):
                mm = pe.transpose(p_s[0:1, a * P:(a + 1) * P], kmax[:, a:a + 1], g["ident"][:, :])
            mm.then_inc(s["kTurned"], 1)
            pe.wait_ge(s["krow"], 1)
            pe.wait_ge(s["ones"], 1)

            def project(t):
                b = t % 2
                if t >= 2:
                    pe.wait_ge(s["qs"], t - 1)
                    pe.wait_ge(s["vs"], t - 1)
                at = slice(t * P, (t + 1) * P)
                for i in range(HALF):
                    mm = pe.matmul(p_q[:, b, 0:D], turned[:, i, at], wq[:, i, :], start=(i == 0), stop=(i == HALF - 1))
                mm.then_inc(s["q"], 1)
                for i in range(HALF):
                    pe.matmul(p_kv[:, b, 0:D], turned[:, i, at], wk[:, i, :], start=(i == 0), stop=False)
                pe.matmul(p_kv[:, b, 0:D], ones[0:1, :], krow[:, :], start=False, stop=True)
                for i in range(HALF):
                    mm = pe.matmul(p_kv[:, b, D:2 * D], turned[:, i, at], wv[:, i, :], start=(i == 0), stop=(i == HALF - 1))
                mm.then_inc(s["kv"], 1)

            def contract(t):
                b, r = t % 2, rows(t)
                pe.wait_ge(s["vs"], t + 1)
                for a in range(HALF):
                    pe.matmul(p_c[:, a * P:(a + 1) * P], vs[0:r, b, a * P:(a + 1) * P], ek[0:r, b, a * P:(a + 1) * P],
                              start=(t == 0 and a == 0), stop=(t == NT - 1), skip_group_check=True)
                for a in range(HALF):
                    mm = pe.matmul(p_c[:, D + a:D + a + 1], ek[0:r, b, a * P:(a + 1) * P], ones[0:r, 0:1],
                                   start=False, stop=(t == NT - 1), skip_group_check=True)
                mm.then_inc(s["ctx"], 1)
                pe.wait_ge(s["qn"], t + 1)
                if t >= 2:
                    pe.wait_ge(s["qt_out"], t - 1)
                for a in range(HALF):
                    mm = pe.transpose(p_t[:, b, a * P:(a + 1) * P],
                                      qs[:, b, :, :].rearrange("p h w -> p (h w)")[:, a * P:(a + 1) * P], g["ident"][:, :])
                mm.then_inc(s["qt"], 1)

            for t in range(NT):
                project(t)
                if t:
                    contract(t - 1)
            contract(NT - 1)
            pe.wait_ge(s["ctxm"], 2)
            for a in range(HALF):
                mm = pe.matmul(p_s[:, a * D:(a + 1) * D], ctx[:, a, :], wo[:, a, :], start=True, stop=True)
            mm.then_inc(s["m"], 1)
            pe.wait_ge(s["mo"], 2)
            pe.wait_ge(s["qt_out"], NT)
            for t in range(NT):
                if t >= 2:
                    pe.wait_ge(s["added"], t - 1)
                for a in range(HALF):
                    pe.matmul(p_q[:, t % 2, 0:D], qt[:, a, t * P:(t + 1) * P], M[:, a, :], start=(a == 0), stop=False)
                pe.matmul(p_q[:, t % 2, 0:D], ones[0:1, :], bo[:, :], start=False, stop=True).then_inc(s["o"], 1)

        @block.scalar
        def _(act):
            def keys(t):
                b = t % 2
                act.wait_ge(s["kv"], t + 1)
                if t >= 2:
                    act.wait_ge(s["ctx"], t - 1)
                act.activation(ek[:, b, :], p_kv[:, b, 0:D], ACT.Exp, scale=QK_SCALE).then_inc(s["ek"], 1)
                act.activation(vs[:, b, :], p_kv[:, b, D:2 * D], ACT.Copy).then_inc(s["vs"], 1)

            def turned_queries(t):
                act.wait_ge(s["qt"], t + 1)
                act.activation(qt[:, :, t * P:(t + 1) * P], p_t[:, t % 2, 0:D].rearrange("p (a n) -> p a n", a=HALF),
                               ACT.Copy).then_inc(s["qt_out"], 1)

            for t in range(NT):
                act.wait_ge(s["qs"], t + 1)
                act.activation(qs[:, t % 2, :, :], qs[:, t % 2, :, :], ACT.Exp, scale=QK_SCALE).then_inc(s["qexp"], 1)
                keys(t)
                if t:
                    turned_queries(t - 1)
            turned_queries(NT - 1)

        @block.vector
        def _(v):
            v.memset(ones[:, :], 1.0).then_inc(s["ones"], 1)
            for c in range(KB):
                w_ = min(KW, N - c * KW)
                for a in range(HALF):
                    v.wait_ge(s["kT"], HALF * c + a + 1)
                    v.tensor_reduce(kmx[:, a, c:c + 1], (p_q, p_kv)[a][:, c % 2, 0:w_], X_AXIS, ALU.max).then_inc(s["kmx"], 1)
            v.wait_ge(s["kmx"], HALF * KB)
            v.tensor_reduce(kmax[:, :], kmx[:, :, :], X_AXIS, ALU.max).then_inc(s["kmax"], 1)
            v.wait_ge(s["kTurned"], 1)
            v.tensor_scalar(krow[:, :], p_s[0:1, 0:D], -1.0, None, ALU.mult).then_inc(s["krow"], 1)

            def shift(t):
                b = t % 2
                v.wait_ge(s["q"], t + 1)
                q = p_q[:, b, 0:D].rearrange("p (h w) -> p h w", w=DH)
                v.tensor_reduce(qmax[:, b, :], q, X_AXIS, ALU.max).then_inc(s["qmax"], 1)
                v.wait_ge(s["qmax"], t + 1)
                if t >= 2:
                    v.wait_ge(s["qt"], t - 1)
                v.tensor_tensor(qs[:, b, :, :], q, qmax[:, b, :, None].to_broadcast([P, H, DH]),
                                ALU.subtract).then_inc(s["qs"], 1)

            def scale(t):
                b = t % 2
                v.wait_ge(s["qexp"], t + 1)
                v.tensor_reduce(qsum[:, b, :], qs[:, b, :, :], X_AXIS, ALU.add).then_inc(s["qsum"], 1)
                v.wait_ge(s["qsum"], t + 1)
                v.reciprocal(qrec[:, b, :], qsum[:, b, :]).then_inc(s["qrec"], 1)
                v.wait_ge(s["qrec"], t + 1)
                v.tensor_tensor(qs[:, b, :, :], qs[:, b, :, :], qrec[:, b, :, None].to_broadcast([P, H, DH]),
                                ALU.mult).then_inc(s["qn"], 1)

            for t in range(NT):
                shift(t)
                scale(t)
            v.wait_ge(s["ctx"], NT)
            v.reciprocal(rk[:, :], p_c[:, D:D + HALF]).then_inc(s["rk"], 1)
            for a in range(HALF):
                v.tensor_tensor(ctx[:, a, :], p_c[:, a * P:(a + 1) * P], g["blocks"][:, :], ALU.mult).then_inc(s["ctxm"], 1)
            v.wait_ge(s["m"], 1)
            v.wait_ge(s["rk"], 1)
            for a in range(HALF):
                v.tensor_scalar(M[:, a, :], p_s[:, a * D:(a + 1) * D], rk[:, a:a + 1], None, ALU.mult).then_inc(s["mo"], 1)
            for t in range(NT):
                v.wait_ge(s["o"], t + 1)
                v.tensor_tensor(S[:, t, :], S[:, t, :], p_q[:, t % 2, 0:D], ALU.add).then_inc(s["added"], 1)


def mlp(nc, g, name, S, turned, weights, ahead=(), experts=1, load=None, gates=None, job=None):
    with Phase(nc, name) as ph:
        hid = (ph.sb("hid_a", [P, FC, A_N]), ph.sb("hid_b", [P, FC, B_N]))
        ones = ph.sb("ones", [1, P])
        p_u = ph.ps("u", [P, 4, 512])
        p_d = ph.ps("d", [P, 3, 512])
        p_b = ph.ps("b", [P, 512])
        s_ahead, s_ones, s_up, s_hid, s_down, s_added, s_passed = (
            ph.sem(x) for x in ("ahead", "ones", "up", "hid", "down", "added", "passed"))
        s_w = [ph.sem(f"w{b}") for b in range(2)]
        s_folded, s_pb = ph.sem("folded"), ph.sem("pb")
        block = ph.open()
        if job is not None:
            gather_ahead(ph, block, g, job, s_ahead, ahead)
        width, first, tiles = (A_N, B_N), (0, A_N), (A_T, B_T)
        grouped = experts > 1
        UPS, DOWNS = NB * 2 * FC, NT

        def each(eng):
            if not grouped:
                yield 0, 0, 0, False
                return
            with eng.Fori(0, experts // 2 - 1) as pair:
                for b in range(2):
                    yield pair * 2 + b, b, pair, True
            for b in range(2):
                yield experts - 2 + b, b, experts // 2 - 1, b == 0

        n_loads = len(load(0, 0)) if grouped else 0

        def here(eng, b, pair):
            eng.wait_ge(s_w[b], pair * (16 * n_loads) + 16 * n_loads)

        if grouped:
            @block.sync
            def _(sp):
                def fetch(e, b):
                    for out, in_ in load(e, b):
                        sp.dma_start(out, in_).then_inc(s_w[b], 16)

                fetch(0, 0)
                fetch(1, 1)
                with sp.Fori(0, experts // 2 - 1) as pair:
                    for b in range(2):
                        gate(sp, s_down, (pair * 2 + b) * DOWNS + (U + DOWNS), s_passed)
                        fetch(pair * 2 + (b + 2), b)

        @block.tensor
        def _(pe):
            def up(e, b, k, part):
                for f in range(FC):
                    n = part * FC + f
                    pe.wait_ge(s_hid, e * UPS + k * (2 * FC) + (n + 1))
                    for i in range(HALF):
                        mm = pe.matmul(p_u[:, n % 4, 0:width[part]], weights[b]["w1"][:, i, f * P:(f + 1) * P],
                                       turned[:, i, bass.ds(k * (U * P) + first[part], width[part])],
                                       start=(i == 0), stop=(i == HALF - 1))
                    mm.then_inc(s_up, 1)

            def down(e, b, k, part):
                pe.wait_ge(s_hid, e * UPS + k * (2 * FC) + ((part + 1) * FC + 4))
                for j in range(tiles[part]):
                    n = part * A_T + j
                    pe.wait_ge(s_added, e * DOWNS + k * U + (n + 1))
                    for f in range(FC):
                        pe.matmul(p_d[:, n % 3, 0:D], hid[part][:, f, j * P:(j + 1) * P],
                                  weights[b]["w2"][:, f, :], start=(f == 0), stop=False)
                    pe.matmul(p_d[:, n % 3, 0:D], ones[:, :], weights[b]["b2"][:, :], start=False,
                              stop=True).then_inc(s_down, 1)

            def fold(b, pair):
                here(pe, b, pair)
                for f in range(FC):
                    for i in range(HALF):
                        mm = pe.matmul(p_b[:, f:f + 1], weights[b]["w1"][:, i, f * P:(f + 1) * P],
                                       weights[b]["ln_b"][:, i:i + 1], start=(i == 0), stop=(i == HALF - 1))
                mm.then_inc(s_pb, 1)

            pe.sem_inc(s_down, U)
            pe.wait_ge(s_ones, 1)
            if grouped:
                fold(0, 0)
            for e, b, pair, more in each(pe):
                if grouped:
                    pe.wait_ge(s_folded, (HALF + 1) * (e + 1))
                up(e, b, 0, 0)
                with pe.Fori(0, NB - 1) as k:
                    up(e, b, k, 1)
                    down(e, b, k, 0)
                    up(e, b, k + 1, 0)
                    down(e, b, k, 1)
                up(e, b, NB - 1, 1)
                down(e, b, NB - 1, 0)
                if more:
                    fold(1 - b, pair + b)
                down(e, b, NB - 1, 1)

        @block.scalar
        def _(act):
            act.sem_inc(s_hid, 4)
            for e, b, pair, more in each(act):
                if grouped:
                    act.wait_ge(s_folded, (HALF + 1) * (e + 1))
                with act.Fori(0, NB) as k:
                    for part in range(2):
                        act.wait_ge(s_down, e * DOWNS + k * U + (first[part] // P + tiles[part]))
                        for f in range(FC):
                            n = part * FC + f
                            act.wait_ge(s_up, e * UPS + k * (2 * FC) + (n + 1))
                            act.activation(hid[part][:, f, :], p_u[:, n % 4, 0:width[part]], ACT.Gelu,
                                           bias=weights[b]["b1"][:, f:f + 1]).then_inc(s_hid, 1)

        @block.vector
        def _(v):
            v.memset(ones[:, :], 1.0).then_inc(s_ones, 1)
            v.sem_inc(s_added, 2)

            def fold(b, pair, count):
                w = weights[b]
                here(v, b, pair)
                v.wait_ge(s_pb, count)
                v.tensor_tensor(w["b1"][:, :], w["b1"][:, :], p_b[:, 0:FC], ALU.add).then_inc(s_folded, 1)
                for i in range(HALF):
                    v.tensor_scalar(w["w1"][:, i, :], w["w1"][:, i, :], w["ln_g"][:, i:i + 1], None,
                                    ALU.mult).then_inc(s_folded, 1)

            def add(e, k, n):
                v.wait_ge(s_down, e * DOWNS + k * U + (U + n + 1))
                if grouped:
                    v.scalar_tensor_tensor(S[:, k * U + n, :], p_d[:, n % 3, 0:D], gates[:, k * U + n, bass.ds(e, 1)],
                                           S[:, k * U + n, :], ALU.mult, ALU.add).then_inc(s_added, 1)
                else:
                    v.tensor_tensor(S[:, k * U + n, :], S[:, k * U + n, :], p_d[:, n % 3, 0:D],
                                    ALU.add).then_inc(s_added, 1)

            if grouped:
                fold(0, 0, 1)
            for e, b, pair, more in each(v):
                with v.Fori(0, NB - 1) as k:
                    for n in range(U):
                        add(e, k, n)
                for n in range(U):
                    if more and n == A_T:
                        fold(1 - b, pair + b, e + 2)
                    add(e, NB - 1, n)


def mixer(nc, io, g, S, turned, spare, tables):
    with ExitStack() as ctx:
        def sb(name, shape, dtype=F32):
            return ctx.enter_context(nc.sbuf_tensor("mix_" + name, shape, dtype))

        lnp = sb("lnp", [P, 4, HALF])
        wq, wk, wv, wo = (sb(n, [P, HALF, D]) for n in ("wq", "wk", "wv", "wo"))
        bo, b2 = sb("bo", [1, D]), sb("b2", [1, D])
        w1, w2, b1 = sb("w1", [P, HALF, FF]), sb("w2", [P, FC, D]), sb("b1", [P, FC])
        with nc.Fori(0, DEPTH) as layer:
            with Phase(nc, "mixln") as ph:
                loaded = ph.sem("loaded")
                block = ph.open()
                load_ahead(block, loaded, [(lnp[:, :, :], io["mix_ln"][layer])])
            halves = lambda name: io[name][layer].rearrange("(a p) o -> p a o", p=P)
            norm(nc, "mixnorm1", S, spare, turned, g["ident"], lnp[:, 0, :], lnp[:, 1, :],
                 [(wq[:, :, :], halves("wq")), (wk[:, :, :], halves("wk")), (wv[:, :, :], halves("wv")),
                  (wo[:, :, :], halves("wo")), (bo[:, :], io["bo"][bass.ds(layer, 1), :])])
            attention(nc, g, (wq, wk, wv, wo, bo), S, turned, spare,
                      [(w1[:, :, :], halves("w1")), (w2[:, :, :], halves("w2")),
                       (b1[:, :], io["mix_b1"][layer]), (b2[:, :], io["mix_b2"][bass.ds(layer, 1), :])],
                      (0, layer * (ATTN_GROUPS + FF_GROUPS), ATTN_GROUPS, [layer * n for n in halved(ATTN_GROUPS, FF_GROUPS)])
                      + tables)
            norm(nc, "mixnorm2", S, spare, turned, g["ident"], lnp[:, 2, :], lnp[:, 3, :])
            mlp(nc, g, "mixff", S, turned, [{"w1": w1, "w2": w2, "b1": b1, "b2": b2}],
                job=(0, layer * (ATTN_GROUPS + FF_GROUPS) + ATTN_GROUPS, FF_GROUPS,
                     [layer * n + m for n, m in zip(halved(ATTN_GROUPS, FF_GROUPS), halved(ATTN_GROUPS))]) + tables)


def add_to(nc, X, S):
    with Phase(nc, "addto") as ph:
        s_done = ph.sem("done")
        block = ph.open()

        @block.vector
        def _(v):
            with v.Fori(0, NB) as k:
                v.tensor_tensor(X[:, bass.ds(k * U, U), :], X[:, bass.ds(k * U, U), :], S[:, bass.ds(k * U, U), :],
                                ALU.add).then_inc(s_done, 1)


def route(nc, g, turned, wr, br, gates, top2, iota8):
    with Phase(nc, "route2" if top2 else "route") as ph:
        logits = ph.sb("logits", [P, NT, R])
        m = ph.sb("m", [P, NT])
        best = ph.sb("best", [P, NT, 8])
        where = ph.sb("where", [P, NT, 8], U32)
        where_f = ph.sb("where_f", [P, NT, 2])
        hot = ph.sb("hot", [P, NT, R])
        den = ph.sb("den", [P, NT])
        ones = ph.sb("ones", [1, 512])
        by_expert = ph.sb("by_expert", [R, NP])
        p_l = ph.ps("l", [P, 512])
        p_e = ph.ps("e", [P, 2, 512])
        s_e8, s_byexp = ph.sem("e8"), ph.sem("byexp")
        ident = g["ident"]
        s_ones, s_l, s_x, s_e, s_best, s_where = (ph.sem(x) for x in ("ones", "l", "x", "e", "best", "where"))
        block = ph.open()

        @block.tensor
        def _(pe):
            pe.wait_ge(s_ones, 1)
            for c in range(-(-NP // 512)):
                at = slice(c * 512, min(NP, (c + 1) * 512))
                w_ = at.stop - at.start
                if c >= 2:
                    pe.wait_ge(s_byexp, c - 1)
                for a in range(HALF):
                    pe.matmul(p_e[0:R, c % 2, 0:w_], wr[:, a, :], turned[:, a, at], start=(a == 0), stop=False)
                pe.matmul(p_e[0:R, c % 2, 0:w_], br[:, :], ones[:, 0:w_], start=False, stop=True).then_inc(s_e8, 1)
            pe.wait_ge(s_byexp, -(-NP // 512))
            for t in range(NT):
                mm = pe.transpose(p_l[:, t * R:(t + 1) * R], by_expert[:, t * P:(t + 1) * P], ident[0:R, 0:R])
            mm.then_inc(s_l, 1)

        @block.scalar
        def _(act):
            for c in range(-(-NP // 512)):
                at = slice(c * 512, min(NP, (c + 1) * 512))
                act.wait_ge(s_e8, c + 1)
                act.activation(by_expert[:, at], p_e[0:R, c % 2, 0:at.stop - at.start], ACT.Copy).then_inc(s_byexp, 1)
            act.wait_ge(s_x, 2)
            act.activation(logits[:, :, :], logits[:, :, :], ACT.Exp).then_inc(s_e, 1)

        @block.vector
        def _(v):
            steps = [0]

            def step(ins):
                steps[0] += 1
                ins.then_inc(s_x, 1)
                v.wait_ge(s_x, steps[0])

            v.memset(ones[:, :], 1.0).then_inc(s_ones, 1)
            v.wait_ge(s_l, 1)
            lg = p_l[:, 0:NT * R].rearrange("p (t e) -> p t e", e=R)
            step(v.tensor_reduce(m[:, :], lg, X_AXIS, ALU.max))
            step(v.tensor_tensor(logits[:, :, :], lg, m[:, :, None].to_broadcast([P, NT, R]), ALU.subtract))
            v.wait_ge(s_e, 1)
            step(v.tensor_reduce(den[:, :], logits[:, :, :], X_AXIS, ALU.add))
            step(v.reciprocal(m[:, :], den[:, :]))
            probs = logits if top2 else gates
            step(v.tensor_tensor(probs[:, :, :], logits[:, :, :], m[:, :, None].to_broadcast([P, NT, R]), ALU.mult))
            if top2:
                for t in range(NT):
                    v.max(best[:, t, :], probs[:, t, :]).then_inc(s_best, 1)
                v.wait_ge(s_best, NT)
                for t in range(NT):
                    v.max_index(where[:, t, :], best[:, t, :], probs[:, t, :]).then_inc(s_where, 1)
                v.wait_ge(s_where, NT)
                step(v.tensor_copy(where_f[:, :, :], where[:, :, 0:2]))
                step(v.tensor_tensor(den[:, :], best[:, :, 0], best[:, :, 1], ALU.add))
                step(v.reciprocal(m[:, :], den[:, :]))
                step(v.tensor_tensor(best[:, :, 0:2], best[:, :, 0:2], m[:, :, None].to_broadcast([P, NT, 2]), ALU.mult))
                for n, to in ((0, gates), (1, hot)):
                    step(v.tensor_tensor(to[:, :, :], where_f[:, :, n, None].to_broadcast([P, NT, R]),
                                         iota8[:, None, :].to_broadcast([P, NT, R]), ALU.is_equal))
                    step(v.tensor_tensor(to[:, :, :], to[:, :, :], best[:, :, n, None].to_broadcast([P, NT, R]), ALU.mult))
                step(v.tensor_tensor(gates[:, :, :], gates[:, :, :], hot[:, :, :], ALU.add))


QS = float(DH) ** 0.25


def taylor_project(nc, g, w, turned, QK, v1, fac, job):
    wqkv, bqkv, temp, valid = w
    with Phase(nc, "tproj") as ph:
        ones = ph.sb("ones", [1, P])
        sq = ph.sb("sq", [P, 2, 2 * D])
        ssq = ph.sb("ssq", [P, NT, 2, H])
        nrm = ph.sb("nrm", [P, NT, 2, H])
        p_qk = ph.ps("qk", [P, 2, 512])
        p_v = ph.ps("v", [P, 2, 512])
        names = "ones qk v qk_out v_out sq ssq root x"
        s = {n: ph.sem(n) for n in names.split()}
        block = ph.open()
        gather_ahead(ph, block, g, job, None, [])

        @block.tensor
        def _(pe):
            pe.wait_ge(s["ones"], 1)
            for t in range(NT):
                if t >= 2:
                    pe.wait_ge(s["v_out"], t - 1)
                at = slice(t * P, (t + 1) * P)
                for out, c0, c1, done in ((p_qk, 0, 2 * D, "qk"), (p_v, 2 * D, 3 * D, "v")):
                    for a in range(HALF):
                        pe.matmul(out[:, t % 2, 0:c1 - c0], turned[:, a, at], wqkv[:, a, c0:c1], start=(a == 0), stop=False)
                    pe.matmul(out[:, t % 2, 0:c1 - c0], ones[:, :], bqkv[:, c0:c1], start=False,
                              stop=True).then_inc(s[done], 1)

        @block.scalar
        def _(act):
            for t in range(NT):
                act.wait_ge(s["qk"], t + 1)
                act.activation(QK[:, t, :], p_qk[:, t % 2, :], ACT.Copy).then_inc(s["qk_out"], 1)
                act.wait_ge(s["v"], t + 1)
                act.activation(v1[:, t, :, 1:HW], p_v[:, t % 2, 0:D].rearrange("p (h w) -> p h w", w=DH),
                               ACT.Copy, scale=valid[:, t:t + 1]).then_inc(s["v_out"], 1)
            act.wait_ge(s["ssq"], NT)
            act.activation(nrm[:, :, :, :], ssq[:, :, :, :], ACT.Sqrt).then_inc(s["root"], 1)

        @block.vector
        def _(v):
            v.memset(ones[:, :], 1.0).then_inc(s["ones"], 1)
            v.tensor_copy(v1[:, :, :, 0], valid[:, :, None].to_broadcast([P, NT, H])).then_inc(s["x"], 1)
            for t in range(NT):
                v.wait_ge(s["qk_out"], t + 1)
                v.tensor_tensor(sq[:, t % 2, :], QK[:, t, :], QK[:, t, :], ALU.mult).then_inc(s["sq"], 1)
                v.wait_ge(s["sq"], t + 1)
                v.tensor_reduce(ssq[:, t, :, :], sq[:, t % 2, :].rearrange("p (s h w) -> p s h w", s=2, w=DH),
                                X_AXIS, ALU.add).then_inc(s["ssq"], 1)
            v.wait_ge(s["root"], 1)
            v.tensor_scalar(nrm[:, :, 0, :], nrm[:, :, 0, :], QS, 1e-12, ALU.mult, ALU.max).then_inc(s["x"], 1)
            v.tensor_scalar(nrm[:, :, 1, :], nrm[:, :, 1, :], 1e-12, None, ALU.max).then_inc(s["x"], 1)
            v.wait_ge(s["x"], 3)
            v.reciprocal(fac[:, :, :, :], nrm[:, :, :, :]).then_inc(s["x"], 1)
            v.wait_ge(s["x"], 4)
            v.tensor_scalar(fac[:, :, 1, :], fac[:, :, 1, :], QS, None, ALU.mult).then_inc(s["x"], 1)
            v.scalar_tensor_tensor(fac[:, :, 0, :], fac[:, :, 0, :], QS * QS,
                                   temp[:, None, :].to_broadcast([P, NT, H]), ALU.mult, ALU.mult).then_inc(s["x"], 1)


OFFSETS = DH // 2
PAIRS = OFFSETS * DH // P
PROJECT_GROUPS, KEYS_GROUPS = 5, 12
PER_BANK = 15


def window(x, n):
    return bass.AP(tensor=x.tensor, offset=x.offset, ap=[x.ap[0], [1, n], x.ap[1]])


def taylor_keys(nc, g, w, QK, v1, fac, kv2, kv_half, kv1, kv0, job, ahead):
    pair_scale, half_mask = w
    ONE, HALVES, ROW_AT = 0, 1, 1 + OFFSETS
    EXT = ROW_AT + DH
    with Phase(nc, "tkeys") as ph:
        ext = ph.sb("ext", [P, H, EXT + OFFSETS])
        kk = ph.sb("kk", [P, H, OFFSETS, DH])
        sums_t = ph.sb("sums_t", [P, H // 2, OFFSETS * DH])
        half_t = ph.sb("half_t", [HW, H, OFFSETS])
        row_t = ph.sb("row_t", [HW, H, DH])
        one_t = ph.sb("one_t", [HW, H])
        p_pairs = ph.ps("pairs", [P, H // 2, 512])
        p_ext = ph.ps("ext", [P, 512])
        p_back = ph.ps("back", [P, 3, 512])
        names = "ahead one k kk used copied back last out"
        s = {n: ph.sem(n) for n in names.split()}
        block = ph.open()
        gather_ahead(ph, block, g, job, s["ahead"], ahead)
        ident = g["ident"]

        def rows(h):
            return slice(h % 2 * 64, h % 2 * 64 + HW)

        @block.tensor
        def _(pe):
            for t in range(NT):
                pe.wait_ge(s["k"], 3 * (t + 1))
                for h in range(H):
                    if h % 2 == 0:
                        pe.wait_ge(s["kk"], t * (H // 2) + h // 2 + 1)
                    pe.matmul(p_pairs[rows(h), h // 2, :], v1[:, t, h, :], kk[:, h, :, :].rearrange("p d i -> p (d i)"),
                              start=(t == 0), stop=(t == NT - 1), skip_group_check=True)
                    mm = pe.matmul(p_ext[0:HW, h * EXT:(h + 1) * EXT], v1[:, t, h, :], ext[:, h, 0:EXT],
                                   start=(t == 0 and h == 0), stop=(t == NT - 1), skip_group_check=True)
                    if h % 2:
                        mm.then_inc(s["used"], 1)
            pe.wait_ge(s["copied"], 5)
            for odd in range(2):
                for h in range(odd, H, 2):
                    for c in range(PAIRS):
                        n = h * PAIRS + c
                        mm = pe.transpose(p_back[:, n // PER_BANK, n % PER_BANK * HW:(n % PER_BANK + 1) * HW],
                                          sums_t[rows(h), h // 2, c * P:(c + 1) * P], ident[rows(h), rows(h)])
                mm.then_inc(s["back"], 1)
                pe.wait_ge(s["back"], odd + 1)
            pe.transpose(p_pairs[:, 0, 0:HW], half_t[:, :, :].rearrange("p h d -> p (h d)"), ident[0:HW, 0:HW])
            for h in range(H):
                pe.transpose(p_pairs[0:DH, 1, h * HW:(h + 1) * HW], row_t[:, h, :], ident[0:HW, 0:HW])
            for h in range(H):
                mm = pe.transpose(p_pairs[0:1, 2, h * HW:(h + 1) * HW], one_t[:, h:h + 1], ident[0:HW, 0:HW])
            mm.then_inc(s["last"], 1)

        @block.scalar
        def _(act):
            act.wait_ge(s["used"], NT * (H // 2))
            act.activation(sums_t[64:64 + HW, :, :], p_pairs[64:64 + HW, :, :], ACT.Copy).then_inc(s["copied"], 1)

        @block.vector
        def _(v):
            v.memset(ext[:, :, ONE], 1.0).then_inc(s["one"], 1)
            for t in range(NT):
                if t:
                    v.wait_ge(s["used"], t * (H // 2))
                for to, width in ((ROW_AT, DH), (EXT, OFFSETS)):
                    v.tensor_tensor(ext[:, :, to:to + width],
                                    QK[:, t, D:2 * D].rearrange("p (h w) -> p h w", w=DH)[:, :, 0:width],
                                    fac[:, t, 1, :, None].to_broadcast([P, H, width]), ALU.mult).then_inc(s["k"], 1)
                v.wait_ge(s["k"], t * 3 + 2)
                v.tensor_tensor(ext[:, :, HALVES:ROW_AT], ext[:, :, ROW_AT:ROW_AT + OFFSETS],
                                ext[:, :, ROW_AT + OFFSETS:EXT], ALU.mult).then_inc(s["k"], 1)
                for h in range(H):
                    last = v.tensor_tensor(kk[:, h, :, :], ext[:, h, None, ROW_AT:EXT].to_broadcast([P, OFFSETS, DH]),
                                           window(ext[:, h, ROW_AT:EXT], OFFSETS), ALU.mult)
                    if h % 2:
                        last.then_inc(s["kk"], 1)
            v.wait_ge(s["used"], NT * (H // 2))
            v.wait_ge(s["copied"], 1)
            v.tensor_copy(sums_t[0:HW, :, :], p_pairs[0:HW, :, :]).then_inc(s["copied"], 1)
            sums_ext = p_ext[0:HW, 0:H * EXT].rearrange("p (h w) -> p h w", w=EXT)
            v.tensor_copy(half_t[:, :, :], sums_ext[:, :, HALVES:ROW_AT]).then_inc(s["copied"], 1)
            v.tensor_copy(row_t[:, :, :], sums_ext[:, :, ROW_AT:EXT]).then_inc(s["copied"], 1)
            v.tensor_copy(one_t[:, :], sums_ext[:, :, ONE]).then_inc(s["copied"], 1)
            v.wait_ge(s["back"], 2)
            for h in range(H):
                for c in range(PAIRS):
                    n = h * PAIRS + c
                    v.tensor_scalar(kv2[:, n, :], p_back[:, n // PER_BANK, n % PER_BANK * HW:(n % PER_BANK + 1) * HW],
                                    pair_scale[:, min(c, 1):min(c, 1) + 1], None, ALU.mult).then_inc(s["out"], 1)
            v.wait_ge(s["last"], 1)
            v.tensor_tensor(kv_half[:, :, :], p_pairs[:, 0, None, 0:HW].to_broadcast([P, H, HW]),
                            half_mask[:, :, None].to_broadcast([P, H, HW]), ALU.mult).then_inc(s["out"], 1)
            v.tensor_scalar(kv1[:, :], p_pairs[0:DH, 1, 0:MSG], QS ** 2 / N, None, ALU.mult).then_inc(s["out"], 1)
            v.tensor_scalar(kv0[:, :], p_pairs[0:1, 2, 0:MSG], QS ** 4 / N, None, ALU.mult).then_inc(s["out"], 1)


JR = 4
GH = H // 2


def taylor_queries(nc, g, w, QK, fac, kv2, kv_half, kv1, kv0, X, spare, job):
    wp, bp, select = w
    with Phase(nc, "tqueries") as ph:
        qrow = ph.sb("qrow", [P, H, DH])
        q_half = ph.sb("q_half", [P, U, H, OFFSETS])
        rest = ph.sb("rest", [P, H, DH])
        parts = ph.sb("parts", [P, H, SPLIT, DH], BF16)
        ident = ph.sb("ident", [P, P], BF16)
        sel = ph.sb("sel", [SPLIT * DH, PAIRS + 1, P], BF16)
        qt = ph.sb("qt", [SPLIT * DH, U, H, P], BF16)
        qi = spare[:, 0:U * H * P // D, :].rearrange("p t f -> p (t f)").rearrange("p (u h n) -> p u h n", u=U, h=H)
        qq = ph.sb("qq", [P, JR, PAIRS, P])
        qq_half = ph.sb("qq_half", [P, P])
        y = ph.sb("y", [P, H, DH])
        rec = ph.sb("rec", [P, H])
        yt = ph.sb("yt", [P, HALF, P])
        ones = ph.sb("ones", [1, P])
        p_t = ph.ctx.enter_context(nc.psum_tensor("tqueries_ps_t", [P, 1024], BF16))
        p_o = ph.ps("o", [P, 512])
        p_i = ph.ps("i", [P, 512])
        p_j = ph.ps("j", [P, JR, 512])
        p_y = ph.ps("y", [P, 512])
        names = ("ones init q hi rest mid parts turned qt i qi j qq yy sum rec y yT yt half o added")
        s = {n: ph.sem(n) for n in names.split()}
        block = ph.open()
        DIFF = DH * SPLIT
        gather_ahead(ph, block, g, job, None, [])

        def passes(eng, body):
            for j in range(U):
                body(0, j, j)
            with eng.Fori(1, NB - 1) as k:
                for j in range(U):
                    body(k * U + j, j, None)
            for j in range(U):
                body((NB - 1) * U + j, j, (NB - 1) * U + j)

        def body_for(step):
            return lambda t, j, n: step(j if n is not None and n < U else t, j, n is None or n >= 1,
                                        n is None or n + 1 < NT, n is None or n + 2 < NT)

        @block.tensor
        def _(pe):
            def turn(t, j):
                pe.wait_ge(s["parts"], t + 1)
                pe.wait_ge(s["qt"], t + 1)
                for h in range(H):
                    mm = pe.transpose(p_t[0:DIFF, h * P:(h + 1) * P], parts[:, h, :, :].rearrange("p s w -> p (s w)"),
                                      ident[:, :])
                mm.then_inc(s["turned"], 1)

            def select_i(t, j, group):
                pe.wait_ge(s["qt"], t + 2)
                pe.wait_ge(s["qi"], t * 2 + (group + 1))
                pe.matmul(p_i[:, :], sel[:, PAIRS, :],
                          qt[:, j, group * GH:(group + 1) * GH, :].rearrange("p h n -> p (h n)"),
                          start=True, stop=True).then_inc(s["i"], 1)

            def select_j(t, j, h):
                pe.wait_ge(s["qq"], t * H + (h + 1))
                for c in range(PAIRS):
                    mm = pe.matmul(p_j[:, h % JR, c * P:(c + 1) * P], sel[:, c, :], qt[:, j, h, :], start=True, stop=True)
                mm.then_inc(s["j"], 1)

            def linear(t, j):
                pe.wait_ge(s["y"], t + 1)
                pe.wait_ge(s["qi"], t * 2 + 3)
                pe.matmul(p_y[:, 0:MSG], ones[:, :], kv0[:, :], start=True, stop=False, skip_group_check=True)
                for h in range(H):
                    pe.matmul(p_y[:, h * HW:(h + 1) * HW], qi[0:DH, j, h, :], kv1[:, h * HW:(h + 1) * HW],
                              start=False, stop=False, skip_group_check=True)

            def sums(t, h):
                pe.wait_ge(s["qq"], t * H + (h + JR + 1))
                for c in range(PAIRS):
                    mm = pe.matmul(p_y[:, h * HW:(h + 1) * HW], qq[:, h % JR, c, :], kv2[:, h * PAIRS + c, :],
                                   start=False, stop=False, skip_group_check=True)
                mm.then_inc(s["yy"], 1)

            def turn_half(j):
                return pe.transpose(p_o[:, D:D + P], q_half[:, j, :, :].rearrange("p h d -> p (h d)"), g["ident"][:, :])

            def turn_y(t, j, after):
                pe.wait_ge(s["y"], t + 2)
                pe.wait_ge(s["added"], t + 1)
                for a in range(HALF):
                    mm = pe.transpose(p_o[:, a * P:(a + 1) * P],
                                      y[:, :, :].rearrange("p h w -> p (h w)")[:, a * P:(a + 1) * P], g["ident"][:, :])
                if after:
                    mm = turn_half((j + 1) % U)
                mm.then_inc(s["yT"], 1)

            def project(t, after):
                pe.wait_ge(s["yt"], t + 1)
                if after:
                    pe.wait_ge(s["half"], t + 2)
                for a in range(HALF):
                    pe.matmul(p_o[:, 0:D], yt[:, a, :], wp[:, a, :], start=(a == 0), stop=False)
                pe.matmul(p_o[:, 0:D], ones[:, :], bp[:, :], start=False, stop=True).then_inc(s["o"], 1)

            def step(t, j, before, after, _):
                nj = (j + 1) % U
                if after:
                    turn(t + 1, nj)
                linear(t, j)
                for h in range(H):
                    if h == 0 and before:
                        turn_y(t - 1, (j - 1) % U, True)
                    if h == 2 and before:
                        project(t - 1, True)
                    sums(t, h)
                    if after and h in (3, 4):
                        select_i(t + 1, nj, h - 3)
                    if h + 3 < H:
                        select_j(t, j, h + 3)
                    elif after:
                        select_j(t + 1, nj, h + 3 - H)
                pe.wait_ge(s["half"], t + 1)
                pe.matmul(p_y[:, 0:MSG], qq_half[:, :], kv_half[:, :, :].rearrange("p h w -> p (h w)"),
                          start=False, stop=False, skip_group_check=True).then_inc(s["sum"], 1)

            pe.wait_ge(s["init"], 2)
            pe.wait_ge(s["ones"], 1)
            turn(0, 0)
            turn_half(0).then_inc(s["yT"], 1)
            for group in range(2):
                select_i(0, 0, group)
            for h in range(3):
                select_j(0, 0, h)
            passes(pe, body_for(step))
            turn_y(NT - 1, U - 1, False)
            project(NT - 1, False)

        @block.scalar
        def _(act):
            def turned(t, j):
                act.wait_ge(s["turned"], t + 1)
                act.activation(qt[:, j, :, :], p_t[0:DIFF, :].rearrange("p (h n) -> p h n", h=H), ACT.Copy).then_inc(s["qt"], 1)

            def half(t):
                act.wait_ge(s["yT"], t + 1)
                act.activation(qq_half[:, :], p_o[:, D:D + P], ACT.Copy).then_inc(s["half"], 1)

            def turned_y(t):
                act.wait_ge(s["yT"], t + 2)
                act.activation(yt[:, :, :], p_o[:, 0:D].rearrange("p (a n) -> p a n", a=HALF), ACT.Copy).then_inc(s["yt"], 1)

            def high(t):
                act.wait_ge(s["q"], 2 * t + 1)
                act.activation(parts[:, :, 0, :], qrow[:, :, :], ACT.Copy).then_inc(s["hi"], 1)

            def middle(t):
                act.wait_ge(s["rest"], t + 1)
                act.activation(parts[:, :, 1, :], rest[:, :, :], ACT.Copy).then_inc(s["mid"], 1)

            def selected(t, j, group):
                act.wait_ge(s["i"], t * 2 + (group + 1))
                act.activation(qi[:, j, group * GH:(group + 1) * GH, :], p_i[:, :].rearrange("p (h n) -> p h n", h=GH),
                               ACT.Copy).then_inc(s["qi"], 1)

            def step(t, j, before, after, after2):
                if after:
                    turned(t + 1, (j + 1) % U)
                if before:
                    half(t)
                    turned_y(t - 1)
                if after2:
                    high(t + 2)
                    middle(t + 2)
                if after:
                    for group in range(2):
                        selected(t + 1, (j + 1) % U, group)

            act.sem_inc(s["qt"], 1)
            act.sem_inc(s["qi"], 1)
            high(0)
            middle(0)
            turned(0, 0)
            half(0)
            high(1)
            middle(1)
            for group in range(2):
                selected(0, 0, group)
            passes(act, body_for(step))
            turned_y(NT - 1)

        @block.vector
        def _(v):
            def scaled(t, j, first=False):
                if not first:
                    v.wait_ge(s["parts"], t)
                    v.wait_ge(s["q"], 2 * t)
                v.tensor_tensor(qrow[:, :, :], QK[:, t, 0:D].rearrange("p (h w) -> p h w", w=DH),
                                fac[:, t, 0, :, None].to_broadcast([P, H, DH]), ALU.mult).then_inc(s["q"], 1)
                v.wait_ge(s["q"], 2 * t + 1)
                v.tensor_tensor(q_half[:, j, :, :], qrow[:, :, 0:OFFSETS], qrow[:, :, OFFSETS:DH], ALU.mult).then_inc(s["q"], 1)

            def middle(t):
                v.wait_ge(s["hi"], t + 1)
                v.tensor_tensor(rest[:, :, :], qrow[:, :, :], parts[:, :, 0, :], ALU.subtract).then_inc(s["rest"], 1)

            def low(t):
                v.wait_ge(s["mid"], t + 1)
                v.tensor_tensor(parts[:, :, 2, :], rest[:, :, :], parts[:, :, 1, :], ALU.subtract).then_inc(s["parts"], 1)

            def products(t, j, h):
                v.wait_ge(s["qi"], t * 2 + (h // GH + 2))
                v.wait_ge(s["yy"], t * H + (h + 1))
                v.wait_ge(s["j"], t * H + (h + 1))
                v.tensor_tensor(qq[:, h % JR, :, :], p_j[:, h % JR, :].rearrange("p (c n) -> p c n", n=P),
                                qi[:, j, h, None, :].to_broadcast([P, PAIRS, P]), ALU.mult).then_inc(s["qq"], 1)

            def quotient(t):
                v.wait_ge(s["sum"], t + 1)
                yy = p_y[:, 0:MSG].rearrange("p (h w) -> p h w", w=HW)
                v.reciprocal(rec[:, :], yy[:, :, 0]).then_inc(s["rec"], 1)
                v.wait_ge(s["rec"], t + 1)
                v.tensor_tensor(y[:, :, :], yy[:, :, 1:HW], rec[:, :, None].to_broadcast([P, H, DH]), ALU.mult).then_inc(s["y"], 1)

            def add(t):
                v.wait_ge(s["o"], t + 1)
                v.tensor_tensor(X[:, t, :], X[:, t, :], p_o[:, 0:D], ALU.add).then_inc(s["added"], 1)

            def step(t, j, before, after, after2):
                for h in range(H):
                    products(t, j, h)
                    if h == 1 and before:
                        quotient(t - 1)
                    if h == 2 and after2:
                        scaled(t + 2, (j + 2) % U)
                    if h == 3 and after2:
                        middle(t + 2)
                    if h == 4 and after2:
                        low(t + 2)
                    if h == 5 and before:
                        add(t - 1)

            v.memset(ones[:, :], 1.0).then_inc(s["ones"], 1)
            v.tensor_copy(ident[:, :], g["ident"][:, :]).then_inc(s["init"], 1)
            v.tensor_copy(sel[:, :, :], select[:, :, :]).then_inc(s["init"], 1)
            v.sem_inc(s["yy"], JR)
            v.sem_inc(s["qq"], JR)
            v.sem_inc(s["y"], 1)
            v.sem_inc(s["added"], 1)
            for t in range(2):
                scaled(t, t, t == 0)
                middle(t)
                low(t)
            passes(v, body_for(step))
            quotient(NT - 1)
            add(NT - 1)


def experts3(nc, g, X, turned, gates, ws, cols, bo):
    EX = R
    with Phase(nc, "experts3") as ph:
        h1 = ph.sb("h1", [P, 2, HALF, B_N])
        h2 = ph.sb("h2", [P, 2, HALF, B_N])
        scale, bias = ph.sb("scale", [P, 2, EX * HALF]), ph.sb("bias", [P, 2, EX * HALF])
        root = ph.sb("root", [P, 2, EX * HALF])
        ones = ph.sb("ones", [1, P])
        p_1 = ph.ps("p1", [P, 2, 512])
        p_2 = ph.ps("p2", [P, 2, 512])
        p_y = ph.ps("py", [P, 4, 512])
        names = "ones x root cols u1 h1 u2 h2 y added"
        s = {n: ph.sem(n) for n in names.split()}
        block = ph.open()
        width, first, tiles = (A_N, B_N), (0, A_N), (A_T, B_T)
        items = [(e, part) for e in range(EX) for part in range(2)]
        n_items = len(items)

        def per_item(k, m):
            return k * (HALF * n_items) + HALF * m

        @block.tensor
        def _(pe):
            pe.wait_ge(s["ones"], 1)
            with pe.Fori(0, NB) as k:
                def one(m):
                    e, part = items[m]
                    for f in range(HALF):
                        pe.wait_ge(s["h1"], per_item(k, m) + (f + 1))
                        for i in range(HALF):
                            mm = pe.matmul(p_1[:, f, 0:width[part]], ws[0][:, e, i, f * P:(f + 1) * P],
                                           turned[:, i, bass.ds(k * (U * P) + first[part], width[part])],
                                           start=(i == 0), stop=(i == HALF - 1))
                        mm.then_inc(s["u1"], 1)

                def two(m):
                    e, part = items[m]
                    pe.wait_ge(s["h1"], per_item(k, m) + 2 * HALF)
                    for f in range(HALF):
                        pe.wait_ge(s["h2"], per_item(k, m) + (f + 1))
                        for i in range(HALF):
                            mm = pe.matmul(p_2[:, f, 0:width[part]], ws[1][:, e, i, f * P:(f + 1) * P],
                                           h1[:, m % 2, i, 0:width[part]], start=(i == 0), stop=(i == HALF - 1))
                        mm.then_inc(s["u2"], 1)

                def three(m):
                    e, part = items[m]
                    pe.wait_ge(s["h2"], per_item(k, m) + 2 * HALF)
                    for j in range(tiles[part]):
                        n = e * U + part * A_T + j
                        pe.wait_ge(s["added"], k * (EX * U) + (n + 1))
                        for i in range(HALF):
                            pe.matmul(p_y[:, n % 4, 0:D], h2[:, m % 2, i, j * P:(j + 1) * P], ws[2][:, e, i, :],
                                      start=(i == 0), stop=False)
                        pe.matmul(p_y[:, n % 4, 0:D], ones[:, :], bo[:, e * D:(e + 1) * D], start=False,
                                  stop=True).then_inc(s["y"], 1)

                for m in range(n_items + 2):
                    if m < n_items:
                        one(m)
                    if 1 <= m <= n_items:
                        two(m - 1)
                    if m >= 2:
                        three(m - 2)

        @block.scalar
        def _(act):
            act.sem_inc(s["h1"], HALF)
            act.sem_inc(s["h2"], HALF)
            act.wait_ge(s["x"], 1)
            act.activation(root[:, :, :], root[:, :, :], ACT.Sqrt).then_inc(s["root"], 1)
            act.wait_ge(s["cols"], 2)
            with act.Fori(0, NB) as k:
                def relu(m, layer):
                    e, part = items[m]
                    up, out, hid, p_ = (("u1", "h1", h1, p_1), ("u2", "h2", h2, p_2))[layer]
                    for f in range(HALF):
                        act.wait_ge(s[up], per_item(k, m) + (f + 1))
                        act.activation(hid[:, m % 2, f, 0:width[part]], p_[:, f, 0:width[part]], ACT.Relu,
                                       bias=bias[:, layer, e * HALF + f:e * HALF + f + 1],
                                       scale=scale[:, layer, e * HALF + f:e * HALF + f + 1]).then_inc(s[out], 1)

                for m in range(n_items + 1):
                    if m < n_items:
                        relu(m, 0)
                    if m:
                        relu(m - 1, 1)

        @block.vector
        def _(v):
            v.memset(ones[:, :], 1.0).then_inc(s["ones"], 1)
            v.sem_inc(s["added"], 4)
            v.tensor_scalar(root[:, :, :], cols[:, :, 4, :], 0.001, None, ALU.add).then_inc(s["x"], 1)
            v.wait_ge(s["root"], 1)
            v.reciprocal(root[:, :, :], root[:, :, :]).then_inc(s["x"], 1)
            v.tensor_tensor(bias[:, :, :], cols[:, :, 0, :], cols[:, :, 3, :], ALU.subtract).then_inc(s["x"], 1)
            v.wait_ge(s["x"], 3)
            v.tensor_tensor(scale[:, :, :], cols[:, :, 1, :], root[:, :, :], ALU.mult).then_inc(s["cols"], 1)
            v.wait_ge(s["cols"], 1)
            v.tensor_tensor(bias[:, :, :], bias[:, :, :], scale[:, :, :], ALU.mult).then_inc(s["x"], 1)
            v.wait_ge(s["x"], 4)
            v.tensor_tensor(bias[:, :, :], bias[:, :, :], cols[:, :, 2, :], ALU.add).then_inc(s["cols"], 1)
            with v.Fori(0, NB) as k:
                for e, part in items:
                    for j in range(tiles[part]):
                        n = e * U + part * A_T + j
                        t = k * U + (part * A_T + j)
                        v.wait_ge(s["y"], k * (EX * U) + (n + 1))
                        v.scalar_tensor_tensor(X[:, t, :], p_y[:, n % 4, 0:D], gates[:, t, e:e + 1], X[:, t, :],
                                               ALU.mult, ALU.add).then_inc(s["added"], 1)


def build(nc, io, out):
    with ExitStack() as ctx:
        def sb(name, shape, dtype=F32, to=ctx):
            return to.enter_context(nc.sbuf_tensor(name, shape, dtype))

        def dram(name, shape):
            return nc.dram_tensor(name, shape, F32).ap()

        def halves(name, n=None):
            a = io[name] if n is None else io[name][n]
            return a.rearrange("(a p) o -> p a o", p=P)

        g = {n: sb("idx_" + n, [EP, ET + 2 * GT], I32) for n in ("src0", "dst0", "src1", "dst1", "put")}
        for layer in range(2):
            g[f"got{layer}"] = [[ctx.enter_context(nc.semaphore(f"got{layer}{side}{b}")) for b in range(2)] for side in range(2)]
            for n in ("scattered",):
                g[f"{n}{layer}"] = [ctx.enter_context(nc.semaphore(f"{n}{layer}{b}")) for b in range(2)]
        g["dst"] = sb("idx_dst", [EP, ET], I32)
        g["ident"] = sb("ident", [P, P])
        g["blocks"] = sb("blocks", [P, P])
        iota8 = sb("iota8", [P, R])
        X = sb("X", [P, NT, D])
        XN = sb("XN", [P, NT, D])
        table0, table1 = dram("table0", [NP, ROW]), dram("table1", [R * NP, ROW])
        dtable1 = dram("dtable1", [R * NP, H])
        totals0, totals1 = dram("totals0", [NP, ROW]), dram("totals1", [NP, ROW])
        firsts0, firsts1 = dram("firsts0", [ET, ROW]), dram("firsts1", [ET, ROW])
        rows0 = tuple(dram(f"{n}_rows0", [(NG + 2) * GE, ROW]) for n in ("src", "dst"))
        rows1 = (dram("src_rows1", [(NG + 2) * GE, ROW]), dram("dst_rows1", [(NG + 2) * GE, H]))
        tables1 = ((table1, dtable1), rows1)
        edge_prep(nc, io, g, [(X[:, :, :], io["x"].rearrange("(t p) f -> p t f", p=P)), (iota8[:, :], io["iota"][:, 0:R].partition_broadcast(P))])

        with ExitStack() as part:
            HT = sb("HT_g0", [P, HALF, NP], to=part)
            norm(nc, "norm0", X, XN, HT, g["ident"])
            gnn_table(nc, io, g, 0, HT, table0, None)
        with ExitStack() as part:
            HT = sb("HT_m0", [P, HALF, NP], to=part)
            spare = sb("spare_m0", [P, NT, D], to=part)
            mixer(nc, io, g, XN, HT, spare, ((table0, table0), rows0))
        edges(nc, io, g, 0, *rows0, totals0, firsts0)
        combine(nc, io, g, 0, totals0, firsts0, X)
        add_to(nc, X, XN)

        with ExitStack() as part:
            HT = sb("HT_f0", [P, HALF, NP], to=part)
            gates = sb("gates0", [P, NT, R], to=part)
            wr, br = sb("wr0", [P, HALF, R], to=part), sb("br0", [1, R], to=part)
            weights = [{"w1": sb(f"moe_w1{b}", [P, HALF, FF], to=part), "w2": sb(f"moe_w2{b}", [P, FC, D], to=part),
                        "b1": sb(f"moe_b1{b}", [P, FC], to=part), "b2": sb(f"moe_b2{b}", [1, D], to=part),
                        "ln_g": sb(f"moe_g{b}", [P, HALF], to=part), "ln_b": sb(f"moe_b{b}", [P, HALF], to=part)}
                       for b in range(2)]
            norm(nc, "norm1", X, XN, HT, g["ident"], ahead=[(wr[:, :, :], halves("wr0")), (br[:, :], io["br0"])])
            route(nc, g, HT, wr, br, gates, True, iota8)
            norm(nc, "norm2", XN, XN, HT, g["ident"])

            def load(e, b):
                w = weights[b]
                return [(w["w1"][:, :, :], halves("moe_w1", e)), (w["w2"][:, :, :], halves("moe_w2", e)),
                        (w["b1"][:, :], io["moe_b1"][e]), (w["b2"][:, :], io["moe_b2"][e]),
                        (w["ln_g"][:, :], io["moe_g"][e]), (w["ln_b"][:, :], io["moe_b"][e])]

            mlp(nc, g, "moe", X, HT, weights, experts=R, load=load, gates=gates)

        with ExitStack() as part:
            QK = sb("QK", [P, NT, 2 * D], to=part)
            v1 = sb("v1", [P, NT, H, HW], to=part)
            fac = sb("fac", [P, NT, 2, H], to=part)
            pair_scale, half_mask = sb("pair_scale", [P, 2], to=part), sb("half_mask", [P, H], to=part)
            with ExitStack() as inner:
                HT = sb("HT_g1", [P, HALF, NP], to=inner)
                wqkv, bqkv = sb("wqkv", [P, HALF, 3 * D], to=inner), sb("bqkv", [1, 3 * D], to=inner)
                temp, valid = sb("temp", [P, H], to=inner), sb("valid", [P, NT], to=inner)
                norm(nc, "norm3", X, XN, HT, g["ident"],
                     ahead=[(wqkv[:, :, :], halves("wqkv")), (bqkv[:, :], io["bqkv"]),
                            (temp[:, :], io["temp"].partition_broadcast(P)), (valid[:, :], io["valid"]),
                            (pair_scale[:, :], io["pair_scale"]), (half_mask[:, :], io["half_mask"])])
                gnn_table(nc, io, g, 1, HT, table1, dtable1)
                taylor_project(nc, g, (wqkv, bqkv, temp, valid), HT, QK, v1, fac,
                               (1, 0, PROJECT_GROUPS, [0, 0]) + tables1)
            kv2, kv_half = sb("kv2", [P, H * PAIRS, HW], to=part), sb("kv_half", [P, H, HW], to=part)
            kv1, kv0 = sb("kv1", [DH, MSG], to=part), sb("kv0", [1, MSG], to=part)
            wp, bp = sb("wp", [P, HALF, D], to=part), sb("bp", [1, D], to=part)
            select = sb("select", [SPLIT * DH, PAIRS + 1, P], to=part)
            taylor_keys(nc, g, (pair_scale, half_mask), QK, v1, fac, kv2, kv_half, kv1, kv0,
                        (1, PROJECT_GROUPS, KEYS_GROUPS, halved(PROJECT_GROUPS)) + tables1,
                        [(wp[:, :, :], halves("wproj")), (bp[:, :], io["bproj"]), (select[:, :, :], io["select"])])
            taylor_queries(nc, g, (wp, bp, select), QK, fac, kv2, kv_half, kv1, kv0, X, XN,
                           (1, PROJECT_GROUPS + KEYS_GROUPS, NG + 2 - PROJECT_GROUPS - KEYS_GROUPS,
                            halved(PROJECT_GROUPS, KEYS_GROUPS)) + tables1)
        edges(nc, io, g, 1, *rows1, totals1, firsts1)
        combine(nc, io, g, 1, totals1, firsts1, X)

        with ExitStack() as part:
            HT = sb("HT_f1", [P, HALF, NP], to=part)
            gates = sb("gates1", [P, NT, R], to=part)
            wr, br = sb("wr1", [P, HALF, R], to=part), sb("br1", [1, R], to=part)
            ws = [sb(f"e3_w{n}", [P, R, HALF, D], to=part) for n in range(3)]
            cols = sb("e3_cols", [P, 2, 5, R * HALF], to=part)
            bo = sb("e3_bo", [1, R * D], to=part)
            norm(nc, "norm4", X, XN, HT, g["ident"],
                 ahead=[(wr[:, :, :], halves("wr1")), (br[:, :], io["br1"]), (cols[:, :, :, :], io["e3_cols"]), (bo[:, :], io["e3_bo"])]
                 + [(w[:, e, :, :], halves(f"e3_w{n}", e)) for n, w in enumerate(ws) for e in range(R)])
            route(nc, g, HT, wr, br, gates, False, iota8)
            experts3(nc, g, X, HT, gates, ws, cols, bo)
        dump(nc, X, out)


def dump(nc, X, out):
    with Phase(nc, "dump") as ph:
        saved = ph.sem("saved")
        block = ph.open()

        @block.sync
        def _(sp):
            full = (NT - 1) * P
            sp.dma_start(out[0:full, :].rearrange("(t p) f -> p t f", p=P), X[:, 0:NT - 1, :]).then_inc(saved, 16)
            sp.dma_start(out[full:N, :], X[0:LAST, NT - 1, :]).then_inc(saved, 16)
            sp.wait_ge(saved, 32)


def kernel(**inputs):
    import concourse.bacc as _bacc
    from concourse.bass_utils import run_bass_kernel_spmd as _run

    nc = _bacc.Bacc("TRN2", target_bir_lowering=False, num_devices=1)
    arrays, io = {}, {}

    def give(name, a, dtype=None):
        a = np.ascontiguousarray(a)
        arrays["in_" + name] = a
        io[name] = nc.dram_tensor("in_" + name, a.shape, mybir.dt.from_np(a.dtype), kind="ExternalInput").ap()

    def pad(a, rows):
        return np.concatenate([a, np.zeros((rows - a.shape[0],) + a.shape[1:], a.dtype)])

    i = {k: np.asarray(v) for k, v in inputs.items()}
    give("x", pad(i["x"], NP))
    src, dst, typ = i["src"], i["dst"], i["edge_type_8"]
    tiles = dst.reshape(ET, EP)
    give("src_c", src.reshape(ET, EP).T)
    give("dst_c", tiles.T)
    give("type_c", typ.reshape(ET, EP).T)
    nxt = np.full((ET, EP), -1, dst.dtype)
    nxt[:, :-1] = tiles[:, 1:]
    give("next_c", nxt.T)
    give("first_c", np.broadcast_to(tiles[:, 0], (EP, ET)))
    give("dst_row", pad(dst, E + 2 * GE)[None, :])
    by_head = np.broadcast_to(tiles.reshape(NG, GT, 1, EP), (NG, GT, H, EP)).reshape(NG, GT * H, EP)
    give("dst_x", pad(by_head, NG + 2))
    attr = np.ones((4, E + 2 * GE), np.float32)
    attr[:3, :E] = i["edge_attr_3"].T
    attr[:3, E:] = 0
    give("attr", attr)
    give("enc_w", np.concatenate([i["L0_gnn_edge_W"].T, i["L0_gnn_edge_b"][None]]))
    lead = tiles[:, 0]
    before = np.concatenate([np.array([-1], dst.dtype), lead[:-1]])
    give("dst_f", lead.reshape(FT, FQ).T)
    give("prev_f", before.reshape(FT, FQ).T)
    give("dst_fx", np.broadcast_to(lead, (H, ET)))
    give("prev_fx", np.broadcast_to(before, (H, ET)))
    give("iota", np.arange(NP, dtype=np.float32)[None, :])
    give("ident", np.eye(P, dtype=np.float32))
    give("blocks", (np.arange(P)[:, None] // DH == np.arange(P) // DH).astype(np.float32))
    give("headmask", (np.arange(D).reshape(HALF, P).T[:, :, None] // DH == np.arange(H)).astype(np.float32))
    give("gnn_bias", i["L0_gnn_bias"][None, :])

    def columns(a, parts):
        return np.swapaxes(a.reshape(a.shape[:-1] + (parts, P)), -1, -2)

    lnp = np.stack([columns(i["L0_mix_" + n], HALF) for n in ("ln1_g", "ln1_b", "ln2_g", "ln2_b")], 2)
    give("mix_ln", lnp)
    for n in ("Wq", "Wk", "Wv", "Wo", "W1", "W2", "bo"):
        give(n.lower(), i["L0_mix_" + n])
    give("mix_b1", columns(i["L0_mix_b1"], FC))
    give("mix_b2", i["L0_mix_b2"])

    give("wr0", i["L0_ffn_Wr"])
    give("br0", i["L0_ffn_br"][None])
    give("wr1", i["L1_ffn_Wr"])
    give("br1", i["L1_ffn_br"][None])
    give("moe_w1", i["L0_ffn_W1"])
    give("moe_w2", i["L0_ffn_W2"])
    give("moe_b1", columns(i["L0_ffn_b1"], FC))
    give("moe_b2", i["L0_ffn_b2"][:, None])
    give("moe_g", columns(i["L0_ffn_ln_g"], HALF))
    give("moe_b", columns(i["L0_ffn_ln_b"], HALF))
    give("wqkv", i["L1_mix_Wqkv"].T)
    give("bqkv", i["L1_mix_bqkv"][None])
    give("temp", i["L1_mix_temperature"].reshape(1, H))
    give("valid", (np.arange(NP).reshape(NT, P).T < N).astype(np.float32))
    give("wproj", i["L1_mix_Wproj"].T)
    give("bproj", i["L1_mix_bproj"][None])
    row = np.arange(P)
    takes = [(row % DH + c * (P // DH) + row // DH) % DH for c in range(PAIRS)] + [row % DH]
    feature = np.arange(SPLIT * DH)[:, None] % DH
    give("select", np.stack([feature == n for n in takes], 1).astype(np.float32))
    once = np.where(row < DH, 0.5, 1.0) / N
    give("pair_scale", np.stack([once, np.full(P, 1.0 / N)], 1).astype(np.float32))
    give("half_mask", ((row[:, None] // OFFSETS == np.arange(H)) / N).astype(np.float32))
    for n, name in enumerate(("W1", "W2", "Wo")):
        give(f"e3_w{n}", i["L1_ffn_" + name])
    cols = np.stack([np.stack([i[f"L1_ffn_{n}{layer}"] for n in ("b", "g", "be", "m", "v")]) for layer in (1, 2)])
    give("e3_cols", cols.reshape(2, 5, R, HALF, P).transpose(4, 0, 1, 2, 3).reshape(P, 2, 5, R * HALF))
    give("e3_bo", i["L1_ffn_bo"].reshape(1, R * D))

    def with_scores(w):
        w = w.reshape(-1, H, DH, D).transpose(0, 3, 1, 2)
        full = np.zeros((w.shape[0], D, ROW), np.float32)
        full[:, :, :MSG].reshape(w.shape[0], D, H, HW)[:, :, :, :DH] = w
        return full

    for layer, w, names in ((0, i["L0_gnn_W"][None], ("L0_gnn_a_src", "L0_gnn_a_dst")),
                            (1, i["L1_gnn_W"], ("L1_gnn_attn_src", "L1_gnn_attn_dst"))):
        give(f"gnn_w{layer}", w)
        give(f"gnn_wt{layer}", with_scores(w))
        give(f"a{layer}", np.stack([i[n].reshape(HALF, P).T for n in names], 1))

    out = nc.dram_tensor("out_0", (N, D), F32, kind="ExternalOutput").ap()
    build(nc, io, out)
    r = _run(nc, [arrays], core_ids=[0])
    return r.results[0]["out_0"]
```
